# Optimizing a Trainium2 kernel written in Bass

```python
import numpy as np
import jax
import jax.numpy as jnp

def _softmax(x, axis=-1):
    return jax.nn.softmax(x, axis=axis)

def _gelu(x):
    return jax.nn.gelu(x, approximate=True)

def _silu(x):
    return jax.nn.silu(x)

def _sigmoid(x):
    return jax.nn.sigmoid(x)

def _layernorm(x, axis=-1, eps=1e-05):
    m = jnp.mean(x, axis=axis, keepdims=True)
    v = jnp.var(x, axis=axis, keepdims=True)
    return (x - m) / jnp.sqrt(v + eps)

def _scatter_add(tgt, idx, src, axis=0):
    return tgt.at[idx].add(src)

def _segment_sum(src, seg, n):
    return jax.ops.segment_sum(src, seg, n)
kernel_name = 'mk_conv_seq_d4_conv_nchw64_r4_9de1a8'

def setup_inputs(seed: int=0):
    np.random.seed(seed)
    _w = jnp.asarray

    def _rec_inputs():
        import jax
        import jax.numpy as jnp
        _gk = jax.random.key(seed)
        x = -0.000125 + 0.9999 * jax.random.normal(jax.random.fold_in(_gk, 1), (8, 16, 64, 64), jnp.float32)
        return x
    x = _rec_inputs()

    def _L0_conv_setup():
        import jax, jax.numpy as jnp
        import numpy as np
        B, C, H, W = (8, 16, 64, 64)
        HEADS = 8
        EPS_LN = 1e-05
        EPS_L2 = 1e-12

        def _dwconv(x, w, b):
            kh, kw = (w.shape[2], w.shape[3])
            y = jax.lax.conv_general_dilated(x, w, (1, 1), ((kh // 2, kh // 2), (kw // 2, kw // 2)), dimension_numbers=('NCHW', 'OIHW', 'NCHW'), feature_group_count=x.shape[1])
            return y + b[None, :, None, None]

        def _proj(x, w, b):
            return jnp.einsum('bchw,oc->bohw', x, w) + b[None, :, None, None]

        def _l2norm(x):
            return x / jnp.maximum(jnp.linalg.norm(x, axis=-1, keepdims=True), EPS_L2)

        def _split_h(t):
            b, c, h, w = t.shape
            cp = c // HEADS
            return t.reshape(b, HEADS, cp, h, w).transpose(0, 1, 3, 4, 2).reshape(b, HEADS, h, w * cp)

        def _split_w(t):
            b, c, h, w = t.shape
            cp = c // HEADS
            return t.reshape(b, HEADS, cp, h, w).transpose(0, 1, 4, 3, 2).reshape(b, HEADS, w, h * cp)

        def _merge_h(t, h, w):
            b = t.shape[0]
            cp = t.shape[-1] // w
            return t.reshape(b, HEADS, h, w, cp).transpose(0, 1, 4, 2, 3).reshape(b, HEADS * cp, h, w)

        def _merge_w(t, h, w):
            b = t.shape[0]
            cp = t.shape[-1] // h
            return t.reshape(b, HEADS, w, h, cp).transpose(0, 1, 4, 3, 2).reshape(b, HEADS * cp, h, w)
        key = jax.random.key(seed)
        ks = jax.random.split(key, 16)
        d = {'x': jax.random.normal(ks[0], (B, C, H, W), jnp.float32)}
        d['ln_w'] = jnp.ones((C,), jnp.float32)
        d['ln_b'] = jnp.zeros((C,), jnp.float32)
        specs = [('w01', 'b01', 1, 7), ('w11', 'b11', 1, 11), ('w21', 'b21', 1, 21), ('w02', 'b02', 7, 1), ('w12', 'b12', 11, 1), ('w22', 'b22', 21, 1)]
        for i, (wn, bn, kh, kw) in enumerate(specs):
            d[wn] = jax.random.normal(ks[i + 1], (C, 1, kh, kw), jnp.float32) * 0.05
            d[bn] = jnp.zeros((C,), jnp.float32)
        d['proj_w'] = jax.random.normal(ks[8], (C, C), jnp.float32) * 0.05
        d['proj_b'] = jnp.zeros((C,), jnp.float32)
        return d
    _L0_conv_all = _L0_conv_setup()
    _L0_conv_in = {k: v for k, v in _L0_conv_all.items() if k in ('ln_w', 'ln_b', 'w01', 'b01', 'w11', 'b11', 'w21', 'b21', 'w02', 'b02', 'w12', 'b12', 'w22', 'b22', 'proj_w', 'proj_b')}
    del _L0_conv_all

    def _L1_conv_setup():
        import jax, jax.numpy as jnp
        from jax import lax
        import numpy as np
        B, C, H, W = (8, 16, 64, 64)
        K = 9
        R = (K - 1) // 2
        HIDDEN = 32

        def _forward(x, gauss_kernel, w1, b1, w2, b2):
            Bx, Cx, Hx, Wx = x.shape
            Kx = gauss_kernel.shape[0]
            r = (Kx - 1) // 2
            h = jax.nn.relu(jnp.einsum('bchw,co->bohw', x, w1) + b1[None, :, None, None])
            ks = jax.nn.relu(jnp.einsum('bohw,o->bhw', h, w2[:, 0]) + b2[0]) * 20.0 + 1.0
            sigma = ks / 3.0
            logits = -gauss_kernel[None, None, None] / (2.0 * sigma[..., None, None] ** 2)
            wgt = jnp.exp(logits)
            wgt = wgt / jnp.sum(wgt, axis=(-2, -1), keepdims=True)
            wflat = wgt.reshape(Bx, Hx, Wx, Kx * Kx)
            xp = jnp.pad(x, ((0, 0), (0, 0), (r, r), (r, r)))

            def step(acc, idx):
                u = idx // Kx
                v = idx % Kx
                xs = lax.dynamic_slice(xp, (0, 0, u, v), (Bx, Cx, Hx, Wx))
                wk = lax.dynamic_slice_in_dim(wflat, idx, 1, axis=3)[..., 0]
                return (acc + xs * wk[:, None, :, :], None)
            low_freq, _ = lax.scan(step, jnp.zeros_like(x), jnp.arange(Kx * Kx))
            enhanced = x + low_freq
            mu = jnp.mean(enhanced, axis=(2, 3), keepdims=True)
            var = jnp.var(enhanced, axis=(2, 3), keepdims=True)
            return (enhanced - mu) / jnp.sqrt(var + 1e-05)
        key = jax.random.key(seed)
        k1, k2, k3, k4, k5 = jax.random.split(key, 5)
        x = jax.random.normal(k1, (B, C, H, W), dtype=jnp.float32)
        off = jnp.arange(K, dtype=jnp.float32) - R
        gauss_kernel = off[:, None] ** 2 + off[None, :] ** 2
        w1 = jax.random.normal(k2, (C, HIDDEN), dtype=jnp.float32) * (1.0 / np.sqrt(C))
        b1 = jax.random.normal(k3, (HIDDEN,), dtype=jnp.float32) * 0.01
        w2 = jax.random.normal(k4, (HIDDEN, 1), dtype=jnp.float32) * (1.0 / np.sqrt(HIDDEN))
        b2 = jax.random.normal(k5, (1,), dtype=jnp.float32) * 0.01
        return {'x': x, 'gauss_kernel': gauss_kernel, 'w1': w1, 'b1': b1, 'w2': w2, 'b2': b2}
    _L1_conv_all = _L1_conv_setup()
    _L1_conv_in = {k: v for k, v in _L1_conv_all.items() if k in ('gauss_kernel', 'w1', 'b1', 'w2', 'b2')}
    del _L1_conv_all

    def _L2_conv_setup():
        import jax, jax.numpy as jnp
        import numpy as np
        BN_EPS = 1e-05

        def _binarize_ste(w):
            return w + jax.lax.stop_gradient(jnp.sign(w) - w)

        def _conv3x3(x, w):
            return jax.lax.conv_general_dilated(x, w, window_strides=(1, 1), padding=((1, 1), (1, 1)), dimension_numbers=('NCHW', 'OIHW', 'NCHW'))
        key = jax.random.key(seed)
        ks = jax.random.split(key, 5)
        N, C, H, W = (16, 16, 56, 56)
        return {'x': jax.random.normal(ks[0], (N, C, H, W), dtype=jnp.float32), 'shift1': jax.random.normal(ks[1], (1, C, 1, 1), dtype=jnp.float32) * 0.1, 'shift2': jax.random.normal(ks[2], (1, C, 1, 1), dtype=jnp.float32) * 0.1, 'weight': jax.random.normal(ks[3], (C, C, 3, 3), dtype=jnp.float32), 'w1': jax.random.uniform(ks[4], (1, C, 1, 1), dtype=jnp.float32) * 0.001, 'gamma': jnp.ones((C,), dtype=jnp.float32), 'beta': jnp.zeros((C,), dtype=jnp.float32), 'running_mean': jnp.zeros((C,), dtype=jnp.float32), 'running_var': jnp.ones((C,), dtype=jnp.float32)}
    _L2_conv_all = _L2_conv_setup()
    _L2_conv_in = {k: v for k, v in _L2_conv_all.items() if k in ('shift1', 'shift2', 'weight', 'w1', 'gamma', 'beta', 'running_mean', 'running_var')}
    del _L2_conv_all

    def _L3_conv_setup():
        import jax, jax.numpy as jnp
        from jax import lax
        import numpy as np
        B, C, H, W = (8, 16, 64, 64)
        K = 9
        R = (K - 1) // 2
        HIDDEN = 32

        def _forward(x, gauss_kernel, w1, b1, w2, b2):
            Bx, Cx, Hx, Wx = x.shape
            Kx = gauss_kernel.shape[0]
            r = (Kx - 1) // 2
            h = jax.nn.relu(jnp.einsum('bchw,co->bohw', x, w1) + b1[None, :, None, None])
            ks = jax.nn.relu(jnp.einsum('bohw,o->bhw', h, w2[:, 0]) + b2[0]) * 20.0 + 1.0
            sigma = ks / 3.0
            logits = -gauss_kernel[None, None, None] / (2.0 * sigma[..., None, None] ** 2)
            wgt = jnp.exp(logits)
            wgt = wgt / jnp.sum(wgt, axis=(-2, -1), keepdims=True)
            wflat = wgt.reshape(Bx, Hx, Wx, Kx * Kx)
            xp = jnp.pad(x, ((0, 0), (0, 0), (r, r), (r, r)))

            def step(acc, idx):
                u = idx // Kx
                v = idx % Kx
                xs = lax.dynamic_slice(xp, (0, 0, u, v), (Bx, Cx, Hx, Wx))
                wk = lax.dynamic_slice_in_dim(wflat, idx, 1, axis=3)[..., 0]
                return (acc + xs * wk[:, None, :, :], None)
            low_freq, _ = lax.scan(step, jnp.zeros_like(x), jnp.arange(Kx * Kx))
            enhanced = x + low_freq
            mu = jnp.mean(enhanced, axis=(2, 3), keepdims=True)
            var = jnp.var(enhanced, axis=(2, 3), keepdims=True)
            return (enhanced - mu) / jnp.sqrt(var + 1e-05)
        key = jax.random.key(seed)
        k1, k2, k3, k4, k5 = jax.random.split(key, 5)
        x = jax.random.normal(k1, (B, C, H, W), dtype=jnp.float32)
        off = jnp.arange(K, dtype=jnp.float32) - R
        gauss_kernel = off[:, None] ** 2 + off[None, :] ** 2
        w1 = jax.random.normal(k2, (C, HIDDEN), dtype=jnp.float32) * (1.0 / np.sqrt(C))
        b1 = jax.random.normal(k3, (HIDDEN,), dtype=jnp.float32) * 0.01
        w2 = jax.random.normal(k4, (HIDDEN, 1), dtype=jnp.float32) * (1.0 / np.sqrt(HIDDEN))
        b2 = jax.random.normal(k5, (1,), dtype=jnp.float32) * 0.01
        return {'x': x, 'gauss_kernel': gauss_kernel, 'w1': w1, 'b1': b1, 'w2': w2, 'b2': b2}
    _L3_conv_all = _L3_conv_setup()
    _L3_conv_in = {k: v for k, v in _L3_conv_all.items() if k in ('gauss_kernel', 'w1', 'b1', 'w2', 'b2')}
    del _L3_conv_all
    return {'x': x, 'L0_conv_ln_w': _L0_conv_in['ln_w'], 'L0_conv_ln_b': _L0_conv_in['ln_b'], 'L0_conv_w01': _L0_conv_in['w01'], 'L0_conv_b01': _L0_conv_in['b01'], 'L0_conv_w11': _L0_conv_in['w11'], 'L0_conv_b11': _L0_conv_in['b11'], 'L0_conv_w21': _L0_conv_in['w21'], 'L0_conv_b21': _L0_conv_in['b21'], 'L0_conv_w02': _L0_conv_in['w02'], 'L0_conv_b02': _L0_conv_in['b02'], 'L0_conv_w12': _L0_conv_in['w12'], 'L0_conv_b12': _L0_conv_in['b12'], 'L0_conv_w22': _L0_conv_in['w22'], 'L0_conv_b22': _L0_conv_in['b22'], 'L0_conv_proj_w': _L0_conv_in['proj_w'], 'L0_conv_proj_b': _L0_conv_in['proj_b'], 'L1_conv_gauss_kernel': _L1_conv_in['gauss_kernel'], 'L1_conv_w1': _L1_conv_in['w1'], 'L1_conv_b1': _L1_conv_in['b1'], 'L1_conv_w2': _L1_conv_in['w2'], 'L1_conv_b2': _L1_conv_in['b2'], 'L2_conv_shift1': _L2_conv_in['shift1'], 'L2_conv_shift2': _L2_conv_in['shift2'], 'L2_conv_weight': _L2_conv_in['weight'], 'L2_conv_w1': _L2_conv_in['w1'], 'L2_conv_gamma': _L2_conv_in['gamma'], 'L2_conv_beta': _L2_conv_in['beta'], 'L2_conv_running_mean': _L2_conv_in['running_mean'], 'L2_conv_running_var': _L2_conv_in['running_var'], 'L3_conv_gauss_kernel': _L3_conv_in['gauss_kernel'], 'L3_conv_w1': _L3_conv_in['w1'], 'L3_conv_b1': _L3_conv_in['b1'], 'L3_conv_w2': _L3_conv_in['w2'], 'L3_conv_b2': _L3_conv_in['b2']}

def reference(x, L0_conv_ln_w, L0_conv_ln_b, L0_conv_w01, L0_conv_b01, L0_conv_w11, L0_conv_b11, L0_conv_w21, L0_conv_b21, L0_conv_w02, L0_conv_b02, L0_conv_w12, L0_conv_b12, L0_conv_w22, L0_conv_b22, L0_conv_proj_w, L0_conv_proj_b, L1_conv_gauss_kernel, L1_conv_w1, L1_conv_b1, L1_conv_w2, L1_conv_b2, L2_conv_shift1, L2_conv_shift2, L2_conv_weight, L2_conv_w1, L2_conv_gamma, L2_conv_beta, L2_conv_running_mean, L2_conv_running_var, L3_conv_gauss_kernel, L3_conv_w1, L3_conv_b1, L3_conv_w2, L3_conv_b2):
    import jax
    import jax.numpy as jnp

    def _L0_conv_ref(x, ln_w, ln_b, w01, b01, w11, b11, w21, b21, w02, b02, w12, b12, w22, b22, proj_w, proj_b):
        import jax, jax.numpy as jnp
        import numpy as np
        B, C, H, W = (8, 16, 64, 64)
        HEADS = 8
        EPS_LN = 1e-05
        EPS_L2 = 1e-12

        def _dwconv(x, w, b):
            kh, kw = (w.shape[2], w.shape[3])
            y = jax.lax.conv_general_dilated(x, w, (1, 1), ((kh // 2, kh // 2), (kw // 2, kw // 2)), dimension_numbers=('NCHW', 'OIHW', 'NCHW'), feature_group_count=x.shape[1])
            return y + b[None, :, None, None]

        def _proj(x, w, b):
            return jnp.einsum('bchw,oc->bohw', x, w) + b[None, :, None, None]

        def _l2norm(x):
            return x / jnp.maximum(jnp.linalg.norm(x, axis=-1, keepdims=True), EPS_L2)

        def _split_h(t):
            b, c, h, w = t.shape
            cp = c // HEADS
            return t.reshape(b, HEADS, cp, h, w).transpose(0, 1, 3, 4, 2).reshape(b, HEADS, h, w * cp)

        def _split_w(t):
            b, c, h, w = t.shape
            cp = c // HEADS
            return t.reshape(b, HEADS, cp, h, w).transpose(0, 1, 4, 3, 2).reshape(b, HEADS, w, h * cp)

        def _merge_h(t, h, w):
            b = t.shape[0]
            cp = t.shape[-1] // w
            return t.reshape(b, HEADS, h, w, cp).transpose(0, 1, 4, 2, 3).reshape(b, HEADS * cp, h, w)

        def _merge_w(t, h, w):
            b = t.shape[0]
            cp = t.shape[-1] // h
            return t.reshape(b, HEADS, w, h, cp).transpose(0, 1, 4, 3, 2).reshape(b, HEADS * cp, h, w)
        b, c, h, w = x.shape
        residual = x
        mu = jnp.mean(x, axis=1, keepdims=True)
        var = jnp.var(x, axis=1, keepdims=True)
        x1 = (x - mu) / jnp.sqrt(var + EPS_LN) * ln_w[None, :, None, None] + ln_b[None, :, None, None]
        out1 = _dwconv(x1, w01, b01) + _dwconv(x1, w11, b11) + _dwconv(x1, w21, b21)
        out2 = _dwconv(x1, w02, b02) + _dwconv(x1, w12, b12) + _dwconv(x1, w22, b22)
        out1 = _proj(out1, proj_w, proj_b)
        out2 = _proj(out2, proj_w, proj_b)
        k1 = _split_h(out1)
        v1 = k1
        k2 = _split_w(out2)
        v2 = k2
        q2 = _split_w(out1)
        q1 = _split_h(out2)
        q1 = _l2norm(q1)
        k1 = _l2norm(k1)
        q2 = _l2norm(q2)
        k2 = _l2norm(k2)
        attn1 = jax.nn.softmax(jnp.einsum('bnid,bnjd->bnij', q1, k1), axis=-1)
        out3 = jnp.einsum('bnij,bnjd->bnid', attn1, v1) + q1
        attn2 = jax.nn.softmax(jnp.einsum('bnid,bnjd->bnij', q2, k2), axis=-1)
        out4 = jnp.einsum('bnij,bnjd->bnid', attn2, v2) + q2
        out3 = _merge_h(out3, h, w)
        out4 = _merge_w(out4, h, w)
        return _proj(out3, proj_w, proj_b) + _proj(out4, proj_w, proj_b) + residual

    def _L1_conv_ref(x, gauss_kernel, w1, b1, w2, b2):
        import jax, jax.numpy as jnp
        from jax import lax
        import numpy as np
        B, C, H, W = (8, 16, 64, 64)
        K = 9
        R = (K - 1) // 2
        HIDDEN = 32

        def _forward(x, gauss_kernel, w1, b1, w2, b2):
            Bx, Cx, Hx, Wx = x.shape
            Kx = gauss_kernel.shape[0]
            r = (Kx - 1) // 2
            h = jax.nn.relu(jnp.einsum('bchw,co->bohw', x, w1) + b1[None, :, None, None])
            ks = jax.nn.relu(jnp.einsum('bohw,o->bhw', h, w2[:, 0]) + b2[0]) * 20.0 + 1.0
            sigma = ks / 3.0
            logits = -gauss_kernel[None, None, None] / (2.0 * sigma[..., None, None] ** 2)
            wgt = jnp.exp(logits)
            wgt = wgt / jnp.sum(wgt, axis=(-2, -1), keepdims=True)
            wflat = wgt.reshape(Bx, Hx, Wx, Kx * Kx)
            xp = jnp.pad(x, ((0, 0), (0, 0), (r, r), (r, r)))

            def step(acc, idx):
                u = idx // Kx
                v = idx % Kx
                xs = lax.dynamic_slice(xp, (0, 0, u, v), (Bx, Cx, Hx, Wx))
                wk = lax.dynamic_slice_in_dim(wflat, idx, 1, axis=3)[..., 0]
                return (acc + xs * wk[:, None, :, :], None)
            low_freq, _ = lax.scan(step, jnp.zeros_like(x), jnp.arange(Kx * Kx))
            enhanced = x + low_freq
            mu = jnp.mean(enhanced, axis=(2, 3), keepdims=True)
            var = jnp.var(enhanced, axis=(2, 3), keepdims=True)
            return (enhanced - mu) / jnp.sqrt(var + 1e-05)
        return _forward(x, gauss_kernel, w1, b1, w2, b2)

    def _L2_conv_ref(x, shift1, shift2, weight, w1, gamma, beta, running_mean, running_var):
        import jax, jax.numpy as jnp
        import numpy as np
        BN_EPS = 1e-05

        def _binarize_ste(w):
            return w + jax.lax.stop_gradient(jnp.sign(w) - w)

        def _conv3x3(x, w):
            return jax.lax.conv_general_dilated(x, w, window_strides=(1, 1), padding=((1, 1), (1, 1)), dimension_numbers=('NCHW', 'OIHW', 'NCHW'))
        wb = _binarize_ste(weight)
        out1 = _conv3x3(x + shift1, wb)
        out2 = _conv3x3(x + shift2, wb)
        out = out1 + w1 * out2
        c = lambda v: v.reshape(1, -1, 1, 1)
        inv = jax.lax.rsqrt(c(running_var) + BN_EPS)
        out = (out - c(running_mean)) * inv * c(gamma) + c(beta)
        out = out + x
        return jnp.clip(out, -1.0, 1.0)

    def _L3_conv_ref(x, gauss_kernel, w1, b1, w2, b2):
        import jax, jax.numpy as jnp
        from jax import lax
        import numpy as np
        B, C, H, W = (8, 16, 64, 64)
        K = 9
        R = (K - 1) // 2
        HIDDEN = 32

        def _forward(x, gauss_kernel, w1, b1, w2, b2):
            Bx, Cx, Hx, Wx = x.shape
            Kx = gauss_kernel.shape[0]
            r = (Kx - 1) // 2
            h = jax.nn.relu(jnp.einsum('bchw,co->bohw', x, w1) + b1[None, :, None, None])
            ks = jax.nn.relu(jnp.einsum('bohw,o->bhw', h, w2[:, 0]) + b2[0]) * 20.0 + 1.0
            sigma = ks / 3.0
            logits = -gauss_kernel[None, None, None] / (2.0 * sigma[..., None, None] ** 2)
            wgt = jnp.exp(logits)
            wgt = wgt / jnp.sum(wgt, axis=(-2, -1), keepdims=True)
            wflat = wgt.reshape(Bx, Hx, Wx, Kx * Kx)
            xp = jnp.pad(x, ((0, 0), (0, 0), (r, r), (r, r)))

            def step(acc, idx):
                u = idx // Kx
                v = idx % Kx
                xs = lax.dynamic_slice(xp, (0, 0, u, v), (Bx, Cx, Hx, Wx))
                wk = lax.dynamic_slice_in_dim(wflat, idx, 1, axis=3)[..., 0]
                return (acc + xs * wk[:, None, :, :], None)
            low_freq, _ = lax.scan(step, jnp.zeros_like(x), jnp.arange(Kx * Kx))
            enhanced = x + low_freq
            mu = jnp.mean(enhanced, axis=(2, 3), keepdims=True)
            var = jnp.var(enhanced, axis=(2, 3), keepdims=True)
            return (enhanced - mu) / jnp.sqrt(var + 1e-05)
        return _forward(x, gauss_kernel, w1, b1, w2, b2)

    def _gn(v, G=32, eps=1e-05):
        B_, C_, H_, W_ = v.shape
        g = v.reshape(B_, G, C_ // G, H_, W_)
        m = jnp.mean(g, axis=(2, 3, 4), keepdims=True)
        s = jnp.var(g, axis=(2, 3, 4), keepdims=True)
        return ((g - m) / jnp.sqrt(s + eps)).reshape(v.shape)

    def _ln_c(v, eps=1e-06):
        m = jnp.mean(v, axis=1, keepdims=True)
        s = jnp.var(v, axis=1, keepdims=True)
        return (v - m) / jnp.sqrt(s + eps)

    def _ln_t(v, eps=1e-05):
        m = jnp.mean(v, axis=-1, keepdims=True)
        s = jnp.var(v, axis=-1, keepdims=True)
        return (v - m) / jnp.sqrt(s + eps)

    def _to_tokens(v):
        B_, C_, H_, W_ = v.shape
        return v.reshape(B_, C_, H_ * W_).transpose(0, 2, 1)

    def _from_tokens(t, like):
        B_, C_, H_, W_ = like.shape
        return t.transpose(0, 2, 1).reshape(B_, C_, H_, W_)
    x = _L0_conv_ref(x, L0_conv_ln_w, L0_conv_ln_b, L0_conv_w01, L0_conv_b01, L0_conv_w11, L0_conv_b11, L0_conv_w21, L0_conv_b21, L0_conv_w02, L0_conv_b02, L0_conv_w12, L0_conv_b12, L0_conv_w22, L0_conv_b22, L0_conv_proj_w, L0_conv_proj_b)
    x = _L1_conv_ref(x, L1_conv_gauss_kernel, L1_conv_w1, L1_conv_b1, L1_conv_w2, L1_conv_b2)
    x = _L2_conv_ref(x, L2_conv_shift1, L2_conv_shift2, L2_conv_weight, L2_conv_w1, L2_conv_gamma, L2_conv_beta, L2_conv_running_mean, L2_conv_running_var)
    x = _L3_conv_ref(x, L3_conv_gauss_kernel, L3_conv_w1, L3_conv_b1, L3_conv_w2, L3_conv_b2)
    return x

_drawn_inputs = setup_inputs


def setup_inputs(seed=0):
    import zlib

    import numpy as np

    out = dict(_drawn_inputs(seed))
    spreads = {'L0_conv_ln_w': (1.0, 0.6),
     'L0_conv_ln_b': (0.0, 0.796),
     'L0_conv_b01': (0.0, 0.435),
     'L0_conv_b11': (0.0, 0.288),
     'L0_conv_b21': (0.0, 0.298),
     'L0_conv_b02': (0.0, 0.425),
     'L0_conv_b12': (0.0, 0.353),
     'L0_conv_b22': (0.0, 0.313),
     'L0_conv_proj_b': (0.0, 0.1),
     'L2_conv_gamma': (1.0, 0.2),
     'L2_conv_beta': (0.0, 0.1),
     'L2_conv_running_mean': (0.0, 0.297),
     'L2_conv_running_var': (1.0, 0.2)}
    factors = {'L2_conv_shift2': 27.979, 'L2_conv_w1': 42.577, 'L3_conv_b1': 5.557}
    for name, (base, spread) in spreads.items():
        noise = np.random.default_rng([zlib.crc32(name.encode()), seed]).standard_normal(out[name].shape)
        drawn = base * np.exp(spread * noise) if base else spread * noise
        out[name] = jnp.asarray(drawn.astype(out[name].dtype))
    for name, factor in factors.items():
        out[name] = (out[name] * factor).astype(out[name].dtype)
    return out
```

```python
from contextlib import ExitStack

import numpy as np

import concourse.bass as bass
from concourse import mybir

F32 = mybir.dt.float32
ALU = mybir.AluOpType
ACT = mybir.ActivationFunctionType

P = 128
B, C, H, W = 8, 16, 64, 64
HEADS = 8
CP = C // HEADS
PIX = H * W
BANK = 512
ROWS = BANK // W
CHUNKS = PIX // BANK
PXT = PIX // P

KW = (21, 11, 7)
TAPS = sum(KW)
CENTRE = KW[0] // 2
BAND = H + W - 1

KG = 9
R = KG // 2
BLK = 8
PADDED = H + 2 * R
CB = W // BLK
RB = H // BLK
QC = 2 * BLK
HIDDEN = 32
HALF = B // 2
OFF_BAND = -1e34

LN_EPS = 1e-5
L2_EPS_SQ = 1e-24
NORM_EPS = 1e-5

VECS = ["ln_w", "ln_b", "proj_b", "shift1", "shift2", "gamma", "beta", "mean", "var", "w1",
        "g1_b1", "g1_b2", "g3_b1", "g3_b2"]
VEC = {name: i for i, name in enumerate(VECS)}


def spread(ap, shape):
    return ap.broadcast_to(list(shape))


def build(nc, d, out):
    keep = ExitStack()
    with keep:
        def sb(stack, name, shape):
            return stack.enter_context(nc.sbuf_tensor(name, shape, F32))

        def sem(name):
            return keep.enter_context(nc.semaphore(name))

        ident = sb(keep, "ident", [P, P])
        vec = sb(keep, "vec", [P, len(VECS)])
        ones = sb(keep, "ones", [P, 1])
        pad_a = sb(keep, "pad_a", [P, PADDED, PADDED])
        pad_b = sb(keep, "pad_b", [P, PADDED, PADDED])
        ps = keep.enter_context(nc.psum_tensor("ps", [P, 8, BANK], F32))

        zeroed = sem("zeroed")
        with ExitStack() as l0:
            x0 = sb(l0, "x0", [P, PIX])
            xrow = sb(l0, "xrow", [P, HEADS, B, H])
            xcol = sb(l0, "xcol", [P, HEADS, B, W])
            toep = sb(l0, "toep", [P, 2, HEADS, W])
            ptab = sb(l0, "ptab", [P, HEADS, HEADS, CP])
            beta = sb(l0, "beta_o", [P, 2, HEADS])
            projblk = sb(l0, "projblk", [P, P])
            const_in = sem("const_in")
            with ExitStack() as ln:
                l0_norm(nc, sem, lambda n, s: sb(ln, n, s), d, ident, vec, ones, pad_a, pad_b, ps, x0,
                        xrow, xcol, toep, ptab, beta, projblk, const_in, zeroed)
            attn = sb(l0, "attn", [P, B, HEADS, H])
            with ExitStack() as hd:
                l0_heads(nc, sem, lambda n, s: sb(hd, n, s), ident, ones, ps,
                         xrow, xcol, toep, ptab, beta, attn)
            with ExitStack() as fin:
                l0_out(nc, sem, lambda n, s: sb(fin, n, s), ident, vec, ps, x0, attn, projblk, pad_a)
        with ExitStack() as g:
            blur(nc, sem, lambda n, s: sb(g, "g1_" + n, s), "g1", d, ident, vec, ps, pad_a, pad_a, None)
        with ExitStack() as c:
            binconv(nc, sem, lambda n, s: sb(c, n, s), d, vec, ps, pad_a, pad_b)
        with ExitStack() as g:
            blur(nc, sem, lambda n, s: sb(g, "g3_" + n, s), "g3", d, ident, vec, ps, pad_b, None, out)


def l0_norm(nc, sem, sb, d, ident, vec, ones, pad_a, pad_b, ps, x0, xrow, xcol, toep, ptab, beta,
            projblk, const_in, zeroed):
    centre = sb("centre", [P, P])
    meansel = sb("meansel", [P, B])
    shift_eye = sb("shift_eye", [TAPS, BAND])
    taps = sb("taps", [TAPS, 2, CP, HEADS])
    nb = len(KW) * C + 1
    bias_lhs = sb("bias_lhs", [nb, 2])
    bias_rhs = sb("bias_rhs", [nb, C])
    xc = sb("xc", [P, PIX])
    sq = sb("sq", [P, PIX])
    var = sb("var", [P, PXT * B])
    std = sb("std", [P, PXT * B])
    rstd = sb("rstd", [P, PXT, B])
    wide = sb("wide", [P, PXT, CP, B, HEADS])

    x_in = [sem(f"x_in{j}") for j in range(4)]
    centred = sem("centred")
    xc_copied = sem("xc_copied")
    squared = sem("squared")
    bias_mm = sem("bias_mm")
    bias_read = sem("bias_read")
    toep_mm = sem("toep_mm")
    toep_read = sem("toep_read")
    var_mm = sem("var_mm")
    eps_added = sem("eps_added")
    rooted = sem("rooted")
    rstd_ready = sem("rstd_ready")
    rstd_wide = [sem(f"rstd_wide{cp}") for cp in range(CP)]
    rstd_spread = sem("rstd_spread")
    scaled = sem("scaled")
    normed = sem("normed")
    turned = sem("turned")
    evac_v = sem("evac_v")
    evac_s = sem("evac_s")
    CONSTS = 11

    with nc.Block() as block:
        @block.sync
        def _(sp):
            xv = d["x"].rearrange("b (n cp) h w -> cp b n (h w)", cp=CP)
            sp.dma_start(centre[:], d["centre"]).then_inc(const_in, 16)
            for j in range(4):
                cols = slice(j * PIX // 4, (j + 1) * PIX // 4)
                for cp in range(CP):
                    sp.dma_start(x0[64 * cp:64 * cp + 64, cols],
                                 xv[cp].rearrange("b n f -> (b n) f")[:, cols]).then_inc(x_in[j], 16)
            for t, name in ((ident, "ident"), (vec, "vec"), (meansel, "meansel"),
                            (shift_eye, "shift_eye"), (taps, "taps"), (bias_lhs, "bias_lhs"),
                            (bias_rhs, "bias_rhs"), (ptab, "ptab"), (projblk, "projblk")):
                sp.dma_start(t[:], d[name]).then_inc(const_in, 16)

        @block.gpsimd
        def _(pool):
            pool.memset(ones[:], 1.0).then_inc(zeroed, 1)
            pool.memset(pad_a[:], 0.0).then_inc(zeroed, 1)
            pool.memset(pad_b[:], 0.0).then_inc(zeroed, 1)

        @block.tensor
        def _(pe):
            pe.wait_ge(const_in, 16 * (CONSTS - 1))
            for j in range(CHUNKS):
                if j % 2 == 0:
                    pe.wait_ge(x_in[j // 2], 32)
                pe.matmul(ps[:, j, :], centre[:], x0[:, j * BANK:(j + 1) * BANK],
                          start=True, stop=True).then_inc(centred, 1)
            pe.wait_ge(xc_copied, 5)
            for t in range(2):
                for w in range(W):
                    s = W - 1 - w
                    for cp in range(CP):
                        mm = pe.matmul(ps[64 * cp:64 * cp + 64, t, HEADS * w:HEADS * w + HEADS],
                                       shift_eye[:, s:s + W], taps[:, t, cp, :], start=True, stop=True)
                mm.then_inc(toep_mm, 1)
            for t in range(2):
                mm = pe.matmul(ps[:, 4, C * t:C * t + C], spread(bias_lhs[:, t:t + 1], [nb, P]),
                               bias_rhs[:], start=True, stop=True)
            mm.then_inc(bias_mm, 1)
            pe.wait_ge(squared, CHUNKS)
            pe.wait_ge(xc_copied, CHUNKS)
            for t in range(PXT):
                mm = pe.matmul(ps[:, 7, B * t:B * t + B], sq[:, P * t:P * t + P], meansel[:],
                               start=True, stop=True)
            mm.then_inc(var_mm, 1)
            pe.wait_ge(toep_read, 2)
            pe.wait_ge(bias_read, 4)
            for t in range(PXT):
                if t % 4 == 0:
                    for cp in range(CP):
                        pe.wait_ge(rstd_wide[cp], t // 4 + 1)
                tr = pe.transpose(ps[:, t // 4, P * (t % 4):P * (t % 4) + P],
                                  wide[:, t].rearrange("p c b n -> p (c b n)"), ident[:])
                if t % 4 == 3:
                    tr.then_inc(rstd_spread, 1)
            for g in range(CHUNKS):
                pe.wait_ge(normed, g + 1)
                for hh in range(ROWS):
                    h = ROWS * g + hh
                    for cp in range(CP):
                        mm = pe.matmul(ps[64 * cp:64 * cp + 64, g, 64 * hh:64 * hh + 64],
                                       sq[:, W * h:W * h + W], ident[:, 64 * cp:64 * cp + 64],
                                       start=True, stop=True)
                mm.then_inc(turned, 1)
            cols = sq[:].rearrange("p (h w) -> p w h", w=W)
            for g in range(CHUNKS):
                if g % 2 == 0:
                    pe.wait_ge(evac_v, g // 2 + 1)
                else:
                    pe.wait_ge(evac_s, g // 2 + 1)
                for ww in range(ROWS):
                    w = ROWS * g + ww
                    for cp in range(CP):
                        mm = pe.matmul(ps[64 * cp:64 * cp + 64, g, 64 * ww:64 * ww + 64],
                                       cols[:, w, :], ident[:, 64 * cp:64 * cp + 64],
                                       start=True, stop=True)
                mm.then_inc(turned, 1)

        def turned_out(lay, g):
            return lay[:].rearrange("p n b h -> p h b n")[:, ROWS * g:ROWS * g + ROWS]

        def turned_in(g):
            return ps[:, g, :].rearrange("p (h b n) -> p h b n", h=ROWS, b=B)

        def widen(copy, j, cp):
            tiles = slice(4 * j, 4 * j + 4)
            copy(wide[:, tiles, cp], spread(rstd[:, tiles, :].unsqueeze(3), [P, 4, B, HEADS]))\
                .then_inc(rstd_wide[cp], 1)

        @block.scalar
        def _(act):
            for j in range(CHUNKS):
                act.wait_ge(xc_copied, j + 1)
                act.activation(sq[:, j * BANK:(j + 1) * BANK], xc[:, j * BANK:(j + 1) * BANK], ACT.Square).then_inc(squared, 1)
            act.wait_ge(eps_added, 1)
            act.activation(std[:], var[:], ACT.Sqrt).then_inc(rooted, 1)
            act.wait_ge(rstd_ready, 1)
            for j in range(CHUNKS):
                widen(act.copy, j, 1)
            for j in range(CHUNKS):
                act.wait_ge(scaled, j + 1)
                act.activation(sq[:, j * BANK:(j + 1) * BANK], xc[:, j * BANK:(j + 1) * BANK],
                               ACT.Identity, bias=vec[:, VEC["ln_b"]:VEC["ln_b"] + 1],
                               scale=vec[:, VEC["ln_w"]:VEC["ln_w"] + 1]).then_inc(normed, 1)
            for lay, base in ((xrow, 0), (xcol, CHUNKS)):
                for g in range(1, CHUNKS, 2):
                    act.wait_ge(turned, base + g + 1)
                    act.copy(turned_out(lay, g), turned_in(g)).then_inc(evac_s, 1)

        @block.vector
        def _(dve):
            for j in range(CHUNKS):
                dve.wait_ge(centred, j + 1)
                dve.tensor_copy(xc[:, j * BANK:(j + 1) * BANK], ps[:, j, :]).then_inc(xc_copied, 1)
            for t in range(2):
                dve.wait_ge(toep_mm, t + 1)
                dve.tensor_copy(toep[:, t], ps[:, t, :].rearrange("p (w n) -> p n w", n=HEADS))\
                    .then_inc(toep_read, 1)
            dve.wait_ge(bias_mm, 1)
            for t in range(2):
                for cp in range(CP):
                    src = ps[64 * cp:64 * cp + 64, 4, C * t:C * t + C].rearrange("p (n c) -> p c n", c=CP)
                    dve.tensor_copy(beta[64 * cp:64 * cp + 64, t, :], src[:, cp, :]).then_inc(bias_read, 1)
            dve.wait_ge(var_mm, 1)
            dve.tensor_scalar(var[:], ps[:, 7, 0:PXT * B], LN_EPS, None, ALU.add).then_inc(eps_added, 1)
            dve.wait_ge(rooted, 1)
            dve.reciprocal(rstd[:].rearrange("p t b -> p (t b)"), std[:]).then_inc(rstd_ready, 1)
            dve.wait_ge(rstd_ready, 1)
            for j in range(CHUNKS):
                widen(dve.tensor_copy, j, 0)
            for j in range(CHUNKS):
                dve.wait_ge(rstd_spread, j + 1)
                dve.tensor_tensor(xc[:, j * BANK:(j + 1) * BANK], xc[:, j * BANK:(j + 1) * BANK],
                                  ps[:, j, :], ALU.mult).then_inc(scaled, 1)
            for lay, base in ((xrow, 0), (xcol, CHUNKS)):
                for g in range(0, CHUNKS, 2):
                    dve.wait_ge(turned, base + g + 1)
                    dve.tensor_copy(turned_out(lay, g), turned_in(g)).then_inc(evac_v, 1)


def l0_heads(nc, sem, sb, ident, ones, ps, xrow, xcol, toep, ptab, beta, attn):
    wts = [sb(f"wts{t}", [P, HEADS, CP, W]) for t in range(2)]
    o1r = [sb(f"o1r{s}", [P, B, H]) for s in range(2)]
    o2c = [sb(f"o2c{s}", [P, B, W]) for s in range(2)]
    o1c = sb("o1c", [P, B, W])
    o2r = sb("o2r", [P, B, H])
    sqs = sb("sqs", [P, 4, BANK])
    nsq = sb("nsq", [P, 16])
    half = sb("half", [P, 16])
    rn = sb("rn", [P, 16])
    q1 = sb("q1", [P, B, H])
    k1 = sb("k1", [P, B, H])
    q2 = sb("q2", [P, B, W])
    k2 = sb("k2", [P, B, W])
    e = [sb(f"e{t}", [P, B, H]) for t in range(2)]
    rz = sb("rz", [P, 8])

    wts_ready = sem("wts_ready")
    conv_mm = sem("conv_mm")
    conv_out = sem("conv_out")
    tr_mm = sem("tr_mm")
    o1c_ready = sem("o1c_ready")
    o2r_ready = sem("o2r_ready")
    sq_ready = sem("sq_ready")
    nsq_mm = sem("nsq_mm")
    nsq_ready = sem("nsq_ready")
    half_ready = sem("half_ready")
    rn_ready = sem("rn_ready")
    rn_spread = sem("rn_spread")
    unit = sem("unit")
    score_mm = sem("score_mm")
    exped = sem("exped")
    z_mm = sem("z_mm")
    rz_ready = sem("rz_ready")
    rz_spread = sem("rz_spread")
    prob = sem("prob")
    av_mm = sem("av_mm")
    attn_out = sem("attn_out")

    QUAD = [(64 * cp, 64 * cp + 64) for cp in range(CP)]

    def wait_apart(eng, semaphore, value):
        eng.wait_ge(semaphore, value)
        eng.nop(nofuse=True)

    def conv(pe, m, k):
        t, n = divmod(k, HEADS)
        if n == 0:
            pe.wait_ge(wts_ready, 2 * m + t + 1)
            if not (isinstance(m, int) and m == 0):
                pe.wait_ge(conv_out, 2 * (m - 1) + t + 1)
        src = (xrow, xcol)[t]
        mm = pe.matmul(ps[:, t, :], wts[t][:, n].rearrange("p c w -> p (c w)"),
                       src[:, n].rearrange("p b h -> p (b h)"), start=(n == 0), stop=(n == HEADS - 1))
        if n == HEADS - 1:
            mm.then_inc(conv_mm, 1)

    def turn(pe, a, s):
        if not (isinstance(a, int) and a == 0):
            pe.wait_ge(exped, 2 * a)
        wait_apart(pe, conv_out, 2 * a + 2)
        for first in range(2):
            for b in range(B):
                for i, (src, bank) in enumerate(((o1r[s], 2), (o2c[s], 3))):
                    lo, hi = QUAD[first ^ i]
                    mm = pe.matmul(ps[lo:hi, bank, 64 * b:64 * b + 64], src[lo:hi, b, :],
                                   ident[lo:hi, lo:hi], start=True, stop=True)
                    if first == 1 and b == B - 1:
                        mm.then_inc(tr_mm, 1)

    def square_sums(pe, a):
        if not (isinstance(a, int) and a == 0):
            pe.wait_ge(prob, 2 * a)
        for t in range(4):
            pe.wait_ge(sq_ready, 4 * a + t + 1)
            for k in range(4):
                mm = pe.matmul(ps[:, 4, 4 * t + k:4 * t + k + 1], sqs[:, t, P * k:P * k + P],
                               ones[:], start=True, stop=True)
        mm.then_inc(nsq_mm, 1)

    def spread_norms(pe, a):
        pe.wait_ge(rn_ready, a + 1)
        if not (isinstance(a, int) and a == 0):
            pe.wait_ge(attn_out, a)
        for t in range(4):
            for k in range(4):
                tr = pe.transpose(ps[:, 4 + t, P * k:P * k + P],
                                  spread(rn[:, 4 * t + k:4 * t + k + 1], [P, P]), ident[:])
            tr.then_inc(rn_spread, 1)

    def scores(pe, a):
        for t, (q, k) in enumerate(((q1, k1), (q2, k2))):
            pe.wait_ge(unit, 4 * a + 2 * t + 2)
            if t == 0:
                pe.wait_ge(o1c_ready, a + 1)
                pe.wait_ge(o2r_ready, a + 1)
            for b in range(B):
                for lo, hi in QUAD:
                    mm = pe.matmul(ps[lo:hi, 2 + t, 64 * b:64 * b + 64], k[:, b, :], q[:, b, :],
                                   start=True, stop=True)
            mm.then_inc(score_mm, 1)

    def z_sums(pe, a):
        pe.wait_ge(exped, 2 * a + 2)
        for t in range(2):
            for k in range(4):
                mm = pe.matmul(ps[:, 2, 4 * t + k:4 * t + k + 1],
                               e[t][0:64, 2 * k:2 * k + 2, :].rearrange("p b i -> p (b i)"),
                               ones[0:64, :], start=True, stop=True)
        mm.then_inc(z_mm, 1)

    def spread_z(pe, a):
        pe.wait_ge(rz_ready, a + 1)
        for t in range(2):
            for k in range(4):
                tr = pe.transpose(ps[:, 4 + t, P * k:P * k + P],
                                  spread(rz[:, 4 * t + k:4 * t + k + 1], [P, P]), ident[:])
            tr.then_inc(rz_spread, 1)

    def outputs(pe, a):
        wait_apart(pe, prob, 2 * a + 2)
        for first in range(2):
            for b0 in range(B // 2):
                steps = []
                for i, (b, bank) in enumerate(((b0, 7), (b0 + 4, 6))):
                    lo, hi = QUAD[first ^ i]
                    o = ps[lo:hi, bank, 64 * b0:64 * b0 + 64]
                    steps.append([(o, o1c[lo:hi, b, :], e[0][lo:hi, b, :]),
                                  (o, e[1][lo:hi, b, :], o2r[lo:hi, b, :]),
                                  (o, q2[lo:hi, b, :], ident[lo:hi, lo:hi])])
                for k in range(3):
                    for st in steps:
                        mm = pe.matmul(*st[k], start=(k == 0), stop=(k == 2))
        mm.then_inc(av_mm, 1)

    def pe_head(pe, m, s, conv_on, attn_on):
        a = m - 1
        k = 0

        def some(n):
            nonlocal k
            if conv_on:
                for _ in range(n):
                    conv(pe, m, k)
                    k += 1
        some(2)
        for step, n in ((lambda: turn(pe, a, 1 - s), 3), (lambda: square_sums(pe, a), 3),
                        (lambda: spread_norms(pe, a), 3), (lambda: scores(pe, a), 2),
                        (lambda: z_sums(pe, a), 2), (lambda: spread_z(pe, a), 1),
                        (lambda: outputs(pe, a), 0)):
            if attn_on:
                step()
            some(n)

    def act_head(act, m, s, conv_on, attn_on):
        a = m - 1

        def square(t, src):
            act.activation(sqs[:, t, :], src[:].rearrange("p b h -> p (b h)"), ACT.Square).then_inc(sq_ready, 1)

        def conv_evac(t):
            act.wait_ge(conv_mm, 2 * m + t + 1)
            dst = (o1r, o2c)[t][s]
            if not (isinstance(m, int) and m < 2):
                act.wait_ge(tr_mm, 2 * (m - 1))
            act.activation(dst[:].rearrange("p b h -> p (b h)"), ps[:, t, :], ACT.Identity,
                           bias=beta[:, t, bass.ds(m, 1)], scale=1.0).then_inc(conv_out, 1)

        if attn_on:
            act.wait_ge(tr_mm, 2 * a + 2)
            if not (isinstance(a, int) and a == 0):
                act.wait_ge(av_mm, a)
            act.activation(o2r[:].rearrange("p b h -> p (b h)"), ps[:, 3, :], ACT.Identity)\
                .then_inc(o2r_ready, 1)
            act.wait_ge(conv_out, 2 * a + 2)
            if not (isinstance(a, int) and a == 0):
                act.wait_ge(nsq_mm, a)
            act.wait_ge(o2r_ready, a + 1)
            square(0, o2r)
            square(1, o1r[1 - s])
            act.wait_ge(o1c_ready, a + 1)
            square(2, o1c)
            square(3, o2c[1 - s])
        if conv_on:
            conv_evac(0)
        if attn_on:
            for t in range(2):
                act.wait_ge(score_mm, 2 * a + t + 1)
                if t == 0 and not (isinstance(a, int) and a == 0):
                    act.wait_ge(av_mm, a)
                act.activation(e[t][:].rearrange("p b h -> p (b h)"), ps[:, 2 + t, :], ACT.Exp)\
                    .then_inc(exped, 1)
        if conv_on:
            conv_evac(1)

    def dve_head(dve, a, s):
        first = isinstance(a, int) and a == 0
        dve.wait_ge(tr_mm, 2 * a + 2)
        if not first:
            dve.wait_ge(av_mm, a)
        dve.tensor_copy(o1c[:].rearrange("p b h -> p (b h)"), ps[:, 2, :]).then_inc(o1c_ready, 1)
        dve.wait_ge(nsq_mm, a + 1)
        if not first:
            dve.wait_ge(rn_ready, a)
        dve.tensor_scalar(nsq[:], ps[:, 4, 0:16], L2_EPS_SQ, None, ALU.max).then_inc(nsq_ready, 1)
        dve.wait_ge(o1c_ready, a + 1)
        for t, (dst, src) in enumerate(((q1, o2r), (k1, o1r[s]), (q2, o1c), (k2, o2c[s]))):
            dve.wait_ge(rn_spread, 4 * a + t + 1)
            if t == 0:
                dve.wait_ge(o2r_ready, a + 1)
            dve.tensor_tensor(dst[:].rearrange("p b h -> p (b h)"), src[:].rearrange("p b h -> p (b h)"),
                              ps[:, 4 + t, :], ALU.mult).then_inc(unit, 1)
        dve.wait_ge(z_mm, a + 1)
        dve.reciprocal(rz[:], ps[:, 2, 0:8]).then_inc(rz_ready, 1)
        for t in range(2):
            dve.wait_ge(rz_spread, 2 * a + t + 1)
            ev = e[t][:].rearrange("p b h -> p (b h)")
            dve.tensor_tensor(ev, ev, ps[:, 4 + t, :], ALU.mult).then_inc(prob, 1)
        dve.wait_ge(av_mm, a + 1)
        for i, bank in enumerate((7, 6)):
            ins = dve.tensor_tensor(attn[:, 4 * i:4 * i + 4, bass.ds(a, 1), :].rearrange("p b o h -> p b (o h)"),
                                    ps[:, bank, 0:256].rearrange("p (b h) -> p b h", b=4),
                                    q1[:, 4 * i:4 * i + 4, :], ALU.add)
        ins.then_inc(attn_out, 1)

    def pool_weights(pool, m, t):
        if not (isinstance(m, int) and m == 0):
            wait_apart(pool, conv_mm, 2 * (m - 1) + t + 1)
        shape = [P, HEADS, CP, W]
        pool.tensor_tensor(wts[t][:], spread(toep[:, t].unsqueeze(2), shape),
                           spread(ptab[:, :, bass.ds(m, 1), :].rearrange("p n o c -> p n (o c)").unsqueeze(3), shape),
                           ALU.mult).then_inc(wts_ready, 1)

    def pool_head(pool, m, build_on, attn_on):
        a = m - 1
        if build_on:
            pool_weights(pool, m + 1, 0)
        if attn_on:
            pool.wait_ge(nsq_ready, a + 1)
            if not (isinstance(a, int) and a == 0):
                pool.wait_ge(rn_spread, 4 * a)
            pool.tensor_tensor(rn[:], nsq[:], half[:], ALU.pow).then_inc(rn_ready, 1)
        if build_on:
            pool_weights(pool, m + 1, 1)

    with nc.Block() as block:
        @block.tensor
        def _(pe):
            pe_head(pe, 0, 0, True, False)
            pe_head(pe, 1, 1, True, True)
            with pe.Fori(0, 3) as i:
                for p in range(2):
                    pe_head(pe, 2 * i + 2 + p, p, True, True)
            pe_head(pe, HEADS, 0, False, True)

        @block.scalar
        def _(act):
            act_head(act, 0, 0, True, False)
            act_head(act, 1, 1, True, True)
            with act.Fori(0, 3) as i:
                for p in range(2):
                    act_head(act, 2 * i + 2 + p, p, True, True)
            act_head(act, HEADS, 0, False, True)

        @block.vector
        def _(dve):
            dve_head(dve, 0, 0)
            with dve.Fori(0, 3) as i:
                for p in range(2):
                    dve_head(dve, 2 * i + 1 + p, 1 - p)
            dve_head(dve, HEADS - 1, 1)

        @block.gpsimd
        def _(pool):
            pool.memset(half[:], -0.5).then_inc(half_ready, 1)
            pool_weights(pool, 0, 0)
            pool_weights(pool, 0, 1)
            pool.wait_ge(half_ready, 1)
            pool_head(pool, 0, True, False)
            pool_head(pool, 1, True, True)
            with pool.Fori(0, 5) as i:
                pool_head(pool, i + 2, True, True)
            pool_head(pool, HEADS - 1, False, True)
            pool_head(pool, HEADS, False, True)


def l0_out(nc, sem, sb, ident, vec, ps, x0, attn, projblk, pad):
    img = sb("img", [P, PIX])
    bias2 = sb("bias2", [P, 1])
    turned = sem("o_turned")
    copied_v = sem("o_copied_v")
    copied_s = sem("o_copied_s")
    projected = sem("o_projected")
    added = sem("o_added")
    bias2_ready = sem("o_bias2")
    planes = attn[:].rearrange("p b n h -> p h (b n)")

    def copied(eng, g):
        eng.wait_ge(copied_v if g % 2 == 0 else copied_s, g // 2 + 1)

    with nc.Block() as block:
        @block.tensor
        def _(pe):
            def project(g):
                copied(pe, g)
                pe.matmul(ps[:, g, :], projblk[:], img[:, BANK * g:BANK * g + BANK],
                          start=True, stop=True).then_inc(projected, 1)
            for g in range(CHUNKS):
                for hh in range(ROWS):
                    for cp in range(CP):
                        mm = pe.matmul(ps[64 * cp:64 * cp + 64, g, W * hh:W * hh + W],
                                       planes[:, ROWS * g + hh], ident[:, 64 * cp:64 * cp + 64],
                                       start=True, stop=True)
                mm.then_inc(turned, 1)
                if g > 0:
                    project(g - 1)
            project(CHUNKS - 1)

        @block.scalar
        def _(act):
            for g in range(1, CHUNKS, 2):
                act.wait_ge(turned, g + 1)
                act.copy(img[:, BANK * g:BANK * g + BANK], ps[:, g, :]).then_inc(copied_s, 1)

        @block.vector
        def _(dve):
            pb = vec[:, VEC["proj_b"]:VEC["proj_b"] + 1]
            dve.tensor_tensor(bias2[:], pb, pb, ALU.add).then_inc(bias2_ready, 1)
            dve.wait_ge(bias2_ready, 1)

            def add(g):
                dve.wait_ge(projected, g + 1)
                dve.scalar_tensor_tensor(
                    out=pad[:, R + ROWS * g:R + ROWS * g + ROWS, R:R + W],
                    in0=ps[:, g, :].rearrange("p (h w) -> p h w", w=W), scalar=bias2[:, 0:1],
                    in1=x0[:, BANK * g:BANK * g + BANK].rearrange("p (h w) -> p h w", w=W),
                    op0=ALU.add, op1=ALU.add).then_inc(added, 1)
            for g in range(0, CHUNKS, 2):
                dve.wait_ge(turned, g + 1)
                dve.tensor_copy(img[:, BANK * g:BANK * g + BANK], ps[:, g, :]).then_inc(copied_v, 1)
                if g > 0:
                    add(g - 2)
                    add(g - 1)
            add(CHUNKS - 2)
            add(CHUNKS - 1)


def blur(nc, sem_, sb, tag, d, ident, vec, ps, pad, normed_to, out):
    def sem(name):
        return sem_(f"{tag}_{name}")

    gband = sb("gband", [P, 2, BLK * BLK])
    gmask = sb("gmask", [P, 2, BLK * BLK])
    w1 = sb("w1", [P, 2, P])
    w2 = sb("w2", [P, HALF])
    perm = sb("perm", [P, P])
    tile = [sb(f"tile{s}", [P, CB, BLK, QC]) for s in range(2)]
    xt = [sb(f"xt{s}", [P, CB, B, 2 * C]) for s in range(2)]
    hid = [sb(f"hid{i}", [P, CB, BLK, BLK]) for i in range(2)]
    sm = [sb(f"sm{i}", [P, 4 * B]) for i in range(3)]
    scl = [sb(f"scl{s}", [P, 4, B]) for s in range(2)]
    wgt = [sb(f"wgt{u}", [P, 2, CB, BLK * BLK]) for u in range(B)]
    num = [sb(f"num{s}", [P, BANK]) for s in range(2)]
    rz = sb("rzb", [P, 4, HALF])
    mix = sb("mix", [P, 4, CP, B, HEADS])
    stats = sb("stats", [P, RB, 6])
    mv = sb("mv", [P, 2])
    std = sb("stdb", [P, 2])
    rstd = sb("rstdb", [P, 1])
    result = sb("result", [P, PIX]) if out is not None else None

    loaded = sem("loaded")
    const_ready = sem("const_ready")
    band_ready = sem("band_ready")
    staged = sem("staged")
    xt_mm = sem("xt_mm")
    xt_out = sem("xt_out")
    hid_mm = sem("hid_mm")
    hid_out = sem("hid_out")
    ks_mm = sem("ks_mm")
    small = sem("small")
    scl_spread = sem("scl_spread")
    logit = sem("logit")
    weight = sem("weight")
    blurred = sem("blurred")
    num_out = sem("num_out")
    num_turned = sem("num_turned")
    rz_ready = sem("rz_ready")
    mixed = sem("mixed")
    low_mm = sem("low_mm")
    enhanced = sem("enhanced")
    stat = sem("stat")
    tail = sem("tail")
    rooted = sem("rooted")
    finished = sem("finished")
    stored = sem("stored")

    O_BANK, NT_BANK, XT_BANK, MLP_BANK = 4, 5, 6, 7

    def is0(r):
        return isinstance(r, int) and r == 0

    def pe_hidden(pe, r, i):
        if i == 0:
            if not is0(r):
                pe.wait_ge(small, 4 * (r - 1) + 1)
        else:
            pe.wait_ge(hid_out, 2 * r + 1)
        rows = bass.ds(BLK * r + R, BLK)
        pe.matmul(ps[:, MLP_BANK, :], w1[:, i, :], pad[:, rows, R:R + W],
                  start=True, stop=True).then_inc(hid_mm, 1)

    def pe_ks(pe, r):
        pe.wait_ge(hid_out, 2 * r + 2)
        for k in range(4):
            for i in range(2):
                px = hid[i][:, 2 * k:2 * k + 2].rearrange("p t r c -> p (t r c)")
                mm = pe.matmul(ps[:, MLP_BANK, B * k + HALF * i:B * k + HALF * i + HALF], px, w2[:],
                               start=True, stop=True)
        mm.then_inc(ks_mm, 1)

    def pe_xt(pe, g, s, k):
        if k == 0:
            pe.wait_ge(staged, g + 1)
        if not (is0(g) and k == 0):
            pe.wait_ge(xt_out, 2 * g + k)
        for j in range(4):
            cb = 4 * k + j
            tr = pe.transpose(ps[:, XT_BANK, P * j:P * j + P],
                              tile[s][:, cb].rearrange("p r c -> p (r c)"), perm[:])
        tr.then_inc(xt_mm, 1)

    def pe_spread(pe, r, s, u):
        if u == 0:
            pe.wait_ge(small, 4 * r + 4)
        if not (is0(r) and u < 4):
            pe.wait_ge(logit, 8 * r + u - 3)
        for k in range(4):
            tr = pe.transpose(ps[:, u % 4, P * k:P * k + P], spread(scl[s][:, k, u:u + 1], [P, P]),
                              ident[:])
        tr.then_inc(scl_spread, 1)

    def pe_blur(pe, r, s, i, part):
        if part == 0:
            pe.wait_ge(weight, 8 * r + 4 * i + 4)
            pe.wait_ge(xt_out, 2 * r + 4)
            if not (is0(r) and i == 0):
                pe.wait_ge(num_out, 2 * r + i)
        for cb in range(4 * part, 4 * part + 4):
            for t in range(2):
                for j in range(HALF):
                    b = HALF * i + j
                    mm = pe.matmul(ps[32 * j:32 * j + 32, O_BANK, 64 * cb:64 * cb + 64],
                                   xt[(s + t) % 2][:, cb, b, :], wgt[b][:, t, cb, :],
                                   start=(t == 0), stop=(t == 1))
        if part == 1:
            mm.then_inc(blurred, 1)

    def pe_turn(pe, r, i):
        pe.wait_ge(num_out, 2 * r + i + 1)
        if i == 1:
            pe.wait_ge(mixed, 2 * r + 1)
        elif not is0(r):
            pe.wait_ge(enhanced, r)
        for k in range(4):
            tr = pe.transpose(ps[:, NT_BANK, P * k:P * k + P], num[i][:, P * k:P * k + P], ident[:])
        tr.then_inc(num_turned, 1)

    def pe_low(pe, r):
        pe.wait_ge(mixed, 2 * r + 2)
        for k in range(4):
            px = mix[:, k].rearrange("p c b n -> p (c b n)")
            tr = pe.transpose(ps[:, NT_BANK, P * k:P * k + P], px, ident[:])
        tr.then_inc(low_mm, 1)

    def pe_row(pe, r, s, main, lag, prep):
        for u in range(B):
            if main:
                pe_spread(pe, r, s, u)
            if u == 0 and prep:
                pe_hidden(pe, r + 1, 0)
            if u == 1 and lag:
                pe_blur(pe, r - 1, 1 - s, 1, 0)
            if u == 2:
                if lag:
                    pe_blur(pe, r - 1, 1 - s, 1, 1)
                if main:
                    pe_xt(pe, r + 1, 1 - s, 0)
            if u == 3:
                if lag:
                    pe_turn(pe, r - 1, 1)
                if prep:
                    pe_hidden(pe, r + 1, 1)
            if u == 4:
                if main:
                    pe_xt(pe, r + 1, 1 - s, 1)
                if prep:
                    pe_ks(pe, r + 1)
            if u == 5:
                if lag:
                    pe_low(pe, r - 1)
                if main:
                    pe_blur(pe, r, s, 0, 0)
            if u == 6 and main:
                pe_blur(pe, r, s, 0, 1)
            if u == 7 and main:
                pe_turn(pe, r, 0)

    def act_hidden(act, r, i):
        act.wait_ge(hid_mm, 2 * r + i + 1)
        if not is0(r):
            act.wait_ge(ks_mm, r)
        act.activation(hid[i][:].rearrange("p k r c -> p r k c"),
                       ps[:, MLP_BANK, :].rearrange("p (r k c) -> p r k c", r=BLK, k=CB), ACT.Relu,
                       bias=vec[:, VEC[tag + "_b1"]:VEC[tag + "_b1"] + 1], scale=1.0).then_inc(hid_out, 1)

    def act_xt(act, g, s, k):
        act.wait_ge(xt_mm, 2 * g + k + 1)
        if not (isinstance(g, int) and g < 2):
            act.wait_ge(blurred, 2 * (g - 1))
        act.copy(xt[s][:, 4 * k:4 * k + 4, :, 0:C],
                 ps[:, XT_BANK, :].rearrange("p (k b m) -> p k b m", k=4, b=B)).then_inc(xt_out, 1)

    def act_weight(act, r, u):
        act.wait_ge(logit, 8 * r + u + 1)
        w = wgt[u][:].rearrange("p t k m -> p (t k m)")
        act.activation(w, w, ACT.Exp).then_inc(weight, 1)

    def act_num(act, r, i):
        act.wait_ge(blurred, 2 * r + i + 1)
        if not is0(r):
            act.wait_ge(num_turned, 2 * r + i - 1)
        act.copy(num[i][:], ps[:, O_BANK, :]).then_inc(num_out, 1)

    def act_row(act, r, s, main, lag, prep):
        for u in range(B):
            if main:
                act_weight(act, r, u)
            if u == 0 and prep:
                act_hidden(act, r + 1, 0)
            if u == 2 and lag:
                act_num(act, r - 1, 1)
            if u == 3:
                if main:
                    act_xt(act, r + 1, 1 - s, 0)
                if prep:
                    act_hidden(act, r + 1, 1)
            if u == 4 and main:
                act_xt(act, r + 1, 1 - s, 1)
            if u == 6 and main:
                act_num(act, r, 0)

    def dve_small(dve, r, s, k):
        flat = scl[s][:].rearrange("p k b -> p (k b)")
        if k == 0:
            dve.wait_ge(ks_mm, r + 1)
            dve.tensor_scalar(sm[0][:], ps[:, MLP_BANK, 0:4 * B], vec[:, VEC[tag + "_b2"]:VEC[tag + "_b2"] + 1],
                              0.0, ALU.add, ALU.max).then_inc(small, 1)
            return
        dve.wait_ge(small, 4 * r + k)
        if k == 1:
            dve.tensor_scalar(sm[1][:], sm[0][:], 20.0, 1.0, ALU.mult, ALU.add).then_inc(small, 1)
        if k == 2:
            dve.tensor_tensor(sm[2][:], sm[1][:], sm[1][:], ALU.mult).then_inc(small, 1)
        if k == 3:
            dve.reciprocal(flat, sm[2][:]).then_inc(small, 1)

    def dve_logit(dve, r, u):
        dve.wait_ge(scl_spread, 8 * r + u + 1)
        if not is0(r):
            dve.wait_ge(blurred, 2 * r + u // 4 - 1)
        shape = [P, 2, CB, BLK * BLK]
        s_in = ps[:, u % 4, :].rearrange("p (k m) -> p k m", k=CB).unsqueeze(1)
        dve.tensor_tensor(wgt[u][:], spread(gband[:].unsqueeze(2), shape), spread(s_in, shape),
                          ALU.mult).then_inc(logit, 1)

    def dve_mix(dve, r, i):
        nt = ps[:, NT_BANK, :].rearrange("p (k b m) -> p k b m", k=4, b=HALF)
        dve.wait_ge(num_turned, 2 * r + i + 1)
        dve.reciprocal(rz[:], nt[:, :, :, C]).then_inc(rz_ready, 1)
        dve.wait_ge(rz_ready, 2 * r + i + 1)
        if i == 0 and not is0(r):
            dve.wait_ge(low_mm, r)
        for cp in range(CP):
            ins = dve.tensor_tensor(mix[:, :, cp, HALF * i:HALF * i + HALF, :],
                                    nt[:, :, :, HEADS * cp:HEADS * cp + HEADS],
                                    spread(rz[:].unsqueeze(3), [P, 4, HALF, HEADS]), ALU.mult)
        ins.then_inc(mixed, 1)

    def dve_enhance(dve, r):
        dve.wait_ge(low_mm, r + 1)
        rows = pad[:, bass.ds(BLK * r + R, BLK), R:R + W].rearrange("p r (k c) -> p r k c", c=BLK)
        low = ps[:, NT_BANK, :].rearrange("p (k r c) -> p r k c", k=CB, r=BLK)
        dve.tensor_tensor(rows, rows, low, ALU.add).then_inc(enhanced, 1)

    def dve_stats(dve, r):
        dve.wait_ge(enhanced, r + 1)
        dve.bn_stats(stats[:, bass.ds(r, 1), :].rearrange("p o s -> p (o s)"),
                     pad[:, bass.ds(BLK * r + R, BLK), R:R + W]).then_inc(stat, 1)

    def dve_row(dve, r, s, main, lag, prep):
        for u in range(B):
            if main:
                dve_logit(dve, r, u)
            if u == 0 and lag:
                dve_mix(dve, r - 1, 0)
            if u == 4 and lag:
                dve_mix(dve, r - 1, 1)
            if u == 5 and prep:
                dve_small(dve, r + 1, 1 - s, 0)
            if u == 6:
                if prep:
                    dve_small(dve, r + 1, 1 - s, 1)
                if lag:
                    dve_enhance(dve, r - 1)
                if prep:
                    dve_small(dve, r + 1, 1 - s, 2)
            if u == 7:
                if lag:
                    dve_stats(dve, r - 1)
                if prep:
                    dve_small(dve, r + 1, 1 - s, 3)

    def rows_of(eng, row):
        row(eng, 0, 0, True, False, True)
        with eng.Fori(0, (RB - 2) // 2) as i:
            for p in range(2):
                row(eng, 2 * i + 1 + p, 1 - p, True, True, True)
        row(eng, RB - 1, 1, True, True, False)
        row(eng, RB, 0, False, True, False)

    with nc.Block() as block:
        @block.sync
        def _(sp):
            for t, name in ((w1, "w1"), (w2, "w2"), (gband, "gband")):
                sp.dma_start(t[:], d[f"{tag}_{name}"]).then_inc(loaded, 16)
            sp.dma_start(gmask[:], d["gmask"]).then_inc(loaded, 16)
            sp.dma_start(perm[:], d["perm"]).then_inc(loaded, 16)
            if out is not None:
                for j in range(4):
                    sp.wait_ge(finished, j + 1)
                    cols = slice(j * PIX // 4, (j + 1) * PIX // 4)
                    for cp in range(CP):
                        sp.dma_start(out[cp][:, cols], result[64 * cp:64 * cp + 64, cols]).then_inc(stored, 16)
                sp.wait_ge(stored, 16 * 4 * CP)

        @block.gpsimd
        def _(pool):
            def stage(g, s):
                if not (isinstance(g, int) and g < 2):
                    pool.wait_ge(xt_mm, 2 * (g - 1))
                for cb in range(CB):
                    ins = pool.tensor_copy(tile[s][:, cb], pad[:, bass.ds(BLK * g, BLK), BLK * cb:BLK * cb + QC])
                ins.then_inc(staged, 1)
            stage(0, 0)
            for s in range(2):
                pool.memset(xt[s][:, :, :, C:2 * C], 0.0).then_inc(const_ready, 1)
            pool.wait_ge(const_ready, 2)
            for s in range(2):
                pool.memset(xt[s][:, :, :, C:C + 1], 1.0).then_inc(const_ready, 1)
            stage(1, 1)
            with pool.Fori(0, 3) as i:
                for p in range(2):
                    stage(2 * i + 2 + p, p)
            stage(RB, 0)

        @block.tensor
        def _(pe):
            pe.wait_ge(loaded, 80)
            pe_hidden(pe, 0, 0)
            pe_xt(pe, 0, 0, 0)
            pe_hidden(pe, 0, 1)
            pe_xt(pe, 0, 0, 1)
            pe_ks(pe, 0)
            pe.wait_ge(const_ready, 4)
            rows_of(pe, pe_row)

        @block.scalar
        def _(act):
            act_hidden(act, 0, 0)
            act_xt(act, 0, 0, 0)
            act_hidden(act, 0, 1)
            act_xt(act, 0, 0, 1)
            rows_of(act, act_row)
            act.wait_ge(tail, 2)
            act.activation(std[:, 1:2], std[:, 0:1], ACT.Sqrt).then_inc(rooted, 1)

        @block.vector
        def _(dve):
            dve.wait_ge(loaded, 80)
            dve.scalar_tensor_tensor(out=gband[:].rearrange("p t m -> p (t m)"),
                                     in0=gband[:].rearrange("p t m -> p (t m)"), scalar=-4.5,
                                     in1=gmask[:].rearrange("p t m -> p (t m)"),
                                     op0=ALU.mult, op1=ALU.add).then_inc(band_ready, 1)
            for k in range(4):
                dve_small(dve, 0, 0, k)
            dve.wait_ge(band_ready, 1)
            rows_of(dve, dve_row)
            dve.wait_ge(stat, RB)
            dve.bn_aggr(mv[:], stats[:].rearrange("p r s -> p (r s)")).then_inc(tail, 1)
            dve.wait_ge(tail, 1)
            dve.tensor_scalar(std[:, 0:1], mv[:, 1:2], NORM_EPS, None, ALU.add).then_inc(tail, 1)
            dve.wait_ge(rooted, 1)
            dve.reciprocal(rstd[:], std[:, 1:2]).then_inc(tail, 1)
            dve.wait_ge(tail, 3)
            for j in range(4):
                rows = pad[:, R + 16 * j:R + 16 * j + 16, R:R + W]
                dst = rows if out is None else result[:, j * PIX // 4:(j + 1) * PIX // 4]\
                    .rearrange("p (h w) -> p h w", w=W)
                dve.tensor_scalar(dst, rows, mv[:, 0:1], rstd[:, 0:1], ALU.subtract, ALU.mult)\
                    .then_inc(finished, 1)


def binconv(nc, sem_, sb, d, vec, ps, pad, pad_to):
    def sem(name):
        return sem_("c_" + name)

    T = 9
    raw = sb("raw", [P, T * P])
    pos = sb("pos", [P, T * P])
    wb = sb("wb", [P, T, P])
    w1row = sb("w1row", [P, P])
    wb1 = sb("wb1", [P, T, P])
    wsum = sb("wsum", [P, T, P])
    onehot = sb("onehot", [P, T, T])
    sh = sb("sh", [P, 2, T, T])
    valid = sb("valid", [T, PIX])
    const = sb("const", [T, P])
    bn = sb("bn", [P, 4])
    lin = [sb(f"lin{s}", [P, BLK, W]) for s in range(2)]

    loaded = sem("loaded")
    prep = sem("prep")
    rooted = sem("rooted")
    const_mm = sem("const_mm")
    const_out = sem("const_out")
    conv_mm = sem("conv_mm")
    affine = sem("affine")
    resid = sem("resid")
    clipped = sem("clipped")
    col = lambda name: vec[:, VEC[name]:VEC[name] + 1]

    def scale_rows(dve, dst, k):
        dve.wait_ge(prep, k)
        return dve.tensor_tensor(dst[:], wb[:], spread(w1row[:].unsqueeze(1), [P, T, P]), ALU.mult)

    with nc.Block() as block:
        @block.sync
        def _(sp):
            for t, name in ((raw, "c_weight"), (w1row, "c_w1row"), (onehot, "onehot"), (valid, "valid")):
                sp.dma_start(t[:], d[name]).then_inc(loaded, 16)

        @block.tensor
        def _(pe):
            pe.wait_ge(prep, 6)
            k = 0
            for i, w in enumerate((wb, wb1)):
                for t in range(T):
                    mm = pe.matmul(ps[0:T, 7, 0:P], sh[:, i, t, :], w[:, t, :],
                                   start=(k == 0), stop=(k == 2 * T - 1))
                    k += 1
            mm.then_inc(const_mm, 1)
            pe.wait_ge(const_out, 1)
            pe.wait_ge(prep, 8)
            for g in range(CHUNKS):
                bank = g % 4
                if g >= 4:
                    pe.wait_ge(affine, g - 3)
                for t in range(T):
                    dh, dw = t // 3 - 1, t % 3 - 1
                    rows = pad[:, R + ROWS * g + dh:R + ROWS * g + dh + ROWS, R + dw:R + dw + W]
                    pe.matmul(ps[:, bank, :], wsum[:, t, :], rows, start=(t == 0), stop=False)
                pe.matmul(ps[:, bank, :], const[:], valid[:, BANK * g:BANK * g + BANK],
                          start=False, stop=True).then_inc(conv_mm, 1)

        @block.scalar
        def _(act):
            act.wait_ge(prep, 5)
            act.activation(bn[:, 1:2], bn[:, 0:1], ACT.Sqrt).then_inc(rooted, 1)
            act.wait_ge(prep, 12)
            for g in range(CHUNKS):
                act.wait_ge(conv_mm, g + 1)
                if g >= 2:
                    act.wait_ge(clipped, g - 1)
                act.activation(lin[g % 2][:].rearrange("p r w -> p (r w)"), ps[:, g % 4, :], ACT.Identity,
                               bias=bn[:, 3:4], scale=bn[:, 2:3]).then_inc(affine, 1)

        @block.vector
        def _(dve):
            wf = wb[:].rearrange("p t m -> p (t m)")
            dve.wait_ge(loaded, 64)
            dve.tensor_scalar(pos[:], raw[:], 0.0, None, ALU.is_gt).then_inc(prep, 1)
            dve.wait_ge(prep, 1)
            dve.scalar_tensor_tensor(out=wf, in0=raw[:], scalar=0.0, in1=pos[:], op0=ALU.is_lt,
                                     op1=ALU.subtract).then_inc(prep, 1)
            dve.tensor_scalar(sh[:, 0], onehot[:], col("shift1"), -1.0, ALU.mult, ALU.mult).then_inc(prep, 1)
            dve.tensor_scalar(sh[:, 1], onehot[:], col("shift2"), -1.0, ALU.mult, ALU.mult).then_inc(prep, 1)
            dve.tensor_scalar(bn[:, 0:1], col("var"), NORM_EPS, None, ALU.add).then_inc(prep, 1)
            scale_rows(dve, wb1, 2).then_inc(prep, 1)
            dve.wait_ge(prep, 6)
            dve.tensor_tensor(wsum[:], wb[:], wb1[:], ALU.add).then_inc(prep, 1)
            dve.wait_ge(prep, 7)
            dve.tensor_scalar(wsum[:].rearrange("p t m -> p (t m)"), wsum[:].rearrange("p t m -> p (t m)"),
                              -1.0, None, ALU.mult).then_inc(prep, 1)
            dve.wait_ge(const_mm, 1)
            dve.tensor_copy(const[:], ps[0:T, 7, 0:P]).then_inc(const_out, 1)
            dve.wait_ge(rooted, 1)
            dve.reciprocal(bn[:, 0:1], bn[:, 1:2]).then_inc(prep, 1)
            dve.wait_ge(prep, 9)
            dve.tensor_tensor(bn[:, 2:3], bn[:, 0:1], col("gamma"), ALU.mult).then_inc(prep, 1)
            dve.wait_ge(prep, 10)
            dve.tensor_tensor(bn[:, 3:4], bn[:, 2:3], col("mean"), ALU.mult).then_inc(prep, 1)
            dve.wait_ge(prep, 11)
            dve.tensor_tensor(bn[:, 3:4], col("beta"), bn[:, 3:4], ALU.subtract).then_inc(prep, 1)
            for g in range(CHUNKS):
                dve.wait_ge(affine, g + 1)
                rows = lambda t: t[:, R + ROWS * g:R + ROWS * g + ROWS, R:R + W]
                dve.tensor_tensor(lin[g % 2][:], lin[g % 2][:], rows(pad), ALU.add).then_inc(resid, 1)
                dve.wait_ge(resid, g + 1)
                dve.tensor_scalar(rows(pad_to), lin[g % 2][:], 1.0, -1.0, ALU.min, ALU.max).then_inc(clipped, 1)



def shape_constants():
    ident = np.eye(P, dtype=np.float32)
    plane_b = (np.arange(P) // HEADS) % B
    same = plane_b[:, None] == plane_b[None, :]
    centre = (ident - same / C).astype(np.float32)
    meansel = ((plane_b[:, None] == np.arange(B)) / C).astype(np.float32)
    shift_eye = np.zeros((TAPS, BAND), np.float32)
    row = 0
    for width in KW:
        for k in range(width):
            shift_eye[row, k + (KW[0] - width) // 2 + (W - 1) - CENTRE] = 1.0
            row += 1
    qi, qj = np.divmod(np.arange(P), QC)
    pr, pc = np.divmod(np.arange(BLK * BLK), BLK)
    u = qi[:, None, None] + BLK * np.arange(2)[None, :, None] - pr[None, None, :]
    v = (qj[:, None, None] - pc[None, None, :]) + 0 * u
    inside = (u >= 0) & (u < KG) & (v >= 0) & (v < KG)
    gmask = np.where(inside, 0.0, OFF_BAND).astype(np.float32)
    perm = np.eye(P, dtype=np.float32).reshape(P, CP, B, HEADS).transpose(0, 2, 1, 3).reshape(P, P)
    onehot = np.broadcast_to(np.eye(9, dtype=np.float32), (P, 9, 9)).copy()
    valid = np.zeros((9, H, W), np.float32)
    for t in range(9):
        dh, dw = t // 3 - 1, t % 3 - 1
        valid[t, max(0, -dh):H - max(0, dh), max(0, -dw):W - max(0, dw)] = 1.0
    return {"ident": ident, "centre": centre, "meansel": meansel, "shift_eye": shift_eye,
            "perm": perm, "gmask": gmask, "onehot": onehot, "valid": valid.reshape(9, PIX)}, (u, v, inside)


def lay_out(i):
    a, (u, v, inside) = shape_constants()
    part = np.arange(P)
    plane_cp, plane_b, plane_n = part // 64, (part // HEADS) % B, part % HEADS
    chan = CP * plane_n + plane_cp
    f = {k: np.asarray(x) for k, x in i.items()}
    a["x"] = f["x"]

    vec = np.zeros((P, len(VECS)), np.float32)
    for name, src in (("ln_w", "L0_conv_ln_w"), ("ln_b", "L0_conv_ln_b"), ("proj_b", "L0_conv_proj_b"),
                      ("shift1", "L2_conv_shift1"), ("shift2", "L2_conv_shift2"),
                      ("gamma", "L2_conv_gamma"), ("beta", "L2_conv_beta"),
                      ("mean", "L2_conv_running_mean"), ("var", "L2_conv_running_var"),
                      ("w1", "L2_conv_w1")):
        vec[:, VEC[name]] = f[src].reshape(C)[chan]
    for tag, lay in (("g1", "L1_conv_"), ("g3", "L3_conv_")):
        vec[:, VEC[tag + "_b1"]] = f[lay + "b1"][part % HIDDEN]
        vec[:, VEC[tag + "_b2"]] = f[lay + "b2"][0]
        w1 = np.zeros((P, 2, HALF, HIDDEN), np.float32)
        w1[part, plane_b // HALF, plane_b % HALF] = f[lay + "w1"][chan]
        a[tag + "_w1"] = w1.reshape(P, 2, P)
        w2 = np.zeros((P, HALF), np.float32)
        w2[part, part // HIDDEN] = f[lay + "w2"][part % HIDDEN, 0]
        a[tag + "_w2"] = w2
        g = np.zeros((P, 2, BLK * BLK), np.float32)
        g[inside] = f[lay + "gauss_kernel"][u[inside], v[inside]]
        a[tag + "_gband"] = g
    a["vec"] = vec

    taps = [np.concatenate([f["L0_conv_w" + k + str(t)].reshape(C, -1).T for k in "210"]) for t in (1, 2)]
    a["taps"] = np.stack(taps, 1).reshape(TAPS, 2, HEADS, CP).transpose(0, 1, 3, 2)
    one = np.ones(1, np.float32)
    a["bias_lhs"] = np.stack([np.concatenate([f["L0_conv_b" + k + str(t)] for k in "210"] + [one])
                              for t in (1, 2)], 1)
    pw = f["L0_conv_proj_w"]
    a["bias_rhs"] = np.concatenate([pw.T] * 3 + [f["L0_conv_proj_b"][None]])
    ptab = pw.reshape(HEADS, CP, HEADS, CP).transpose(3, 2, 0, 1)
    a["ptab"] = np.repeat(ptab, 64, axis=0)
    same = plane_b[:, None] == plane_b[None, :]
    ii, oo = np.nonzero(same)
    blk = np.zeros((P, P), np.float32)
    blk[ii, oo] = pw[chan[oo], chan[ii]]
    a["projblk"] = blk
    wt = f["L2_conv_weight"].reshape(C, C, 9)
    cw = np.zeros((P, 9, P), np.float32)
    cw[ii, :, oo] = wt[chan[oo], chan[ii]]
    a["c_weight"] = cw.reshape(P, 9 * P)
    a["c_w1row"] = np.repeat(f["L2_conv_w1"].reshape(1, C)[:, chan], P, axis=0)
    return {k: np.ascontiguousarray(x) for k, x in a.items()}


def kernel(**inputs):
    import concourse.bacc as bacc
    from concourse.bass_utils import run_bass_kernel_spmd

    arrays = lay_out(inputs)
    nc = bacc.Bacc("TRN2", target_bir_lowering=False, num_devices=1)
    d = {k: nc.dram_tensor(f"in_{k}", x.shape, F32, kind="ExternalInput").ap() for k, x in arrays.items()}
    out = nc.dram_tensor("out", (B, C, H, W), F32, kind="ExternalOutput").ap()
    planes = out.rearrange("b (n cp) h w -> cp b n (h w)", cp=CP)
    build(nc, d, [planes[cp].rearrange("b n f -> (b n) f") for cp in range(CP)])
    r = run_bass_kernel_spmd(nc, [{f"in_{k}": x for k, x in arrays.items()}], core_ids=[0])
    return r.results[0]["out"]
```

```python
from contextlib import ExitStack

import numpy as np

import concourse.bass as bass
from concourse import mybir

F32 = mybir.dt.float32
ALU = mybir.AluOpType
ACT = mybir.ActivationFunctionType

P = 128
B, C, H, W = 8, 16, 64, 64
HEADS = 8
CP = C // HEADS
PIX = H * W
BANK = 512
ROWS = BANK // W
CHUNKS = PIX // BANK
PXT = PIX // P

KW = (21, 11, 7)
CENTRE = KW[0] // 2
BAND = H + W - 1

KG = 9
R = KG // 2
BLK = 8
PADDED = H + 2 * R
CB = W // BLK
RB = H // BLK
QC = 2 * BLK
HIDDEN = 32
HALF = B // 2
OFF_BAND = -1e34

LN_EPS = 1e-5
L2_EPS_SQ = 1e-24
NORM_EPS = 1e-5

VECS = ["ln_w", "ln_b", "proj_b", "shift1", "shift2", "gamma", "beta", "mean", "var", "w1",
        "g1_b1", "g1_b2", "g3_b1", "g3_b2"]
VEC = {name: i for i, name in enumerate(VECS)}


def spread(ap, shape):
    return ap.broadcast_to(list(shape))


def build(nc, d, out):
    keep = ExitStack()
    with keep:
        def sb(stack, name, shape):
            return stack.enter_context(nc.sbuf_tensor(name, shape, F32))

        def sem(name):
            return keep.enter_context(nc.semaphore(name))

        ident = sb(keep, "ident", [P, P])
        vec = sb(keep, "vec", [P, len(VECS)])
        ones = sb(keep, "ones", [P, 1])
        pad_a = sb(keep, "pad_a", [P, PADDED, PADDED])
        pad_b = sb(keep, "pad_b", [P, PADDED, PADDED])
        ps = keep.enter_context(nc.psum_tensor("ps", [P, 8, BANK], F32))

        zeroed = sem("zeroed")
        with ExitStack() as l0:
            x0 = sb(l0, "x0", [P, PIX])
            xrow = sb(l0, "xrow", [P, HEADS, B, H])
            xcol = sb(l0, "xcol", [P, HEADS, B, W])
            toep = sb(l0, "toep", [P, 2, HEADS, P])
            projnb = sb(l0, "projnb", [P, P])
            pair = sb(l0, "pair", [P, P])
            rn = sb(l0, "rn", [P, HEADS * 16])
            beta = sb(l0, "beta_o", [P, 2, HEADS])
            projblk = sb(l0, "projblk", [P, P])
            const_in = sem("const_in")
            with ExitStack() as ln:
                l0_norm(nc, sem, lambda n, s: sb(ln, n, s), d, ident, vec, ones, pad_a, pad_b, ps, x0,
                        xrow, xcol, toep, projnb, pair, beta, projblk, const_in, zeroed)
            o1c = sb(l0, "o1c", [P, HEADS, B, W])
            o2r = sb(l0, "o2r", [P, HEADS, B, H])
            with ExitStack() as cv:
                l0_conv(nc, sem, lambda n, s: sb(cv, n, s), ident, pair, ps, xrow, xcol, toep, projnb,
                        beta, o1c, o2r, rn)
            attn = sb(l0, "attn", [P, B, HEADS, H])
            with ExitStack() as hd:
                l0_attention(nc, sem, lambda n, s: sb(hd, n, s), ident, ones, ps,
                             xrow, o1c, xcol, o2r, rn, attn)
            with ExitStack() as fin:
                l0_out(nc, sem, lambda n, s: sb(fin, n, s), ident, vec, ps, x0, attn, projblk, pad_a)
        with ExitStack() as g:
            blur(nc, sem, lambda n, s: sb(g, "g1_" + n, s), "g1", d, ident, vec, ps, pad_a, pad_a, None)
        with ExitStack() as c:
            binconv(nc, sem, lambda n, s: sb(c, n, s), d, vec, ps, pad_a, pad_b)
        with ExitStack() as g:
            blur(nc, sem, lambda n, s: sb(g, "g3_" + n, s), "g3", d, ident, vec, ps, pad_b, None, out)


def l0_norm(nc, sem, sb, d, ident, vec, ones, pad_a, pad_b, ps, x0, xrow, xcol, toep, projnb, pair, beta,
            projblk, const_in, zeroed):
    centre = sb("centre", [P, P])
    meansel = sb("meansel", [P, B])
    tpart = sb("tpart", [P, len(KW), 2, HEADS, W])
    nb = len(KW) * C + 1
    bias_lhs = sb("bias_lhs", [nb, 2])
    bias_rhs = sb("bias_rhs", [nb, C])
    xc = sb("xc", [P, PIX])
    sq = sb("sq", [P, PIX])
    var = sb("var", [P, PXT * B])
    std = sb("std", [P, PXT * B])
    rstd = sb("rstd", [P, PXT, B])
    wide = sb("wide", [P, PXT, CP, B, HEADS])

    x_in = [sem(f"x_in{j}") for j in range(4)]
    centre_in = sem("centre_in")
    centred = sem("centred")
    xc_copied = sem("xc_copied")
    squared = sem("squared")
    bias_mm = sem("bias_mm")
    bias_read = sem("bias_read")
    toep_in = sem("toep_in")
    toep_sum = sem("toep_sum")
    var_mm = sem("var_mm")
    eps_added = sem("eps_added")
    rooted = sem("rooted")
    rstd_ready = sem("rstd_ready")
    rstd_wide = [sem(f"rstd_wide{cp}") for cp in range(CP)]
    rstd_spread = sem("rstd_spread")
    scaled = sem("scaled")
    normed = sem("normed")
    turned = sem("turned")
    evac_v = sem("evac_v")
    evac_s = sem("evac_s")
    CONSTS = 8

    with nc.Block() as block:
        @block.sync
        def _(sp):
            xv = d["x"].rearrange("b (n cp) h w -> cp b n (h w)", cp=CP)
            sp.dma_start(centre[:], d["centre"]).then_inc(centre_in, 16)
            for j in range(4):
                cols = slice(j * PIX // 4, (j + 1) * PIX // 4)
                for cp in range(CP):
                    sp.dma_start(x0[64 * cp:64 * cp + 64, cols],
                                 xv[cp].rearrange("b n f -> (b n) f")[:, cols]).then_inc(x_in[j], 16)
            for t in range(2):
                for k in range(len(KW)):
                    for cp in range(CP):
                        start = ((t * len(KW) + k) * C + cp) * BAND
                        windows = bass.AP(tensor=d["taps"].tensor, offset=start,
                                          ap=[[1, W], [CP * BAND, HEADS], [1, W]])
                        sp.dma_start(tpart[64 * cp:64 * cp + 64, k, t], windows).then_inc(toep_in, 16)

        @block.gpsimd
        def _(pool):
            pool.memset(ones[:], 1.0).then_inc(zeroed, 1)
            pool.memset(pad_a[:], 0.0).then_inc(zeroed, 1)
            pool.memset(pad_b[:], 0.0).then_inc(zeroed, 1)
            flat = lambda k: tpart[:, k].rearrange("p t n w -> p (t n w)")
            pool.memset(toep[:], 0.0).then_inc(zeroed, 1)
            pool.wait_ge(toep_in, 16 * 2 * len(KW) * CP)
            pool.tensor_tensor(flat(0), flat(0), flat(1), ALU.add).then_inc(toep_sum, 1)
            pool.wait_ge(toep_sum, 1)
            pool.wait_ge(zeroed, 4)
            for cp in range(CP):
                part = slice(64 * cp, 64 * cp + 64)
                rows = lambda k: tpart[part, k].rearrange("p t n w -> p (t n) w")
                pool.tensor_tensor(toep[part, :, :, part].rearrange("p t n w -> p (t n) w")[:, :, ::-1],
                                   rows(0), rows(2), ALU.add).then_inc(toep_sum, 1)

        @block.tensor
        def _(pe):
            pe.wait_ge(centre_in, 16)
            for j in range(CHUNKS):
                if j % 2 == 0:
                    pe.wait_ge(x_in[j // 2], 32)
                pe.matmul(ps[:, j, :], centre[:], x0[:, j * BANK:(j + 1) * BANK],
                          start=True, stop=True).then_inc(centred, 1)
            pe.wait_ge(const_in, 16 * CONSTS)
            pe.wait_ge(xc_copied, 5)
            for t in range(2):
                mm = pe.matmul(ps[:, 4, C * t:C * t + C], spread(bias_lhs[:, t:t + 1], [nb, P]),
                               bias_rhs[:], start=True, stop=True)
            mm.then_inc(bias_mm, 1)
            pe.wait_ge(squared, CHUNKS)
            pe.wait_ge(xc_copied, CHUNKS)
            for t in range(PXT):
                mm = pe.matmul(ps[:, 7, B * t:B * t + B], sq[:, P * t:P * t + P], meansel[:],
                               start=True, stop=True)
            mm.then_inc(var_mm, 1)
            pe.wait_ge(bias_read, 4)
            for t in range(PXT):
                if t % 4 == 0:
                    for cp in range(CP):
                        pe.wait_ge(rstd_wide[cp], t // 4 + 1)
                tr = pe.transpose(ps[:, t // 4, P * (t % 4):P * (t % 4) + P],
                                  wide[:, t].rearrange("p c b n -> p (c b n)"), ident[:])
                if t % 4 == 3:
                    tr.then_inc(rstd_spread, 1)
            for g in range(CHUNKS):
                pe.wait_ge(normed, g + 1)
                for hh in range(ROWS):
                    h = ROWS * g + hh
                    for cp in range(CP):
                        mm = pe.matmul(ps[64 * cp:64 * cp + 64, g, 64 * hh:64 * hh + 64],
                                       sq[:, W * h:W * h + W], ident[:, 64 * cp:64 * cp + 64],
                                       start=True, stop=True)
                mm.then_inc(turned, 1)
            cols = sq[:].rearrange("p (h w) -> p w h", w=W)
            for g in range(CHUNKS):
                if g % 2 == 0:
                    pe.wait_ge(evac_v, g // 2 + 1)
                else:
                    pe.wait_ge(evac_s, g // 2 + 1)
                for ww in range(ROWS):
                    w = ROWS * g + ww
                    for cp in range(CP):
                        mm = pe.matmul(ps[64 * cp:64 * cp + 64, g, 64 * ww:64 * ww + 64],
                                       cols[:, w, :], ident[:, 64 * cp:64 * cp + 64],
                                       start=True, stop=True)
                mm.then_inc(turned, 1)

        def turned_out(lay, g):
            return lay[:].rearrange("p n b h -> p h b n")[:, ROWS * g:ROWS * g + ROWS]

        def turned_in(g):
            return ps[:, g, :].rearrange("p (h b n) -> p h b n", h=ROWS, b=B)

        def widen(copy, j, cp):
            tiles = slice(4 * j, 4 * j + 4)
            copy(wide[:, tiles, cp], spread(rstd[:, tiles, :].unsqueeze(3), [P, 4, B, HEADS]))\
                .then_inc(rstd_wide[cp], 1)

        @block.scalar
        def _(act):
            for t, name in ((meansel, "meansel"), (ident, "ident"), (vec, "vec"), (bias_lhs, "bias_lhs"),
                            (bias_rhs, "bias_rhs"), (projnb, "projnb"), (pair, "pair"), (projblk, "projblk")):
                act.dma_start(t[:], d[name]).then_inc(const_in, 16)
            act.wait_ge(const_in, 16 * CONSTS)
            for j in range(CHUNKS):
                act.wait_ge(xc_copied, j + 1)
                act.activation(sq[:, j * BANK:(j + 1) * BANK], xc[:, j * BANK:(j + 1) * BANK], ACT.Square).then_inc(squared, 1)
            act.wait_ge(eps_added, 1)
            act.activation(std[:], var[:], ACT.Sqrt).then_inc(rooted, 1)
            act.wait_ge(rstd_ready, 1)
            for j in range(CHUNKS):
                widen(act.copy, j, 1)
            for j in range(CHUNKS):
                act.wait_ge(scaled, j + 1)
                act.activation(sq[:, j * BANK:(j + 1) * BANK], xc[:, j * BANK:(j + 1) * BANK],
                               ACT.Identity, bias=vec[:, VEC["ln_b"]:VEC["ln_b"] + 1],
                               scale=vec[:, VEC["ln_w"]:VEC["ln_w"] + 1]).then_inc(normed, 1)
            for lay, base in ((xrow, 0), (xcol, CHUNKS)):
                for g in range(1, CHUNKS, 2):
                    act.wait_ge(turned, base + g + 1)
                    act.copy(turned_out(lay, g), turned_in(g)).then_inc(evac_s, 1)

        @block.vector
        def _(dve):
            for j in range(CHUNKS):
                dve.wait_ge(centred, j + 1)
                dve.tensor_copy(xc[:, j * BANK:(j + 1) * BANK], ps[:, j, :]).then_inc(xc_copied, 1)
            dve.wait_ge(bias_mm, 1)
            for t in range(2):
                for cp in range(CP):
                    src = ps[64 * cp:64 * cp + 64, 4, C * t:C * t + C].rearrange("p (n c) -> p c n", c=CP)
                    dve.tensor_copy(beta[64 * cp:64 * cp + 64, t, :], src[:, cp, :]).then_inc(bias_read, 1)
            dve.wait_ge(var_mm, 1)
            dve.tensor_scalar(var[:], ps[:, 7, 0:PXT * B], LN_EPS, None, ALU.add).then_inc(eps_added, 1)
            dve.wait_ge(rooted, 1)
            dve.reciprocal(rstd[:].rearrange("p t b -> p (t b)"), std[:]).then_inc(rstd_ready, 1)
            dve.wait_ge(rstd_ready, 1)
            for j in range(CHUNKS):
                widen(dve.tensor_copy, j, 0)
            for j in range(CHUNKS):
                dve.wait_ge(rstd_spread, j + 1)
                dve.tensor_tensor(xc[:, j * BANK:(j + 1) * BANK], xc[:, j * BANK:(j + 1) * BANK],
                                  ps[:, j, :], ALU.mult).then_inc(scaled, 1)
            for lay, base in ((xrow, 0), (xcol, CHUNKS)):
                for g in range(0, CHUNKS, 2):
                    dve.wait_ge(turned, base + g + 1)
                    dve.tensor_copy(turned_out(lay, g), turned_in(g)).then_inc(evac_v, 1)


def l0_conv(nc, sem, sb, ident, pair, ps, xrow, xcol, toep, projnb, beta, o1c, o2r, rn):
    img = [sb(f"conv_img{t}", [P, H, W]) for t in range(2)]
    sqs = sb("sqs", [P, 4, BANK])
    ssum = sb("ssum", [P, 4, HEADS, B])
    nsq = sb("nsq", [P, HEADS, 4, HALF])
    root = sb("root", [P, HEADS * 16])
    lay = (xrow, xcol)

    conv_mm = sem("conv_mm")
    conv_v = sem("conv_v")
    conv_s = sem("conv_s")
    turn_mm = sem("turn_mm")
    turn_v = sem("turn_v")
    turn_s = sem("turn_s")
    proj_mm = sem("proj_mm")
    proj_out = sem("proj_out")
    squared = sem("q_squared")
    summed = sem("summed")
    nsq_mm = sem("nsq_mm")
    nsq_ready = sem("nsq_ready")
    norm_ready = sem("norm_ready")
    rn_ready = sem("rn_ready")

    JOBS = 2 * CHUNKS
    TENSORS = ((xrow, 2, 0, 0), (o1c, 1, 0, 1), (xcol, 0, 1, 0), (o2r, 3, 1, 1))
    NORM_BANK = 7

    def wait_evacuated(eng, j, on_v, on_s):
        eng.wait_ge(on_v, j // 2 + 1)
        if j > 0:
            eng.wait_ge(on_s, (j + 1) // 2)

    with nc.Block() as block:
        @block.tensor
        def _(pe):
            for j in range(JOBS):
                t, n = divmod(j, HEADS)
                if j >= 4:
                    wait_evacuated(pe, j - 4, conv_v, conv_s)
                pe.matmul(ps[:, j % 4, :], toep[:, t, n, :], lay[t][:, n].rearrange("p b h -> p (b h)"),
                          start=True, stop=True).then_inc(conv_mm, 1)
            for j in range(JOBS):
                t, g = divmod(j, CHUNKS)
                if g == 0:
                    wait_evacuated(pe, (t + 1) * HEADS - 1, conv_v, conv_s)
                if j < 4:
                    wait_evacuated(pe, JOBS - 4 + j, conv_v, conv_s)
                else:
                    wait_evacuated(pe, j - 4, turn_v, turn_s)
                planes = lay[t][:].rearrange("p n b h -> p h (n b)")
                for hh in range(ROWS):
                    for cp in range(CP):
                        half = slice(64 * cp, 64 * cp + 64)
                        mm = pe.matmul(ps[half, j % 4, 64 * hh:64 * hh + 64], planes[:, ROWS * g + hh],
                                       ident[:, half], start=True, stop=True)
                mm.then_inc(turn_mm, 1)
            for i, (_, _, t, inner) in enumerate(TENSORS):
                planes = img[t][:] if inner == 0 else img[t][:].rearrange("p h w -> p w h")
                for g in range(CHUNKS):
                    j = CHUNKS * i + g
                    if j < 4:
                        wait_evacuated(pe, JOBS - 4 + j, turn_v, turn_s)
                    else:
                        pe.wait_ge(proj_out, j - 3)
                    if i == 0 and g == 4:
                        wait_evacuated(pe, JOBS - 1, turn_v, turn_s)
                    for hh in range(ROWS):
                        for cp in range(CP):
                            mm = pe.matmul(ps[64 * cp:64 * cp + 64, j % 4, 64 * hh:64 * hh + 64],
                                           planes[:, ROWS * g + hh], projnb[:, 64 * cp:64 * cp + 64],
                                           start=True, stop=True)
                    mm.then_inc(proj_mm, 1)
            pe.wait_ge(summed, 4 * HEADS)
            pe.matmul(ps[:, NORM_BANK, 0:4 * HEADS * B], pair[:], ssum[:].rearrange("p t m b -> p (t m b)"),
                      start=True, stop=True).then_inc(nsq_mm, 1)

        def evacuate(eng, copy, odd, on_conv, on_turn):
            for j in range(odd, JOBS, 2):
                t, n = divmod(j, HEADS)
                eng.wait_ge(conv_mm, j + 1)
                copy(lay[t][:, n].rearrange("p b h -> p (b h)"), ps[:, j % 4, :]).then_inc(on_conv, 1)
            for j in range(odd, JOBS, 2):
                t, g = divmod(j, CHUNKS)
                eng.wait_ge(turn_mm, j + 1)
                copy(img[t][:, ROWS * g:ROWS * g + ROWS, :].rearrange("p r c -> p (r c)"),
                     ps[:, j % 4, :]).then_inc(on_turn, 1)

        @block.scalar
        def _(act):
            evacuate(act, act.copy, 1, conv_s, turn_s)
            for i in range(len(TENSORS)):
                act.wait_ge(proj_out, CHUNKS * (i + 1))
                for m in range(HEADS):
                    if HEADS * i + m >= 4:
                        act.wait_ge(summed, HEADS * i + m - 3)
                    act.activation(sqs[:, m % 4, :], TENSORS[i][0][:, m].rearrange("p b h -> p (b h)"),
                                   ACT.Square).then_inc(squared, 1)
            act.wait_ge(nsq_ready, CP)
            act.activation(root[:], nsq[:].rearrange("p m t k -> p (m t k)"), ACT.Sqrt).then_inc(norm_ready, 1)

        @block.vector
        def _(dve):
            evacuate(dve, dve.tensor_copy, 0, conv_v, turn_v)
            def row_sums(i, m):
                dve.wait_ge(squared, HEADS * i + m + 1)
                dve.tensor_reduce(ssum[:, TENSORS[i][1], m, :], sqs[:, m % 4, :].rearrange("p (b h) -> p b h", b=B),
                                  mybir.AxisListType.X, ALU.add).then_inc(summed, 1)

            for i, (dst, _, t, _) in enumerate(TENSORS):
                for g in range(CHUNKS):
                    dve.wait_ge(proj_mm, CHUNKS * i + g + 1)
                    dve.tensor_tensor(dst[:, :, :, ROWS * g:ROWS * g + ROWS].rearrange("p m b h -> p h m b"),
                                      ps[:, g % 4, :].rearrange("p (h m b) -> p h m b", h=ROWS, m=HEADS),
                                      spread(beta[:, t, :].unsqueeze(1).unsqueeze(3), [P, ROWS, HEADS, B]),
                                      ALU.add).then_inc(proj_out, 1)
                    if i > 0:
                        row_sums(i - 1, g)
            for m in range(HEADS):
                row_sums(3, m)
            dve.wait_ge(nsq_mm, 1)
            for odd in range(2):
                part = slice(64 * odd, 64 * odd + 64)
                sums = ps[part, NORM_BANK, 0:4 * HEADS * B].rearrange("p (t m k o) -> p o m t k", t=4, m=HEADS, o=2)
                dve.tensor_scalar(nsq[part], sums[:, odd], L2_EPS_SQ, None, ALU.max).then_inc(nsq_ready, 1)
            dve.wait_ge(norm_ready, 1)
            dve.reciprocal(rn[:], root[:]).then_inc(rn_ready, 1)


def l0_attention(nc, sem, sb, ident, ones, ps, o1r, o1c, o2c, o2r, rn, attn):
    q1 = [sb(f"q1{s}", [P, B, H]) for s in range(2)]
    q2 = [sb(f"q2{s}", [P, B, W]) for s in range(2)]
    k1 = sb("k1", [P, B, H])
    k2 = sb("k2", [P, B, W])
    e = [[sb(f"e{s}{t}", [P, B, H]) for t in range(2)] for s in range(2)]
    rz = sb("rz", [P, 8])
    v1 = [sb(f"v1{s}", [P, B, W]) for s in range(2)]
    v2 = [sb(f"v2{s}", [P, B, H]) for s in range(2)]
    rnh = [sb(f"rnh{s}", [P, 16]) for s in range(2)]

    rn_spread = sem("rn_spread")
    unit = sem("unit")
    score_mm = sem("score_mm")
    exped = sem("exped")
    z_mm = sem("z_mm")
    rz_ready = sem("rz_ready")
    rz_spread = sem("rz_spread")
    prob = sem("prob")
    av_mm = sem("av_mm")
    attn_out = sem("attn_out")
    rn_head = sem("rn_head")
    v_head = sem("v_head")

    QUAD = [(64 * cp, 64 * cp + 64) for cp in range(CP)]
    SCORE = (4, 5)
    OUT = (7, 6)

    def wait_apart(eng, semaphore, value):
        eng.wait_ge(semaphore, value)
        eng.nop(nofuse=True)

    def is0(m):
        return isinstance(m, int) and m == 0

    def head(lay, m):
        return lay[:, bass.ds(m, 1)].rearrange("p o b h -> p (o b h)")

    def spread_norms(pe, m, s):
        pe.wait_ge(rn_head, m + 1)
        for t in range(4):
            if not is0(m):
                pe.wait_ge(unit, 4 * (m - 1) + t + 1)
            for k in range(4):
                tr = pe.transpose(ps[:, t, P * k:P * k + P],
                                  spread(rnh[s][:, 4 * t + k:4 * t + k + 1], [P, P]), ident[:])
            tr.then_inc(rn_spread, 1)

    def scores(pe, m, s):
        for t, (q, k) in enumerate(((q1[s], k1), (q2[s], k2))):
            pe.wait_ge(unit, 4 * m + 2 * t + 2)
            if not is0(m):
                pe.wait_ge(prob, 2 * (m - 1) + t + 1)
            for b in range(B):
                for lo, hi in QUAD:
                    mm = pe.matmul(ps[lo:hi, SCORE[t], 64 * b:64 * b + 64], k[:, b, :], q[:, b, :],
                                   start=True, stop=True)
            mm.then_inc(score_mm, 1)

    def z_sums(pe, m, s):
        pe.wait_ge(exped, 2 * m + 2)
        for t in range(2):
            for k in range(4):
                mm = pe.matmul(ps[:, SCORE[0], 4 * t + k:4 * t + k + 1],
                               e[s][t][0:64, 2 * k:2 * k + 2, :].rearrange("p b i -> p (b i)"),
                               ones[0:64, :], start=True, stop=True)
        mm.then_inc(z_mm, 1)

    def spread_z(pe, m):
        pe.wait_ge(rz_ready, m + 1)
        for t in range(2):
            for k in range(4):
                tr = pe.transpose(ps[:, SCORE[t], P * k:P * k + P],
                                  spread(rz[:, 4 * t + k:4 * t + k + 1], [P, P]), ident[:])
            tr.then_inc(rz_spread, 1)

    def outputs(pe, m, s):
        wait_apart(pe, v_head, 2 * m + 2)
        wait_apart(pe, prob, 2 * m + 2)
        if not is0(m):
            wait_apart(pe, attn_out, m)
        for first in range(2):
            for b0 in range(B // 2):
                steps = []
                for i, (b, bank) in enumerate(((b0, OUT[0]), (b0 + 4, OUT[1]))):
                    lo, hi = QUAD[first ^ i]
                    o = ps[lo:hi, bank, 64 * b0:64 * b0 + 64]
                    steps.append([(o, v1[s][lo:hi, b, :], e[s][0][lo:hi, b, :]),
                                  (o, e[s][1][lo:hi, b, :], v2[s][lo:hi, b, :]),
                                  (o, q2[s][lo:hi, b, :], ident[lo:hi, lo:hi])])
                for k in range(3):
                    for st in steps:
                        mm = pe.matmul(*st[k], start=(k == 0), stop=(k == 2))
        mm.then_inc(av_mm, 1)

    def pe_head(pe, m, s, do):
        if do.main:
            scores(pe, m, s)
        if do.lag:
            outputs(pe, m - 1, 1 - s)
        if do.main:
            z_sums(pe, m, s)
        if do.next:
            spread_norms(pe, m + 1, 1 - s)
        if do.main:
            spread_z(pe, m)

    def act_head(act, m, s, do):
        if not do.main:
            return
        for t in range(2):
            act.wait_ge(score_mm, 2 * m + t + 1)
            if t == 0 and not (isinstance(m, int) and m < 2):
                act.wait_ge(av_mm, m - 1)
            act.activation(e[s][t][:].rearrange("p b h -> p (b h)"), ps[:, SCORE[t], :], ACT.Exp)                .then_inc(exped, 1)

    def normalise(dve, m, s):
        for t, (dst, src) in enumerate(((q1[s], o2r), (k1, o1r), (q2[s], o1c), (k2, o2c))):
            dve.wait_ge(rn_spread, 4 * m + t + 1)
            if t == 0 and not (isinstance(m, int) and m < 2):
                dve.wait_ge(attn_out, m - 1)
            dve.tensor_tensor(dst[:].rearrange("p b h -> p (b h)"), head(src, m), ps[:, t, :],
                              ALU.mult).then_inc(unit, 1)

    def add_q1(dve, m, s):
        dve.wait_ge(av_mm, m + 1)
        for i, bank in enumerate(OUT):
            ins = dve.tensor_tensor(attn[:, 4 * i:4 * i + 4, bass.ds(m, 1), :].rearrange("p b o h -> p b (o h)"),
                                    ps[:, bank, 0:256].rearrange("p (b h) -> p b h", b=4),
                                    q1[s][:, 4 * i:4 * i + 4, :], ALU.add)
        ins.then_inc(attn_out, 1)

    def dve_head(dve, m, s, do):
        if do.lag:
            add_q1(dve, m - 1, 1 - s)
        if do.main:
            dve.wait_ge(z_mm, m + 1)
            dve.reciprocal(rz[:], ps[:, SCORE[0], 0:8]).then_inc(rz_ready, 1)
        if do.next:
            normalise(dve, m + 1, 1 - s)
        if do.main:
            for t in range(2):
                dve.wait_ge(rz_spread, 2 * m + t + 1)
                ev = e[s][t][:].rearrange("p b h -> p (b h)")
                dve.tensor_tensor(ev, ev, ps[:, SCORE[t], :], ALU.mult).then_inc(prob, 1)

    def pool_norms(pool, m, s):
        if not (isinstance(m, int) and m < 2):
            pool.wait_ge(rn_spread, 4 * (m - 1))
        pool.tensor_copy(rnh[s][:], rn[:, bass.ds(16 * m, 16)]).then_inc(rn_head, 1)

    def pool_values(pool, m, s):
        if not (isinstance(m, int) and m < 2):
            pool.wait_ge(av_mm, m - 1)
        for dst, src in ((v1[s], o1c), (v2[s], o2r)):
            pool.tensor_copy(dst[:].rearrange("p b h -> p (b h)"), head(src, m)).then_inc(v_head, 1)

    def pool_head(pool, m, s, do):
        if do.next:
            pool_norms(pool, m + 1, 1 - s)
        if do.main:
            pool_values(pool, m, s)

    class Head:

        def __init__(self, m):
            self.main, self.lag, self.next = m < HEADS, m > 0, m + 1 < HEADS

    def heads_of(eng, head_steps):
        for m in range(2):
            head_steps(eng, m, m, Head(m))
        with eng.Fori(0, 2) as i:
            for p in range(2):
                head_steps(eng, 2 * i + 2 + p, p, Head(2))
        for m in range(HEADS - 2, HEADS + 1):
            head_steps(eng, m, m % 2, Head(m))

    with nc.Block() as block:
        @block.tensor
        def _(pe):
            spread_norms(pe, 0, 0)
            heads_of(pe, pe_head)

        @block.scalar
        def _(act):
            heads_of(act, act_head)

        @block.vector
        def _(dve):
            normalise(dve, 0, 0)
            heads_of(dve, dve_head)

        @block.gpsimd
        def _(pool):
            pool_norms(pool, 0, 0)
            heads_of(pool, pool_head)


def l0_out(nc, sem, sb, ident, vec, ps, x0, attn, projblk, pad):
    img = sb("img", [P, PIX])
    bias2 = sb("bias2", [P, 1])
    turned = sem("o_turned")
    copied_v = sem("o_copied_v")
    copied_s = sem("o_copied_s")
    projected = sem("o_projected")
    added = sem("o_added")
    bias2_ready = sem("o_bias2")
    planes = attn[:].rearrange("p b n h -> p h (b n)")

    def copied(eng, g):
        eng.wait_ge(copied_v if g % 2 == 0 else copied_s, g // 2 + 1)

    with nc.Block() as block:
        @block.tensor
        def _(pe):
            def project(g):
                copied(pe, g)
                pe.matmul(ps[:, g, :], projblk[:], img[:, BANK * g:BANK * g + BANK],
                          start=True, stop=True).then_inc(projected, 1)
            for g in range(CHUNKS):
                for hh in range(ROWS):
                    for cp in range(CP):
                        mm = pe.matmul(ps[64 * cp:64 * cp + 64, g, W * hh:W * hh + W],
                                       planes[:, ROWS * g + hh], ident[:, 64 * cp:64 * cp + 64],
                                       start=True, stop=True)
                mm.then_inc(turned, 1)
                if g > 0:
                    project(g - 1)
            project(CHUNKS - 1)

        @block.scalar
        def _(act):
            for g in range(1, CHUNKS, 2):
                act.wait_ge(turned, g + 1)
                act.copy(img[:, BANK * g:BANK * g + BANK], ps[:, g, :]).then_inc(copied_s, 1)

        @block.vector
        def _(dve):
            pb = vec[:, VEC["proj_b"]:VEC["proj_b"] + 1]
            dve.tensor_tensor(bias2[:], pb, pb, ALU.add).then_inc(bias2_ready, 1)
            dve.wait_ge(bias2_ready, 1)

            def add(g):
                dve.wait_ge(projected, g + 1)
                dve.scalar_tensor_tensor(
                    out=pad[:, R + ROWS * g:R + ROWS * g + ROWS, R:R + W],
                    in0=ps[:, g, :].rearrange("p (h w) -> p h w", w=W), scalar=bias2[:, 0:1],
                    in1=x0[:, BANK * g:BANK * g + BANK].rearrange("p (h w) -> p h w", w=W),
                    op0=ALU.add, op1=ALU.add).then_inc(added, 1)
            for g in range(0, CHUNKS, 2):
                dve.wait_ge(turned, g + 1)
                dve.tensor_copy(img[:, BANK * g:BANK * g + BANK], ps[:, g, :]).then_inc(copied_v, 1)
                if g > 0:
                    add(g - 2)
                    add(g - 1)
            add(CHUNKS - 2)
            add(CHUNKS - 1)


def blur(nc, sem_, sb, tag, d, ident, vec, ps, pad, normed_to, out):
    def sem(name):
        return sem_(f"{tag}_{name}")

    gband = sb("gband", [P, 2, BLK * BLK])
    gmask = sb("gmask", [P, 2, BLK * BLK])
    w1 = sb("w1", [P, 2, P])
    w2 = sb("w2", [P, HALF])
    perm = sb("perm", [P, P])
    tile = [sb(f"tile{s}", [P, CB, BLK, QC]) for s in range(2)]
    xt = [sb(f"xt{s}", [P, CB, B, 2 * C]) for s in range(2)]
    hid = [sb(f"hid{i}", [P, CB, BLK, BLK]) for i in range(2)]
    sm = [sb(f"sm{i}", [P, 4 * B]) for i in range(3)]
    scl = [sb(f"scl{s}", [P, 4, B]) for s in range(2)]
    wgt = [sb(f"wgt{u}", [P, 2, CB, BLK * BLK]) for u in range(B)]
    num = [sb(f"num{s}", [P, BANK]) for s in range(2)]
    rz = sb("rzb", [P, 4, HALF])
    mix = sb("mix", [P, 4, CP, B, HEADS])
    stats = sb("stats", [P, RB, 6])
    mv = sb("mv", [P, 2])
    std = sb("stdb", [P, 2])
    rstd = sb("rstdb", [P, 1])
    result = sb("result", [P, PIX]) if out is not None else None

    loaded = sem("loaded")
    const_ready = sem("const_ready")
    band_ready = sem("band_ready")
    staged = sem("staged")
    xt_mm = sem("xt_mm")
    xt_out = sem("xt_out")
    hid_mm = sem("hid_mm")
    hid_out = sem("hid_out")
    ks_mm = sem("ks_mm")
    small = sem("small")
    scl_spread = sem("scl_spread")
    logit = sem("logit")
    weight = sem("weight")
    blurred = sem("blurred")
    num_out = sem("num_out")
    num_turned = sem("num_turned")
    rz_ready = sem("rz_ready")
    mixed = sem("mixed")
    low_mm = sem("low_mm")
    enhanced = sem("enhanced")
    stat = sem("stat")
    tail = sem("tail")
    rooted = sem("rooted")
    finished = sem("finished")
    stored = sem("stored")

    O_BANK, NT_BANK, XT_BANK, MLP_BANK = 4, 5, 6, 7

    def is0(r):
        return isinstance(r, int) and r == 0

    def pe_hidden(pe, r, i):
        if i == 0:
            if not is0(r):
                pe.wait_ge(small, 4 * (r - 1) + 1)
            if not is0(r):
                pe.wait_ge(xt_out, 2 * r)
        else:
            pe.wait_ge(hid_out, 2 * r + 1)
        rows = bass.ds(BLK * r + R, BLK)
        pe.matmul(ps[:, MLP_BANK, :], w1[:, i, :], pad[:, rows, R:R + W],
                  start=True, stop=True).then_inc(hid_mm, 1)

    def pe_ks(pe, r):
        pe.wait_ge(hid_out, 2 * r + 2)
        for k in range(4):
            for i in range(2):
                px = hid[i][:, 2 * k:2 * k + 2].rearrange("p t r c -> p (t r c)")
                mm = pe.matmul(ps[:, MLP_BANK, B * k + HALF * i:B * k + HALF * i + HALF], px, w2[:],
                               start=True, stop=True)
        mm.then_inc(ks_mm, 1)

    def pe_xt(pe, g, s, k):
        bank = (XT_BANK, MLP_BANK)[k]
        if k == 0:
            pe.wait_ge(staged, g + 1)
            if not is0(g):
                pe.wait_ge(xt_out, 2 * g - 1)
        else:
            pe.wait_ge(small, 4 * (RB - 1) + 1 if isinstance(g, int) and g == RB else 4 * g + 1)
        for j in range(4):
            cb = 4 * k + j
            tr = pe.transpose(ps[:, bank, P * j:P * j + P],
                              tile[s][:, cb].rearrange("p r c -> p (r c)"), perm[:])
        tr.then_inc(xt_mm, 1)

    def pe_spread(pe, r, s, u):
        if u == 0:
            pe.wait_ge(small, 4 * r + 4)
        if not (is0(r) and u < 4):
            pe.wait_ge(logit, 8 * r + u - 3)
        for k in range(4):
            tr = pe.transpose(ps[:, u % 4, P * k:P * k + P], spread(scl[s][:, k, u:u + 1], [P, P]),
                              ident[:])
        tr.then_inc(scl_spread, 1)

    def pe_blur(pe, r, s, i, part):
        if part == 0:
            pe.wait_ge(weight, 8 * r + 4 * i + 4)
            pe.wait_ge(xt_out, 2 * r + 4)
            if not (is0(r) and i == 0):
                pe.wait_ge(num_out, 2 * r + i)
        for cb in range(4 * part, 4 * part + 4):
            for t in range(2):
                for j in range(HALF):
                    b = HALF * i + j
                    mm = pe.matmul(ps[32 * j:32 * j + 32, O_BANK, 64 * cb:64 * cb + 64],
                                   xt[(s + t) % 2][:, cb, b, :], wgt[b][:, t, cb, :],
                                   start=(t == 0), stop=(t == 1))
        if part == 1:
            mm.then_inc(blurred, 1)

    def pe_turn(pe, r, i):
        pe.wait_ge(num_out, 2 * r + i + 1)
        if i == 1:
            pe.wait_ge(mixed, 2 * r + 1)
        elif not is0(r):
            pe.wait_ge(enhanced, r)
        for k in range(4):
            tr = pe.transpose(ps[:, NT_BANK, P * k:P * k + P], num[i][:, P * k:P * k + P], ident[:])
        tr.then_inc(num_turned, 1)

    def pe_low(pe, r):
        pe.wait_ge(mixed, 2 * r + 2)
        for k in range(4):
            px = mix[:, k].rearrange("p c b n -> p (c b n)")
            tr = pe.transpose(ps[:, NT_BANK, P * k:P * k + P], px, ident[:])
        tr.then_inc(low_mm, 1)

    def pe_row(pe, r, s, do):
        for u in range(B):
            if u + 2 < B:
                if do.main:
                    pe_spread(pe, r, s, u + 2)
            elif do.next:
                pe_spread(pe, r + 1, 1 - s, u + 2 - B)
            if u == 0 and do.main:
                pe_xt(pe, r + 1, 1 - s, 0)
            if u == 1 and do.next:
                pe_ks(pe, r + 1)
            if u == 2 and do.lag:
                pe_turn(pe, r - 1, 0)
                pe_blur(pe, r - 1, 1 - s, 1, 0)
            if u == 3 and do.lag:
                pe_blur(pe, r - 1, 1 - s, 1, 1)
            if u == 3 and do.main:
                pe_xt(pe, r + 1, 1 - s, 1)
            if u == 5:
                if do.lag:
                    pe_turn(pe, r - 1, 1)
                if do.after_next:
                    pe_hidden(pe, r + 2, 0)
            if u == 6 and do.main:
                pe_blur(pe, r, s, 0, 0)
            if u == 7:
                if do.lag:
                    pe_low(pe, r - 1)
                if do.main:
                    pe_blur(pe, r, s, 0, 1)
                if do.after_next:
                    pe_hidden(pe, r + 2, 1)

    def act_hidden(act, r, i):
        act.wait_ge(hid_mm, 2 * r + i + 1)
        if not is0(r):
            act.wait_ge(ks_mm, r)
        act.activation(hid[i][:].rearrange("p k r c -> p r k c"),
                       ps[:, MLP_BANK, :].rearrange("p (r k c) -> p r k c", r=BLK, k=CB), ACT.Relu,
                       bias=vec[:, VEC[tag + "_b1"]:VEC[tag + "_b1"] + 1], scale=1.0).then_inc(hid_out, 1)

    def act_xt(act, g, s, k):
        act.wait_ge(xt_mm, 2 * g + k + 1)
        if not (isinstance(g, int) and g < 2):
            act.wait_ge(blurred, 2 * (g - 1))
        act.copy(xt[s][:, 4 * k:4 * k + 4, :, 0:C],
                 ps[:, (XT_BANK, MLP_BANK)[k], :].rearrange("p (k b m) -> p k b m", k=4, b=B)).then_inc(xt_out, 1)

    def act_weight(act, r, u):
        act.wait_ge(logit, 8 * r + u + 1)
        w = wgt[u][:].rearrange("p t k m -> p (t k m)")
        act.activation(w, w, ACT.Exp).then_inc(weight, 1)

    def act_num(act, r, i):
        act.wait_ge(blurred, 2 * r + i + 1)
        if not is0(r):
            act.wait_ge(num_turned, 2 * r + i - 1)
        act.copy(num[i][:], ps[:, O_BANK, :]).then_inc(num_out, 1)

    def act_row(act, r, s, do):
        for u in range(B):
            if do.main:
                act_weight(act, r, u)
            if u == 3:
                if do.lag:
                    act_num(act, r - 1, 1)
                if do.main:
                    act_xt(act, r + 1, 1 - s, 0)
            if u == 4 and do.main:
                act_xt(act, r + 1, 1 - s, 1)
            if u == 5 and do.after_next:
                act_hidden(act, r + 2, 0)
            if u == 7:
                if do.main:
                    act_num(act, r, 0)
                if do.after_next:
                    act_hidden(act, r + 2, 1)

    def dve_small(dve, r, s, k):
        flat = scl[s][:].rearrange("p k b -> p (k b)")
        if k == 0:
            dve.wait_ge(ks_mm, r + 1)
            dve.tensor_scalar(sm[0][:], ps[:, MLP_BANK, 0:4 * B], vec[:, VEC[tag + "_b2"]:VEC[tag + "_b2"] + 1],
                              0.0, ALU.add, ALU.max).then_inc(small, 1)
            return
        dve.wait_ge(small, 4 * r + k)
        if k == 1:
            dve.tensor_scalar(sm[1][:], sm[0][:], 20.0, 1.0, ALU.mult, ALU.add).then_inc(small, 1)
        if k == 2:
            dve.tensor_tensor(sm[2][:], sm[1][:], sm[1][:], ALU.mult).then_inc(small, 1)
        if k == 3:
            dve.reciprocal(flat, sm[2][:]).then_inc(small, 1)

    def dve_logit(dve, r, u):
        dve.wait_ge(scl_spread, 8 * r + u + 1)
        if not is0(r):
            dve.wait_ge(blurred, 2 * r + u // 4 - 1)
        shape = [P, 2, CB, BLK * BLK]
        s_in = ps[:, u % 4, :].rearrange("p (k m) -> p k m", k=CB).unsqueeze(1)
        dve.tensor_tensor(wgt[u][:], spread(gband[:].unsqueeze(2), shape), spread(s_in, shape),
                          ALU.mult).then_inc(logit, 1)

    def dve_mix(dve, r, i):
        nt = ps[:, NT_BANK, :].rearrange("p (k b m) -> p k b m", k=4, b=HALF)
        dve.wait_ge(num_turned, 2 * r + i + 1)
        dve.reciprocal(rz[:], nt[:, :, :, C]).then_inc(rz_ready, 1)
        dve.wait_ge(rz_ready, 2 * r + i + 1)
        if i == 0 and not is0(r):
            dve.wait_ge(low_mm, r)
        for cp in range(CP):
            ins = dve.tensor_tensor(mix[:, :, cp, HALF * i:HALF * i + HALF, :],
                                    nt[:, :, :, HEADS * cp:HEADS * cp + HEADS],
                                    spread(rz[:].unsqueeze(3), [P, 4, HALF, HEADS]), ALU.mult)
        ins.then_inc(mixed, 1)

    def dve_enhance(dve, r):
        dve.wait_ge(low_mm, r + 1)
        rows = pad[:, bass.ds(BLK * r + R, BLK), R:R + W].rearrange("p r (k c) -> p r k c", c=BLK)
        low = ps[:, NT_BANK, :].rearrange("p (k r c) -> p r k c", k=CB, r=BLK)
        dve.tensor_tensor(rows, rows, low, ALU.add).then_inc(enhanced, 1)

    def dve_stats(dve, r):
        dve.wait_ge(enhanced, r + 1)
        dve.bn_stats(stats[:, bass.ds(r, 1), :].rearrange("p o s -> p (o s)"),
                     pad[:, bass.ds(BLK * r + R, BLK), R:R + W]).then_inc(stat, 1)

    def dve_row(dve, r, s, do):
        for u in range(B):
            if do.main:
                dve_logit(dve, r, u)
            if u == 0 and do.lag2:
                dve_enhance(dve, r - 2)
            if u == 1 and do.lag2:
                dve_stats(dve, r - 2)
            if 1 < u < 5 and do.next:
                dve_small(dve, r + 1, 1 - s, u - 2)
                if u == 4:
                    dve_small(dve, r + 1, 1 - s, 3)
            if u == 3 and do.lag:
                dve_mix(dve, r - 1, 0)
            if u == 5 and do.lag:
                dve_mix(dve, r - 1, 1)

    class Row:

        def __init__(self, r):
            self.main, self.lag, self.lag2 = r < RB, 0 < r <= RB, r > 1
            self.next, self.after_next = r + 1 < RB, r + 2 < RB

    def rows_of(eng, row):
        for r in range(2):
            row(eng, r, r, Row(r))
        with eng.Fori(0, 2) as i:
            for p in range(2):
                row(eng, 2 * i + 2 + p, p, Row(2))
        for r in range(RB - 2, RB + 2):
            row(eng, r, r % 2, Row(r))

    with nc.Block() as block:
        @block.sync
        def _(sp):
            for t, name in ((w1, "w1"), (w2, "w2"), (gband, "gband")):
                sp.dma_start(t[:], d[f"{tag}_{name}"]).then_inc(loaded, 16)
            sp.dma_start(gmask[:], d["gmask"]).then_inc(loaded, 16)
            sp.dma_start(perm[:], d["perm"]).then_inc(loaded, 16)
            if out is not None:
                for j in range(4):
                    sp.wait_ge(finished, j + 1)
                    cols = slice(j * PIX // 4, (j + 1) * PIX // 4)
                    for cp in range(CP):
                        sp.dma_start(out[cp][:, cols], result[64 * cp:64 * cp + 64, cols]).then_inc(stored, 16)
                sp.wait_ge(stored, 16 * 4 * CP)

        @block.gpsimd
        def _(pool):
            def stage(g, s):
                if not (isinstance(g, int) and g < 2):
                    pool.wait_ge(xt_mm, 2 * (g - 1))
                for odd in range(2):
                    cols = pad[:, bass.ds(BLK * g, BLK), BLK * odd:BLK * odd + W]
                    ins = pool.tensor_copy(tile[s][:].rearrange("p (k o) r c -> p o k r c", o=2)[:, odd],
                                           cols.rearrange("p r (k c) -> p k r c", c=QC))
                ins.then_inc(staged, 1)
            stage(0, 0)
            for s in range(2):
                pool.memset(xt[s][:, :, :, C:2 * C], 0.0).then_inc(const_ready, 1)
            pool.wait_ge(const_ready, 2)
            for s in range(2):
                pool.memset(xt[s][:, :, :, C:C + 1], 1.0).then_inc(const_ready, 1)
            stage(1, 1)
            with pool.Fori(0, 3) as i:
                for p in range(2):
                    stage(2 * i + 2 + p, p)
            stage(RB, 0)

        @block.tensor
        def _(pe):
            pe.wait_ge(loaded, 80)
            pe_hidden(pe, 0, 0)
            pe_xt(pe, 0, 0, 0)
            pe_hidden(pe, 0, 1)
            pe_ks(pe, 0)
            pe_xt(pe, 0, 0, 1)
            pe_hidden(pe, 1, 0)
            pe_hidden(pe, 1, 1)
            pe.wait_ge(const_ready, 4)
            pe_spread(pe, 0, 0, 0)
            pe_spread(pe, 0, 0, 1)
            rows_of(pe, pe_row)

        @block.scalar
        def _(act):
            act_hidden(act, 0, 0)
            act_xt(act, 0, 0, 0)
            act_hidden(act, 0, 1)
            act_xt(act, 0, 0, 1)
            act_hidden(act, 1, 0)
            act_hidden(act, 1, 1)
            rows_of(act, act_row)
            act.wait_ge(tail, 2)
            act.activation(std[:, 1:2], std[:, 0:1], ACT.Sqrt).then_inc(rooted, 1)

        @block.vector
        def _(dve):
            dve.wait_ge(loaded, 80)
            dve.scalar_tensor_tensor(out=gband[:].rearrange("p t m -> p (t m)"),
                                     in0=gband[:].rearrange("p t m -> p (t m)"), scalar=-4.5,
                                     in1=gmask[:].rearrange("p t m -> p (t m)"),
                                     op0=ALU.mult, op1=ALU.add).then_inc(band_ready, 1)
            for k in range(4):
                dve_small(dve, 0, 0, k)
            dve.wait_ge(band_ready, 1)
            rows_of(dve, dve_row)
            dve.wait_ge(stat, RB)
            dve.bn_aggr(mv[:], stats[:].rearrange("p r s -> p (r s)")).then_inc(tail, 1)
            dve.wait_ge(tail, 1)
            dve.tensor_scalar(std[:, 0:1], mv[:, 1:2], NORM_EPS, None, ALU.add).then_inc(tail, 1)
            dve.wait_ge(rooted, 1)
            dve.reciprocal(rstd[:], std[:, 1:2]).then_inc(tail, 1)
            dve.wait_ge(tail, 3)
            for j in range(4):
                rows = pad[:, R + 16 * j:R + 16 * j + 16, R:R + W]
                dst = rows if out is None else result[:, j * PIX // 4:(j + 1) * PIX // 4]\
                    .rearrange("p (h w) -> p h w", w=W)
                dve.tensor_scalar(dst, rows, mv[:, 0:1], rstd[:, 0:1], ALU.subtract, ALU.mult)\
                    .then_inc(finished, 1)


def binconv(nc, sem_, sb, d, vec, ps, pad, pad_to):
    def sem(name):
        return sem_("c_" + name)

    T = 9
    raw = sb("raw", [P, T * P])
    pos = sb("pos", [P, T * P])
    wb = sb("wb", [P, T, P])
    w1row = sb("w1row", [P, P])
    wb1 = sb("wb1", [P, T, P])
    wsum = sb("wsum", [P, T, P])
    onehot = sb("onehot", [P, T, T])
    sh = sb("sh", [P, 2, T, T])
    valid = sb("valid", [T, PIX])
    const = sb("const", [T, P])
    bn = sb("bn", [P, 4])
    lin = [sb(f"lin{s}", [P, BLK, W]) for s in range(2)]

    loaded = sem("loaded")
    prep = sem("prep")
    rooted = sem("rooted")
    const_mm = sem("const_mm")
    const_out = sem("const_out")
    conv_mm = sem("conv_mm")
    affine = sem("affine")
    resid = sem("resid")
    clipped = sem("clipped")
    col = lambda name: vec[:, VEC[name]:VEC[name] + 1]

    def scale_rows(dve, dst, k):
        dve.wait_ge(prep, k)
        return dve.tensor_tensor(dst[:], wb[:], spread(w1row[:].unsqueeze(1), [P, T, P]), ALU.mult)

    with nc.Block() as block:
        @block.sync
        def _(sp):
            for t, name in ((raw, "c_weight"), (w1row, "c_w1row"), (onehot, "onehot"), (valid, "valid")):
                sp.dma_start(t[:], d[name]).then_inc(loaded, 16)

        @block.tensor
        def _(pe):
            pe.wait_ge(prep, 6)
            k = 0
            for i, w in enumerate((wb, wb1)):
                for t in range(T):
                    mm = pe.matmul(ps[0:T, 7, 0:P], sh[:, i, t, :], w[:, t, :],
                                   start=(k == 0), stop=(k == 2 * T - 1))
                    k += 1
            mm.then_inc(const_mm, 1)
            pe.wait_ge(const_out, 1)
            pe.wait_ge(prep, 8)
            for g in range(CHUNKS):
                bank = g % 4
                if g >= 4:
                    pe.wait_ge(affine, g - 3)
                for t in range(T):
                    dh, dw = t // 3 - 1, t % 3 - 1
                    rows = pad[:, R + ROWS * g + dh:R + ROWS * g + dh + ROWS, R + dw:R + dw + W]
                    pe.matmul(ps[:, bank, :], wsum[:, t, :], rows, start=(t == 0), stop=False)
                pe.matmul(ps[:, bank, :], const[:], valid[:, BANK * g:BANK * g + BANK],
                          start=False, stop=True).then_inc(conv_mm, 1)

        @block.scalar
        def _(act):
            act.wait_ge(prep, 5)
            act.activation(bn[:, 1:2], bn[:, 0:1], ACT.Sqrt).then_inc(rooted, 1)
            act.wait_ge(prep, 12)
            for g in range(CHUNKS):
                act.wait_ge(conv_mm, g + 1)
                if g >= 2:
                    act.wait_ge(clipped, g - 1)
                act.activation(lin[g % 2][:].rearrange("p r w -> p (r w)"), ps[:, g % 4, :], ACT.Identity,
                               bias=bn[:, 3:4], scale=bn[:, 2:3]).then_inc(affine, 1)

        @block.vector
        def _(dve):
            wf = wb[:].rearrange("p t m -> p (t m)")
            dve.wait_ge(loaded, 64)
            dve.tensor_scalar(pos[:], raw[:], 0.0, None, ALU.is_gt).then_inc(prep, 1)
            dve.wait_ge(prep, 1)
            dve.scalar_tensor_tensor(out=wf, in0=raw[:], scalar=0.0, in1=pos[:], op0=ALU.is_lt,
                                     op1=ALU.subtract).then_inc(prep, 1)
            dve.tensor_scalar(sh[:, 0], onehot[:], col("shift1"), -1.0, ALU.mult, ALU.mult).then_inc(prep, 1)
            dve.tensor_scalar(sh[:, 1], onehot[:], col("shift2"), -1.0, ALU.mult, ALU.mult).then_inc(prep, 1)
            dve.tensor_scalar(bn[:, 0:1], col("var"), NORM_EPS, None, ALU.add).then_inc(prep, 1)
            scale_rows(dve, wb1, 2).then_inc(prep, 1)
            dve.wait_ge(prep, 6)
            dve.tensor_tensor(wsum[:], wb[:], wb1[:], ALU.add).then_inc(prep, 1)
            dve.wait_ge(prep, 7)
            dve.tensor_scalar(wsum[:].rearrange("p t m -> p (t m)"), wsum[:].rearrange("p t m -> p (t m)"),
                              -1.0, None, ALU.mult).then_inc(prep, 1)
            dve.wait_ge(const_mm, 1)
            dve.tensor_copy(const[:], ps[0:T, 7, 0:P]).then_inc(const_out, 1)
            dve.wait_ge(rooted, 1)
            dve.reciprocal(bn[:, 0:1], bn[:, 1:2]).then_inc(prep, 1)
            dve.wait_ge(prep, 9)
            dve.tensor_tensor(bn[:, 2:3], bn[:, 0:1], col("gamma"), ALU.mult).then_inc(prep, 1)
            dve.wait_ge(prep, 10)
            dve.tensor_tensor(bn[:, 3:4], bn[:, 2:3], col("mean"), ALU.mult).then_inc(prep, 1)
            dve.wait_ge(prep, 11)
            dve.tensor_tensor(bn[:, 3:4], col("beta"), bn[:, 3:4], ALU.subtract).then_inc(prep, 1)
            for g in range(CHUNKS):
                dve.wait_ge(affine, g + 1)
                rows = lambda t: t[:, R + ROWS * g:R + ROWS * g + ROWS, R:R + W]
                dve.tensor_tensor(lin[g % 2][:], lin[g % 2][:], rows(pad), ALU.add).then_inc(resid, 1)
                dve.wait_ge(resid, g + 1)
                dve.tensor_scalar(rows(pad_to), lin[g % 2][:], 1.0, -1.0, ALU.min, ALU.max).then_inc(clipped, 1)



def shape_constants():
    ident = np.eye(P, dtype=np.float32)
    plane_b = (np.arange(P) // HEADS) % B
    same = plane_b[:, None] == plane_b[None, :]
    centre = (ident - same / C).astype(np.float32)
    meansel = ((plane_b[:, None] == np.arange(B)) / C).astype(np.float32)
    qi, qj = np.divmod(np.arange(P), QC)
    pr, pc = np.divmod(np.arange(BLK * BLK), BLK)
    u = qi[:, None, None] + BLK * np.arange(2)[None, :, None] - pr[None, None, :]
    v = (qj[:, None, None] - pc[None, None, :]) + 0 * u
    inside = (u >= 0) & (u < KG) & (v >= 0) & (v < KG)
    gmask = np.where(inside, 0.0, OFF_BAND).astype(np.float32)
    perm = np.eye(P, dtype=np.float32).reshape(P, CP, B, HEADS).transpose(0, 2, 1, 3).reshape(P, P)
    pair = np.tile(np.eye(64, dtype=np.float32), (CP, CP))
    onehot = np.broadcast_to(np.eye(9, dtype=np.float32), (P, 9, 9)).copy()
    valid = np.zeros((9, H, W), np.float32)
    for t in range(9):
        dh, dw = t // 3 - 1, t % 3 - 1
        valid[t, max(0, -dh):H - max(0, dh), max(0, -dw):W - max(0, dw)] = 1.0
    return {"ident": ident, "centre": centre, "meansel": meansel,
            "perm": perm, "pair": pair, "gmask": gmask, "onehot": onehot, "valid": valid.reshape(9, PIX)}, (u, v, inside)


def lay_out(i):
    a, (u, v, inside) = shape_constants()
    part = np.arange(P)
    plane_cp, plane_b, plane_n = part // 64, (part // HEADS) % B, part % HEADS
    chan = CP * plane_n + plane_cp
    f = {k: np.asarray(x) for k, x in i.items()}
    a["x"] = f["x"]

    vec = np.zeros((P, len(VECS)), np.float32)
    for name, src in (("ln_w", "L0_conv_ln_w"), ("ln_b", "L0_conv_ln_b"), ("proj_b", "L0_conv_proj_b"),
                      ("shift1", "L2_conv_shift1"), ("shift2", "L2_conv_shift2"),
                      ("gamma", "L2_conv_gamma"), ("beta", "L2_conv_beta"),
                      ("mean", "L2_conv_running_mean"), ("var", "L2_conv_running_var"),
                      ("w1", "L2_conv_w1")):
        vec[:, VEC[name]] = f[src].reshape(C)[chan]
    for tag, lay in (("g1", "L1_conv_"), ("g3", "L3_conv_")):
        vec[:, VEC[tag + "_b1"]] = f[lay + "b1"][part % HIDDEN]
        vec[:, VEC[tag + "_b2"]] = f[lay + "b2"][0]
        w1 = np.zeros((P, 2, HALF, HIDDEN), np.float32)
        w1[part, plane_b // HALF, plane_b % HALF] = f[lay + "w1"][chan]
        a[tag + "_w1"] = w1.reshape(P, 2, P)
        w2 = np.zeros((P, HALF), np.float32)
        w2[part, part // HIDDEN] = f[lay + "w2"][part % HIDDEN, 0]
        a[tag + "_w2"] = w2
        g = np.zeros((P, 2, BLK * BLK), np.float32)
        g[inside] = f[lay + "gauss_kernel"][u[inside], v[inside]]
        a[tag + "_gband"] = g
    a["vec"] = vec

    taps = np.zeros((2, len(KW), C, BAND), np.float32)
    for t in range(2):
        for k, width in enumerate(KW):
            first = W - 1 - width // 2
            taps[t, k, :, first:first + width] = f[f"L0_conv_w{2 - k}{t + 1}"].reshape(C, width)
    a["taps"] = taps
    one = np.ones(1, np.float32)
    a["bias_lhs"] = np.stack([np.concatenate([f["L0_conv_b" + k + str(t)] for k in "210"] + [one])
                              for t in (1, 2)], 1)
    pw = f["L0_conv_proj_w"]
    a["bias_rhs"] = np.concatenate([pw.T] * 3 + [f["L0_conv_proj_b"][None]])
    same = plane_b[:, None] == plane_b[None, :]
    ii, oo = np.nonzero(same)
    blk = np.zeros((P, P), np.float32)
    blk[ii, oo] = pw[chan[oo], chan[ii]]
    a["projblk"] = blk
    nb = lambda m: m.reshape(CP, B, HEADS, P).transpose(0, 2, 1, 3).reshape(P, P)
    a["projnb"] = nb(nb(blk).T).T
    wt = f["L2_conv_weight"].reshape(C, C, 9)
    cw = np.zeros((P, 9, P), np.float32)
    cw[ii, :, oo] = wt[chan[oo], chan[ii]]
    a["c_weight"] = cw.reshape(P, 9 * P)
    a["c_w1row"] = np.repeat(f["L2_conv_w1"].reshape(1, C)[:, chan], P, axis=0)
    return {k: np.ascontiguousarray(x) for k, x in a.items()}


def kernel(**inputs):
    import concourse.bacc as bacc
    from concourse.bass_utils import run_bass_kernel_spmd

    arrays = lay_out(inputs)
    nc = bacc.Bacc("TRN2", target_bir_lowering=False, num_devices=1)
    d = {k: nc.dram_tensor(f"in_{k}", x.shape, F32, kind="ExternalInput").ap() for k, x in arrays.items()}
    out = nc.dram_tensor("out", (B, C, H, W), F32, kind="ExternalOutput").ap()
    planes = out.rearrange("b (n cp) h w -> cp b n (h w)", cp=CP)
    build(nc, d, [planes[cp].rearrange("b n f -> (b n) f") for cp in range(CP)])
    r = run_bass_kernel_spmd(nc, [{f"in_{k}": x for k, x in arrays.items()}], core_ids=[0])
    return r.results[0]["out"]
```

```python
from contextlib import ExitStack

import numpy as np

import concourse.bass as bass
from concourse import mybir

F32 = mybir.dt.float32
F32R = mybir.dt.float32r
ALU = mybir.AluOpType
ACT = mybir.ActivationFunctionType

P = 128
B, C, H, W = 8, 16, 64, 64
HEADS = 8
CP = C // HEADS
PIX = H * W
BANK = 512
ROWS = BANK // W
CHUNKS = PIX // BANK
PXT = PIX // P

KW = (21, 11, 7)
CENTRE = KW[0] // 2
BAND = H + W - 1

KG = 9
R = KG // 2
BLK = 8
PADDED = H + 2 * R
CB = W // BLK
RB = H // BLK
QC = 2 * BLK
HIDDEN = 32
HALF = B // 2
OFF_BAND = -1e34

TAPS = 9

LN_EPS = 1e-5
L2_EPS_SQ = 1e-24
NORM_EPS = 1e-5

VECS = ["ln_w", "ln_b", "proj_b", "shift1", "shift2", "gamma", "beta", "mean", "var", "w1",
        "g1_b1", "g1_b2", "g3_b1", "g3_b2"]
VEC = {name: i for i, name in enumerate(VECS)}


def spread(ap, shape):
    return ap.broadcast_to(list(shape))


def build(nc, d, band, out):
    keep = ExitStack()
    with keep:
        def sb(stack, name, shape):
            return stack.enter_context(nc.sbuf_tensor(name, shape, F32))

        def sem(name):
            return keep.enter_context(nc.semaphore(name))

        ident = sb(keep, "ident", [P, P])
        vec = sb(keep, "vec", [P, len(VECS)])
        pad_a = sb(keep, "pad_a", [P, PADDED, PADDED])
        ps = keep.enter_context(nc.psum_tensor("ps", [P, 8, BANK], F32))

        later = {}
        for name, shape in (("gmask", [P, 2, BLK * BLK]), ("perm", [P, P]),
                            ("g1_gband", [P, 2, BLK * BLK]), ("g1_w1", [P, 2, P]), ("g1_w2", [P, 2, 32]),
                            ("g3_gband", [P, 2, BLK * BLK]), ("g3_w1", [P, 2, P]), ("g3_w2", [P, 2, 32]),
                            ("c_weight", [P, TAPS * P])):
            later[name] = (sb(keep, name, shape), sem(name + "_in"))
        with ExitStack() as l0:
            x0 = sb(l0, "x0", [P, PIX])
            xrow = sb(l0, "xrow", [P, HEADS, B, H])
            xcol = sb(l0, "xcol", [P, HEADS, B, W])
            toep = sb(l0, "toep", [P, 2, C, P])
            pair = sb(l0, "pair", [P, P])
            rn = sb(l0, "rn", [P, HEADS * 16])
            beta = sb(l0, "beta_o", [P, 2, HEADS])
            projblk = sb(l0, "projblk", [P, P])
            const_in = sem("const_in")
            with ExitStack() as ln:
                l0_norm(nc, sem, lambda n, s: sb(ln, n, s), d, ident, vec, pad_a, ps, x0,
                        xrow, xcol, toep, pair, beta, projblk, const_in, later, band)
            o1c = sb(l0, "o1c", [P, HEADS, B, W])
            o2r = sb(l0, "o2r", [P, HEADS, B, H])
            with ExitStack() as cv:
                l0_conv(nc, sem, lambda n, s: sb(cv, n, s), ident, pair, ps, xrow, xcol, toep, projblk,
                        beta, o1c, o2r, rn)
            attn_c = sb(l0, "attn_c", [P, B, HEADS, W])
            attn_r = sb(l0, "attn_r", [P, B, HEADS, H])
            with ExitStack() as hd:
                after = l0_out(sem, lambda n, s: sb(hd, n, s), ident, vec, ps, x0, attn_c, attn_r,
                               projblk, pad_a, xrow[:].rearrange("p n b h -> p (n b h)"))
                l0_attention(nc, sem, lambda n, s: sb(hd, n, s), ident, ps,
                             xrow, o1c, xcol, o2r, rn, attn_c, attn_r, after)
        pad_b = sb(keep, "pad_b", [P, PADDED, PADDED])
        norm = sb(keep, "norm", [P, 2])
        wb = keep.enter_context(nc.sbuf_tensor("wb", [P, TAPS, P], F32R))
        with ExitStack() as g:
            negative = sb(g, "negative", [P, TAPS * P])
            raw, raw_in = later["c_weight"]
            wb_ready = sem("wb_ready")
            blur(nc, sem, lambda n, s: sb(g, "g1_" + n, s), "g1", later, ident, vec, ps, pad_a, norm, pad_b, None,
                 beside=lambda dve: binary_weights(dve, raw, negative, wb, raw_in, wb_ready))
        with ExitStack() as c:
            binconv(nc, sem, lambda n, s: sb(c, n, s),
                    lambda n, s: c.enter_context(nc.sbuf_tensor(n, s, F32R)), vec, ps, wb, norm, pad_a, pad_b)
        with ExitStack() as g:
            blur(nc, sem, lambda n, s: sb(g, "g3_" + n, s), "g3", later, ident, vec, ps, pad_b, norm, None, out)


def turned_view(lay):
    return lay[:].rearrange("p n b h -> p (n b h)").rearrange("p (m i) -> p m i", i=32)


def l0_norm(nc, sem, sb, d, ident, vec, pad_a, ps, x0, xrow, xcol, toep, pair, beta,
            projblk, const_in, later, band):
    centre = sb("centre", [P, P])
    meansel = sb("meansel", [P, 32])
    var_row = sb("var_row", [P, 2 * BANK])
    taps = sb("taps", [2 * C, len(KW), BAND])
    windows = sb("windows", [P, 2, C, W])
    mask = sb("mask", [P, 2, 2])
    nb = len(KW) * C + 1
    bias_lhs = sb("bias_lhs", [nb, 2])
    bias_rhs = sb("bias_rhs", [nb, C])
    xc = sb("xc", [P, PIX])
    sq = sb("sq", [P, PIX])
    var = sb("var", [P, PXT * B])
    std = sb("std", [P, PXT * B])
    rstd = sb("rstd", [P, PXT, B])
    wide = sb("wide", [P, PXT, CP, B, HEADS])

    x_in = [sem(f"x_in{j}") for j in range(4)]
    centre_in = sem("centre_in")
    centred = sem("centred")
    xc_copied = sem("xc_copied")
    squared = sem("squared")
    bias_mm = sem("bias_mm")
    bias_read = sem("bias_read")
    zeroed = sem("zeroed")
    taps_in = sem("taps_in")
    taps_summed = sem("taps_summed")
    band_out = sem("band_out")
    windows_in = sem("windows_in")
    toep_ready = sem("toep_ready")
    var_mm = sem("var_mm")
    var_out = [sem(f"var_out{a}") for a in range(2)]
    var_turned = sem("var_turned")
    eps_added = sem("eps_added")
    rooted = sem("rooted")
    rstd_ready = sem("rstd_ready")
    rstd_wide = [sem(f"rstd_wide{cp}") for cp in range(CP)]
    rstd_spread = sem("rstd_spread")
    scaled = sem("scaled")
    normed = sem("normed")
    turned = sem("turned")
    evac_v = sem("evac_v")
    evac_s = sem("evac_s")
    CONSTS = 8

    with nc.Block() as block:
        @block.sync
        def _(sp):
            xv = d["x"].rearrange("b (n cp) h w -> cp b n (h w)", cp=CP)
            sp.dma_start(centre[:], d["centre"]).then_inc(centre_in, 16)
            for j in range(4):
                cols = slice(j * PIX // 4, (j + 1) * PIX // 4)
                for cp in range(CP):
                    sp.dma_start(x0[64 * cp:64 * cp + 64, cols],
                                 xv[cp].rearrange("b n f -> (b n) f")[:, cols]).then_inc(x_in[j], 16)
            sp.wait_ge(taps_summed, 2)
            sp.dma_start(band, taps[:, 0, :]).then_inc(band_out, 16)
            sp.wait_ge(band_out, 16)
            for t in range(2):
                for k in range(2):
                    src = bass.AP(tensor=band.tensor, offset=t * C * BAND, ap=[[1, W], [BAND, C], [1, W]])
                    part = slice(64 * k, 64 * k + 64) if t == 0 else slice(k, P, 2)
                    sp.dma_start(windows[part, t], src).then_inc(windows_in, 16)
            for name, (t, arrived) in later.items():
                sp.dma_start(t[:], d[name]).then_inc(arrived, 16)

        @block.gpsimd
        def _(pool):
            pool.memset(pad_a[:], 0.0).then_inc(zeroed, 1)
            pool.wait_ge(windows_in, 16 * 4)
            pool.wait_ge(const_in, 16 * CONSTS)
            pool.tensor_tensor(toep[:, 0].rearrange("p c (k w) -> p c k w", k=2),
                               spread(windows[:, 0, :, ::-1].unsqueeze(2), [P, C, 2, W]),
                               spread(mask[:, 0].unsqueeze(1).unsqueeze(3), [P, C, 2, W]), ALU.mult)\
                .then_inc(toep_ready, 1)
            pool.tensor_tensor(toep[:, 1].rearrange("p c (h k) -> p c h k", k=2),
                               spread(windows[:, 1, :, ::-1].unsqueeze(3), [P, C, H, 2]),
                               spread(mask[:, 1].unsqueeze(1).unsqueeze(1), [P, C, H, 2]), ALU.mult)\
                .then_inc(toep_ready, 1)

        @block.tensor
        def _(pe):
            pe.wait_ge(centre_in, 16)
            for j in range(CHUNKS):
                if j % 2 == 0:
                    pe.wait_ge(x_in[j // 2], 32)
                pe.matmul(ps[:, j, :], centre[:], x0[:, j * BANK:(j + 1) * BANK],
                          start=True, stop=True).then_inc(centred, 1)
            pe.wait_ge(const_in, 16 * CONSTS)
            pe.wait_ge(xc_copied, 5)
            for t in range(2):
                mm = pe.matmul(ps[:, 4, C * t:C * t + C], spread(bias_lhs[:, t:t + 1], [nb, P]),
                               bias_rhs[:], start=True, stop=True)
            mm.then_inc(bias_mm, 1)
            for a in range(2):
                pe.wait_ge(xc_copied, 6 + a)
                for q in range(4):
                    pe.wait_ge(squared, 4 * a + q + 1)
                    mm = pe.matmul(ps[32 * q:32 * q + 32, 5 + a, :], meansel[:],
                                   sq[:, BANK * (4 * a + q):BANK * (4 * a + q + 1)], start=True, stop=True)
                mm.then_inc(var_mm, 1)
            for a in range(2):
                pe.wait_ge(xc_copied, 1 + a)
                pe.wait_ge(var_out[a], 1)
                for c in range(4):
                    tr = pe.transpose(ps[:, a, P * c:P * c + P], var_row[:, BANK * a + P * c:BANK * a + P * c + P],
                                      ident[:])
                tr.then_inc(var_turned, 1)
            pe.wait_ge(bias_read, 4)
            for t in range(PXT):
                if t % 4 == 0:
                    for cp in range(CP):
                        pe.wait_ge(rstd_wide[cp], t // 4 + 1)
                tr = pe.transpose(ps[:, t // 4, P * (t % 4):P * (t % 4) + P],
                                  wide[:, t].rearrange("p c b n -> p (c b n)"), ident[:])
                if t % 4 == 3:
                    tr.then_inc(rstd_spread, 1)
            for base, lines in ((0, sq[:].rearrange("p (i m) -> p i m", m=P)),
                                (CHUNKS, sq[:].rearrange("p (m i) -> p i m", m=P))):
                for g in range(CHUNKS):
                    if base == 0:
                        pe.wait_ge(normed, g + 1)
                    else:
                        pe.wait_ge(evac_s if g % 2 else evac_v, g // 2 + 1)
                    for i in range(4):
                        tr = pe.transpose(ps[:, g, P * i:P * i + P], lines[:, 4 * g + i], ident[:])
                    tr.then_inc(turned, 1)

        def turned_out(lay, g):
            return turned_view(lay)[:, :, 4 * g:4 * g + 4].rearrange("p m i -> p i m")

        def turned_in(g):
            return ps[:, g, :].rearrange("p (i m) -> p i m", m=P)

        def widen(copy, j, cp):
            tiles = slice(4 * j, 4 * j + 4)
            copy(wide[:, tiles, cp], spread(rstd[:, tiles, :].unsqueeze(3), [P, 4, B, HEADS]))\
                .then_inc(rstd_wide[cp], 1)

        @block.scalar
        def _(act):
            act.dma_start(taps[:], d["taps"]).then_inc(taps_in, 16)
            for t, name in ((meansel, "meansel"), (ident, "ident"), (vec, "vec"), (bias_lhs, "bias_lhs"),
                            (bias_rhs, "bias_rhs"), (pair, "pair"), (mask, "mask"), (projblk, "projblk")):
                act.dma_start(t[:], d[name]).then_inc(const_in, 16)
            act.wait_ge(const_in, 16 * CONSTS)
            for j in range(CHUNKS):
                act.wait_ge(xc_copied, j + 1)
                act.activation(sq[:, j * BANK:(j + 1) * BANK], xc[:, j * BANK:(j + 1) * BANK],
                               ACT.Square).then_inc(squared, 1)
            act.wait_ge(var_mm, 2)
            act.copy(var_row[:, BANK:2 * BANK], ps[:, 6, :]).then_inc(var_out[1], 1)
            act.wait_ge(eps_added, 2)
            act.activation(std[:], var[:], ACT.Sqrt).then_inc(rooted, 1)
            act.wait_ge(rstd_ready, 1)
            for j in range(CHUNKS):
                widen(act.copy, j, 1)
            for j in range(CHUNKS):
                act.wait_ge(scaled, j + 1)
                act.activation(sq[:, j * BANK:(j + 1) * BANK], xc[:, j * BANK:(j + 1) * BANK],
                               ACT.Identity, bias=vec[:, VEC["ln_b"]:VEC["ln_b"] + 1],
                               scale=vec[:, VEC["ln_w"]:VEC["ln_w"] + 1]).then_inc(normed, 1)
            for lay, base in ((xrow, 0), (xcol, CHUNKS)):
                for g in range(1, CHUNKS, 2):
                    act.wait_ge(turned, base + g + 1)
                    act.copy(turned_out(lay, g), turned_in(g)).then_inc(evac_s, 1)

        @block.vector
        def _(dve):
            dve.wait_ge(taps_in, 16)
            for k in (1, 2):
                if k == 2:
                    dve.wait_ge(taps_summed, 1)
                dve.tensor_tensor(taps[:, 0], taps[:, 0], taps[:, k], ALU.add).then_inc(taps_summed, 1)
            for j in range(CHUNKS):
                dve.wait_ge(centred, j + 1)
                dve.tensor_copy(xc[:, j * BANK:(j + 1) * BANK], ps[:, j, :]).then_inc(xc_copied, 1)
            dve.wait_ge(bias_mm, 1)
            for t in range(2):
                for cp in range(CP):
                    src = ps[64 * cp:64 * cp + 64, 4, C * t:C * t + C].rearrange("p (n c) -> p c n", c=CP)
                    dve.tensor_copy(beta[64 * cp:64 * cp + 64, t, :], src[:, cp, :]).then_inc(bias_read, 1)
            dve.wait_ge(var_mm, 1)
            dve.tensor_copy(var_row[:, 0:BANK], ps[:, 5, :]).then_inc(var_out[0], 1)
            for a in range(2):
                dve.wait_ge(var_turned, a + 1)
                tiles = ps[:, a, :].rearrange("p (c q m) -> p q c m", c=4, q=4)[:, :, :, 0:B]
                dve.tensor_scalar(var[:].rearrange("p (a q c b) -> p a q c b", a=2, q=4, c=4)[:, a], tiles,
                                  LN_EPS, None, ALU.add).then_inc(eps_added, 1)
            dve.wait_ge(rooted, 1)
            dve.reciprocal(rstd[:].rearrange("p t b -> p (t b)"), std[:]).then_inc(rstd_ready, 1)
            dve.wait_ge(rstd_ready, 1)
            for j in range(CHUNKS):
                widen(dve.tensor_copy, j, 0)
            for j in range(CHUNKS):
                dve.wait_ge(rstd_spread, j + 1)
                dve.tensor_tensor(xc[:, j * BANK:(j + 1) * BANK], xc[:, j * BANK:(j + 1) * BANK],
                                  ps[:, j, :], ALU.mult).then_inc(scaled, 1)
            for lay, base in ((xrow, 0), (xcol, CHUNKS)):
                for g in range(0, CHUNKS, 2):
                    dve.wait_ge(turned, base + g + 1)
                    dve.tensor_copy(turned_out(lay, g), turned_in(g)).then_inc(evac_v, 1)


def l0_conv(nc, sem, sb, ident, pair, ps, xrow, xcol, toep, projblk, beta, o1c, o2r, rn):
    img = [sb(f"conv_img{t}", [P, H, W]) for t in range(2)]
    sqs = sb("sqs", [P, 4, BANK])
    ssum = sb("ssum", [P, 4, HEADS, B])
    nsq = sb("nsq", [P, HEADS, 4, HALF])
    root = sb("root", [P, HEADS * 16])
    lay = (xrow, xcol)

    def channels(t, n):
        return turned_view(lay[t]).rearrange("p (c b n) i -> p n c b i", c=CP, b=B)[:, n]

    conv_mm = sem("conv_mm")
    conv_v = sem("conv_v")
    conv_s = sem("conv_s")
    turn_mm = sem("turn_mm")
    turn_v = sem("turn_v")
    turn_s = sem("turn_s")
    proj_mm = sem("proj_mm")
    proj_out = sem("proj_out")
    squared = sem("q_squared")
    summed = sem("summed")
    nsq_mm = sem("nsq_mm")
    nsq_ready = sem("nsq_ready")
    norm_ready = sem("norm_ready")
    rn_ready = sem("rn_ready")

    JOBS = 2 * CHUNKS
    TENSORS = ((xrow, 2, 0, 0), (o1c, 1, 0, 1), (xcol, 0, 1, 0), (o2r, 3, 1, 1))
    NORM_BANK = 7

    def wait_evacuated(eng, j, on_v, on_s):
        eng.wait_ge(on_v, j // 2 + 1)
        if j > 0:
            eng.wait_ge(on_s, (j + 1) // 2)

    with nc.Block() as block:
        @block.tensor
        def _(pe):
            for j in range(JOBS):
                t, n = divmod(j, HEADS)
                if j >= 4:
                    wait_evacuated(pe, j - 4, conv_v, conv_s)
                for cp in range(CP):
                    mm = pe.matmul(ps[:, j % 4, 256 * cp:256 * cp + 256], toep[:, t, CP * n + cp, :],
                                   channels(t, n)[:, cp], start=True, stop=True)
                mm.then_inc(conv_mm, 1)
            for j in range(JOBS):
                t, g = divmod(j, CHUNKS)
                if g == 0:
                    wait_evacuated(pe, (t + 1) * HEADS - 1, conv_v, conv_s)
                if j < 4:
                    wait_evacuated(pe, JOBS - 4 + j, conv_v, conv_s)
                else:
                    wait_evacuated(pe, j - 4, turn_v, turn_s)
                for i in range(4):
                    mm = pe.transpose(ps[:, j % 4, P * i:P * i + P], turned_view(lay[t])[:, :, 4 * g + i], ident[:])
                mm.then_inc(turn_mm, 1)
            for i, (_, _, t, inner) in enumerate(TENSORS):
                planes = img[t][:] if inner == 0 else img[t][:].rearrange("p h w -> p w h")
                for g in range(CHUNKS):
                    j = CHUNKS * i + g
                    if j < 4:
                        wait_evacuated(pe, JOBS - 4 + j, turn_v, turn_s)
                    else:
                        pe.wait_ge(proj_out, j - 3)
                    if i == 0 and g == 4:
                        wait_evacuated(pe, JOBS - 1, turn_v, turn_s)
                    for hh in range(ROWS):
                        for cp in range(CP):
                            mm = pe.matmul(ps[64 * cp:64 * cp + 64, j % 4, 64 * hh:64 * hh + 64],
                                           planes[:, ROWS * g + hh], projblk[:, 64 * cp:64 * cp + 64],
                                           start=True, stop=True)
                    mm.then_inc(proj_mm, 1)
            pe.wait_ge(summed, 4 * HEADS)
            pe.matmul(ps[:, NORM_BANK, 0:4 * HEADS * B], pair[:], ssum[:].rearrange("p t m b -> p (t m b)"),
                      start=True, stop=True).then_inc(nsq_mm, 1)

        def evacuate(eng, copy, odd, on_conv, on_turn):
            for j in range(odd, JOBS, 2):
                t, n = divmod(j, HEADS)
                eng.wait_ge(conv_mm, j + 1)
                copy(channels(t, n), ps[:, j % 4, :].rearrange("p (c b i) -> p c b i", c=CP, b=B))\
                    .then_inc(on_conv, 1)
            for j in range(odd, JOBS, 2):
                t, g = divmod(j, CHUNKS)
                eng.wait_ge(turn_mm, j + 1)
                if t == 0:
                    copy(img[t][:, ROWS * g:ROWS * g + ROWS, :].rearrange("p r c -> p (r c)"),
                         ps[:, j % 4, :]).then_inc(on_turn, 1)
                else:
                    copy(img[t][:].rearrange("p (k i) h -> p i k h", k=2)[:, 4 * g:4 * g + 4],
                         ps[:, j % 4, :].rearrange("p (i h k) -> p i k h", i=4, k=2)).then_inc(on_turn, 1)

        @block.scalar
        def _(act):
            evacuate(act, act.copy, 1, conv_s, turn_s)
            for i in range(len(TENSORS)):
                act.wait_ge(proj_out, CHUNKS * (i + 1))
                for m in range(HEADS):
                    if HEADS * i + m >= 4:
                        act.wait_ge(summed, HEADS * i + m - 3)
                    act.activation(sqs[:, m % 4, :], TENSORS[i][0][:, m].rearrange("p b h -> p (b h)"),
                                   ACT.Square).then_inc(squared, 1)
            act.wait_ge(nsq_ready, CP)
            act.activation(root[:], nsq[:].rearrange("p m t k -> p (m t k)"), ACT.Sqrt).then_inc(norm_ready, 1)

        @block.vector
        def _(dve):
            evacuate(dve, dve.tensor_copy, 0, conv_v, turn_v)
            def row_sums(i, m):
                dve.wait_ge(squared, HEADS * i + m + 1)
                dve.tensor_reduce(ssum[:, TENSORS[i][1], m, :], sqs[:, m % 4, :].rearrange("p (b h) -> p b h", b=B),
                                  mybir.AxisListType.X, ALU.add).then_inc(summed, 1)

            for i, (dst, _, t, _) in enumerate(TENSORS):
                for g in range(CHUNKS):
                    dve.wait_ge(proj_mm, CHUNKS * i + g + 1)
                    dve.tensor_tensor(dst[:, :, :, ROWS * g:ROWS * g + ROWS].rearrange("p m b h -> p h m b"),
                                      ps[:, g % 4, :].rearrange("p (h b m) -> p h m b", h=ROWS, b=B),
                                      spread(beta[:, t, :].unsqueeze(1).unsqueeze(3), [P, ROWS, HEADS, B]),
                                      ALU.add).then_inc(proj_out, 1)
                    if i > 0:
                        row_sums(i - 1, g)
            for m in range(HEADS):
                row_sums(3, m)
            dve.wait_ge(nsq_mm, 1)
            for odd in range(2):
                part = slice(64 * odd, 64 * odd + 64)
                sums = ps[part, NORM_BANK, 0:4 * HEADS * B].rearrange("p (t m k o) -> p o m t k", t=4, m=HEADS, o=2)
                dve.tensor_scalar(nsq[part], sums[:, odd], L2_EPS_SQ, None, ALU.max).then_inc(nsq_ready, 1)
            dve.wait_ge(norm_ready, 1)
            dve.reciprocal(rn[:], root[:]).then_inc(rn_ready, 1)


def l0_attention(nc, sem, sb, ident, ps, o1r, o1c, o2c, o2r, rn, attn_c, attn_r, after):
    q1 = [sb(f"q1{s}", [P, B, H]) for s in range(2)]
    q2 = [sb(f"q2{s}", [P, B, W]) for s in range(2)]
    k1 = sb("k1", [P, B, H])
    k2 = sb("k2", [P, B, W])
    e = [sb(f"e{t}", [P, B, H]) for t in range(2)]
    rz = [sb(f"rz{t}", [P, B]) for t in range(2)]
    mean = [sb(f"wmean{t}", [P, B, H]) for t in range(2)]
    V = H + 1
    v = [[sb(f"v{s}{t}", [P, B, V]) for t in range(2)] for s in range(2)]
    rnh = [sb(f"rnh{s}", [P, 16]) for s in range(2)]

    ones_set = sem("ones_set")
    rn_head = sem("rn_head")
    v_head = sem("v_head")
    rn_spread = sem("rn_spread")
    unit = sem("unit")
    score_mm = sem("score_mm")
    exped = sem("exped")
    av_mm = sem("av_mm")
    rz_ready = sem("rz_ready")
    averaged = sem("averaged")
    attn_out = sem("attn_out")

    QUAD = [(64 * cp, 64 * cp + 64) for cp in range(CP)]
    NORM, SCORE, OUT = (0, 1), (2, 3), ((4, 5), (6, 7))

    def wait_apart(eng, semaphore, value):
        eng.wait_ge(semaphore, value)
        eng.nop(nofuse=True)

    def is0(m):
        return isinstance(m, int) and m == 0

    def head(lay, m):
        return lay[:, bass.ds(m, 1)].rearrange("p o b h -> p (o b h)")

    def flat(t):
        return t[:].rearrange("p b h -> p (b h)")

    def spread_norms(pe, m, s, pair):
        if pair == 0:
            pe.wait_ge(rn_head, m + 1)
        for t in (2 * pair, 2 * pair + 1):
            if not (is0(m) and pair == 0):
                pe.wait_ge(unit, 4 * m + t - 1)
            for k in range(4):
                tr = pe.transpose(ps[:, NORM[t % 2], P * k:P * k + P],
                                  spread(rnh[s][:, 4 * t + k:4 * t + k + 1], [P, P]), ident[:])
            tr.then_inc(rn_spread, 1)

    def scores(pe, m, s):
        for t, (q, k) in enumerate(((q1[s], k1), (q2[s], k2))):
            pe.wait_ge(unit, 4 * m + 2 * t + 2)
            for b in range(B):
                for lo, hi in QUAD:
                    mm = pe.matmul(ps[lo:hi, SCORE[t], 64 * b:64 * b + 64], k[:, b, :], q[:, b, :],
                                   start=True, stop=True)
            mm.then_inc(score_mm, 1)

    def outputs(pe, m, s, t):
        wait_apart(pe, exped, 2 * m + t + 1)
        wait_apart(pe, v_head, 2 * m + t + 1)
        if not is0(m):
            wait_apart(pe, attn_out, 2 * m + t - 1)
        for first in range(2):
            for b0 in range(B // 2):
                for i, (b, bank) in enumerate(((b0, OUT[t][0]), (b0 + 4, OUT[t][1]))):
                    lo, hi = QUAD[first ^ i]
                    mm = pe.matmul(ps[lo:hi, bank, V * b0:V * b0 + V], e[t][lo:hi, b, :],
                                   v[s][t][lo:hi, b, :], start=True, stop=True)
        mm.then_inc(av_mm, 1)

    def pe_head(pe, m, s, more):
        scores(pe, m, s)
        for t in range(2):
            if more:
                spread_norms(pe, m + 1, 1 - s, t)
            outputs(pe, m, s, t)

    def values(act, m, s):
        for t, src in enumerate((o1c, o2r)):
            if not (isinstance(m, int) and m < 2):
                act.wait_ge(av_mm, 2 * (m - 2) + t + 1)
            act.copy(v[s][t][:, :, 0:H], head(src, m).rearrange("p (b h) -> p b h", b=B)).then_inc(v_head, 1)

    def act_head(act, m, s, more):
        for t in range(2):
            act.wait_ge(score_mm, 2 * m + t + 1)
            act.activation(flat(e[t]), ps[:, SCORE[t], :], ACT.Exp).then_inc(exped, 1)
        if more:
            values(act, m + 1, 1 - s)

    def normalise(dve, m, s, pair):
        dst = ((q1[s], k1), (q2[s], k2))[pair]
        src = ((o2r, o1r), (o1c, o2c))[pair]
        if not (isinstance(m, int) and m < 2):
            dve.wait_ge(attn_out, 2 * (m - 2) + 2)
        for i in range(2):
            t = 2 * pair + i
            dve.wait_ge(rn_spread, 4 * m + t + 1)
            dve.tensor_tensor(flat(dst[i]), head(src[i], m), ps[:, NORM[i], :], ALU.mult).then_inc(unit, 1)

    def finish(dve, m, s, t):
        sums = ps[:, OUT[t][0]:OUT[t][1] + 1, 0:HALF * V].rearrange("p k (b c) -> p k b c", c=V)
        dve.wait_ge(av_mm, 2 * m + t + 1)
        if not is0(m):
            dve.wait_ge(averaged, 2 * m + t - 1)
        dve.reciprocal(rz[t][:].rearrange("p (k b) -> p k b", k=2), sums[:, :, :, H]).then_inc(rz_ready, 1)
        dve.wait_ge(rz_ready, 2 * m + t + 1)
        if not is0(m):
            dve.wait_ge(attn_out, 2 * m + t - 1)
        dve.tensor_tensor(mean[t][:].rearrange("p (k b) h -> p k b h", k=2), sums[:, :, :, 0:H],
                          spread(rz[t][:].rearrange("p (k b) -> p k b", k=2).unsqueeze(3), [P, 2, HALF, H]),
                          ALU.mult).then_inc(averaged, 1)
        dve.wait_ge(averaged, 2 * m + t + 1)
        dst = (attn_c, attn_r)[t][:, :, bass.ds(m, 1), :].rearrange("p b o h -> p b (o h)")
        dve.tensor_tensor(dst, mean[t][:], (q2, q1)[t][s][:], ALU.add).then_inc(attn_out, 1)

    def dve_head(dve, m, s, more):
        for t in range(2):
            if more:
                normalise(dve, m + 1, 1 - s, t)
            finish(dve, m, s, t)

    def norms(pool, m, s):
        if not (isinstance(m, int) and m < 2):
            pool.wait_ge(rn_spread, 4 * (m - 1))
        pool.tensor_copy(rnh[s][:], rn[:, bass.ds(16 * m, 16)]).then_inc(rn_head, 1)

    def pool_head(pool, m, s, more):
        if more:
            norms(pool, m + 1, 1 - s)

    def heads_of(eng, head_steps):
        for m in range(2):
            head_steps(eng, m, m, True)
        with eng.Fori(0, 2) as i:
            for p in range(2):
                head_steps(eng, 2 * i + 2 + p, p, True)
        for m in range(HEADS - 2, HEADS):
            head_steps(eng, m, m % 2, m + 1 < HEADS)

    def wait_attention(eng, t):
        eng.wait_ge(unit, 4 * HEADS)
        eng.wait_ge(attn_out, 2 * HEADS - 1 + t)

    out_tensor, out_scalar, out_vector = after
    with nc.Block() as block:
        @block.tensor
        def _(pe):
            for pair in range(2):
                spread_norms(pe, 0, 0, pair)
            pe.wait_ge(ones_set, 2 * 2)
            heads_of(pe, pe_head)
            out_tensor(pe, wait_attention)

        @block.scalar
        def _(act):
            values(act, 0, 0)
            heads_of(act, act_head)
            out_scalar(act, wait_attention)

        @block.vector
        def _(dve):
            for pair in range(2):
                normalise(dve, 0, 0, pair)
            heads_of(dve, dve_head)
            out_vector(dve, wait_attention)

        @block.gpsimd
        def _(pool):
            norms(pool, 0, 0)
            for s in range(2):
                for t in range(2):
                    pool.memset(v[s][t][:, :, H:V], 1.0).then_inc(ones_set, 1)
            heads_of(pool, pool_head)


def l0_out(sem, sb, ident, vec, ps, x0, attn_c, attn_r, projblk, pad, img):
    bias2 = sb("bias2", [P, 1])
    turned = sem("o_turned")
    copied_v = sem("o_copied_v")
    copied_s = sem("o_copied_s")
    summed = sem("o_summed")
    projected = sem("o_projected")
    added = sem("o_added")
    bias2_ready = sem("o_bias2")
    columns = attn_c[:].rearrange("p b n w -> p w (b n)")
    rows = attn_r[:].rearrange("p b n h -> p h (b n)")

    def on_tensor(pe, wait_attention):
        def project(g):
            pe.wait_ge(summed, g + 1)
            pe.matmul(ps[:, g, :], projblk[:], img[:, BANK * g:BANK * g + BANK],
                      start=True, stop=True).then_inc(projected, 1)

        def turn(planes, g):
            for hh in range(ROWS):
                for cp in range(CP):
                    mm = pe.matmul(ps[64 * cp:64 * cp + 64, g, W * hh:W * hh + W],
                                   planes[:, ROWS * g + hh], ident[:, 64 * cp:64 * cp + 64],
                                   start=True, stop=True)
            mm.then_inc(turned, 1)

        wait_attention(pe, 0)
        for g in range(CHUNKS):
            if g == 6:
                wait_attention(pe, 1)
            turn(columns, g)
        for g in range(CHUNKS):
            pe.wait_ge(copied_v if g % 2 == 0 else copied_s, g // 2 + 1)
            turn(rows, g)
            if g > 0:
                project(g - 1)
        project(CHUNKS - 1)

    def copy_columns(eng, copy, odd, done):
        for g in range(odd, CHUNKS, 2):
            eng.wait_ge(turned, g + 1)
            copy(img[:].rearrange("p (h w) -> p w h", w=W)[:, ROWS * g:ROWS * g + ROWS],
                 ps[:, g, :].rearrange("p (w h) -> p w h", h=H)).then_inc(done, 1)

    def on_scalar(act, wait_attention):
        wait_attention(act, 0)
        copy_columns(act, act.copy, 1, copied_s)

    def on_vector(dve, wait_attention):
        pb = vec[:, VEC["proj_b"]:VEC["proj_b"] + 1]
        dve.tensor_tensor(bias2[:], pb, pb, ALU.add).then_inc(bias2_ready, 1)
        dve.wait_ge(bias2_ready, 1)
        wait_attention(dve, 0)
        copy_columns(dve, dve.tensor_copy, 0, copied_v)
        dve.wait_ge(copied_v, CHUNKS // 2)
        dve.wait_ge(copied_s, CHUNKS // 2)

        def add(g):
            dve.wait_ge(projected, g + 1)
            dve.scalar_tensor_tensor(
                out=pad[:, R + ROWS * g:R + ROWS * g + ROWS, R:R + W],
                in0=ps[:, g, :].rearrange("p (h w) -> p h w", w=W), scalar=bias2[:, 0:1],
                in1=x0[:, BANK * g:BANK * g + BANK].rearrange("p (h w) -> p h w", w=W),
                op0=ALU.add, op1=ALU.add).then_inc(added, 1)
        for g in range(CHUNKS):
            dve.wait_ge(turned, CHUNKS + g + 1)
            part = img[:, BANK * g:BANK * g + BANK]
            dve.tensor_tensor(part, part, ps[:, g, :], ALU.add).then_inc(summed, 1)
            if g > 0:
                add(g - 1)
        add(CHUNKS - 1)

    return on_tensor, on_scalar, on_vector


def blur(nc, sem_, sb, tag, later, ident, vec, ps, pad, norm, to_clear, out, beside=None):
    def sem(name):
        return sem_(f"{tag}_{name}")

    names = (tag + "_w1", tag + "_w2", tag + "_gband", "gmask", "perm")
    w1, w2, gband_in, gmask, perm = (later[name][0] for name in names)
    arrived = [later[name][1] for name in names]
    gband = sb("exponents", [P, 2, BLK * BLK])
    tile = [sb(f"tile{s}", [P, CB, BLK, QC]) for s in range(2)]
    xt = [sb(f"xt{s}", [P, CB, B, 2 * C]) for s in range(2)]
    hid = [sb(f"hid{i}", [P, CB, BLK, BLK]) for i in range(2)]
    sm = [sb(f"sm{i}", [P, 4 * B]) for i in range(2)]
    relu = sb("relu", [P, P])
    scl = [sb(f"scl{s}", [P, 4, B]) for s in range(2)]
    wgt = [[sb(f"wgt{s}{u}", [P, 2, CB, BLK * BLK]) for u in range(B)] for s in range(2)]
    num = [sb(f"num{s}", [P, BANK]) for s in range(2)]
    rz = sb("rzb", [P, 4, HALF])
    mix = sb("mix", [P, 4, CP, B, HEADS])
    stats = sb("stats", [P, RB, 6])
    mv = sb("mv", [P, 2])
    std = sb("stdb", [P, 2])
    shift = sb("shift", [P, 1])
    result = sb("result", [P, PIX]) if out is not None else None

    const_ready = sem("const_ready")
    band_ready = sem("band_ready")
    staged = sem("staged")
    xt_mm = sem("xt_mm")
    xt_out = sem("xt_out")
    hid_mm = sem("hid_mm")
    hid_out = sem("hid_out")
    ks_mm = sem("ks_mm")
    ks_turned = sem("ks_turned")
    small = sem("small")
    scl_spread = sem("scl_spread")
    logit = sem("logit")
    weight = sem("weight")
    blurred = sem("blurred")
    num_out = sem("num_out")
    num_turned = sem("num_turned")
    rz_ready = sem("rz_ready")
    mixed = sem("mixed")
    low_mm = sem("low_mm")
    enhanced = sem("enhanced")
    stat = sem("stat")
    tail = sem("tail")
    rooted = sem("rooted")
    finished = [sem(f"finished{k}") for k in range(2)]
    stored = sem("stored")

    O_BANK, NT_BANK, XT_BANK, MLP_BANK = 4, 5, 6, 7

    def is0(r):
        return isinstance(r, int) and r == 0

    def pe_hidden(pe, r, i):
        if i == 0:
            if not is0(r):
                pe.wait_ge(small, 4 * (r - 1) + 2)
                pe.wait_ge(xt_out, 2 * r)
        else:
            pe.wait_ge(hid_out, 2 * r + 1)
        rows = bass.ds(BLK * r + R, BLK)
        pe.matmul(ps[:, MLP_BANK, :], w1[:, i, :], pad[:, rows, R:R + W],
                  start=True, stop=True).then_inc(hid_mm, 1)

    def pe_ks(pe, r):
        pe.wait_ge(hid_out, 2 * r + 2)
        for i in range(2):
            for k in range(4):
                px = hid[i][:, 2 * k:2 * k + 2].rearrange("p t r c -> p (t r c)")
                mm = pe.matmul(ps[32 * k:32 * k + 32, MLP_BANK, 0:P], w2[:, i, :], px,
                               start=(i == 0), stop=(i == 1))
        mm.then_inc(ks_mm, 1)

    def pe_ks_turn(pe, r):
        pe.wait_ge(small, 4 * r + 1)
        pe.transpose(ps[:, MLP_BANK, P:2 * P], relu[:], ident[:]).then_inc(ks_turned, 1)

    def pe_xt(pe, g, s, k):
        bank = (XT_BANK, MLP_BANK)[k]
        if k == 0:
            pe.wait_ge(staged, g + 1)
            if not is0(g):
                pe.wait_ge(xt_out, 2 * g - 1)
        else:
            pe.wait_ge(small, 4 * (RB - 1) + 2 if isinstance(g, int) and g == RB else 4 * g + 2)
        for j in range(4):
            cb = 4 * k + j
            tr = pe.transpose(ps[:, bank, P * j:P * j + P],
                              tile[s][:, cb].rearrange("p r c -> p (r c)"), perm[:])
        tr.then_inc(xt_mm, 1)

    def pe_spread(pe, r, s, u):
        if u == 0:
            pe.wait_ge(small, 4 * r + 4)
        if not (is0(r) and u < 4):
            pe.wait_ge(logit, 8 * r + u - 3)
        for k in range(4):
            tr = pe.transpose(ps[:, u % 4, P * k:P * k + P], spread(scl[s][:, k, u:u + 1], [P, P]),
                              ident[:])
        tr.then_inc(scl_spread, 1)

    def pe_blur(pe, r, s, i, part):
        if part == 0:
            pe.wait_ge(weight, 8 * r + 4 * i + 4)
            pe.wait_ge(xt_out, 2 * r + 4)
            if not (is0(r) and i == 0):
                pe.wait_ge(num_out, 2 * r + i)
        for cb in range(4 * part, 4 * part + 4):
            for t in range(2):
                for j in range(HALF):
                    b = HALF * i + j
                    mm = pe.matmul(ps[32 * j:32 * j + 32, O_BANK, 64 * cb:64 * cb + 64],
                                   xt[(s + t) % 2][:, cb, b, :], wgt[s][b][:, t, cb, :],
                                   start=(t == 0), stop=(t == 1))
        if part == 1:
            mm.then_inc(blurred, 1)

    def pe_turn(pe, r, i):
        pe.wait_ge(num_out, 2 * r + i + 1)
        if i == 1:
            pe.wait_ge(mixed, 2 * r + 1)
        elif not is0(r):
            pe.wait_ge(enhanced, r)
        for k in range(4):
            tr = pe.transpose(ps[:, NT_BANK, P * k:P * k + P], num[i][:, P * k:P * k + P], ident[:])
        tr.then_inc(num_turned, 1)

    def pe_low(pe, r):
        pe.wait_ge(mixed, 2 * r + 2)
        for k in range(4):
            px = mix[:, k].rearrange("p c b n -> p (c b n)")
            tr = pe.transpose(ps[:, NT_BANK, P * k:P * k + P], px, ident[:])
        tr.then_inc(low_mm, 1)

    def pe_row(pe, r, s, do):
        for u in range(B):
            if u + 2 < B:
                if do.main:
                    pe_spread(pe, r, s, u + 2)
            elif do.next:
                pe_spread(pe, r + 1, 1 - s, u + 2 - B)
            if u < 2 and do.first:
                pe_hidden(pe, 1, u)
            if u == (2 if do.first else 0) and do.next:
                pe_ks(pe, r + 1)
            if u == 1 and do.lag:
                pe_turn(pe, r - 1, 0)
                pe_blur(pe, r - 1, 1 - s, 1, 0)
            if u == (3 if do.first else 2) and do.next:
                pe_ks_turn(pe, r + 1)
            if u == 2 and do.lag:
                pe_blur(pe, r - 1, 1 - s, 1, 1)
            if u == 4 and do.main:
                pe_xt(pe, r + 1, 1 - s, 0)
                pe_xt(pe, r + 1, 1 - s, 1)
            if u == 5 and do.lag:
                pe_turn(pe, r - 1, 1)
            if u == 6:
                if do.after_next:
                    pe_hidden(pe, r + 2, 0)
                if do.main:
                    pe_blur(pe, r, s, 0, 0)
            if u == 7:
                if do.after_next:
                    pe_hidden(pe, r + 2, 1)
                if do.lag:
                    pe_low(pe, r - 1)
                if do.main:
                    pe_blur(pe, r, s, 0, 1)

    def act_hidden(act, r, i):
        act.wait_ge(hid_mm, 2 * r + i + 1)
        if not is0(r):
            act.wait_ge(ks_mm, r)
        act.activation(hid[i][:].rearrange("p k r c -> p r k c"),
                       ps[:, MLP_BANK, :].rearrange("p (r k c) -> p r k c", r=BLK, k=CB), ACT.Relu,
                       bias=vec[:, VEC[tag + "_b1"]:VEC[tag + "_b1"] + 1], scale=1.0).then_inc(hid_out, 1)

    def act_xt(act, g, s, k):
        act.wait_ge(xt_mm, 2 * g + k + 1)
        if not (isinstance(g, int) and g < 2):
            act.wait_ge(blurred, 2 * (g - 1))
        act.copy(xt[s][:, 4 * k:4 * k + 4, :, 0:C],
                 ps[:, (XT_BANK, MLP_BANK)[k], :].rearrange("p (k b m) -> p k b m", k=4, b=B)).then_inc(xt_out, 1)

    def act_weight(act, r, s, u):
        act.wait_ge(logit, 8 * r + u + 1)
        w = wgt[s][u][:].rearrange("p t k m -> p (t k m)")
        act.activation(w, w, ACT.Exp).then_inc(weight, 1)

    def act_num(act, r, i):
        act.wait_ge(blurred, 2 * r + i + 1)
        if not is0(r):
            act.wait_ge(num_turned, 2 * r + i - 1)
        act.copy(num[i][:], ps[:, O_BANK, :]).then_inc(num_out, 1)

    def act_row(act, r, s, do):
        for u in range(B):
            if do.main:
                act_weight(act, r, s, u)
            if u < 2 and do.first:
                act_hidden(act, 1, u)
            if u == 3 and do.lag:
                act_num(act, r - 1, 1)
            if u == 4 and do.main:
                act_xt(act, r + 1, 1 - s, 0)
                act_xt(act, r + 1, 1 - s, 1)
            if u == 6 and do.after_next:
                act_hidden(act, r + 2, 0)
            if u == 7:
                if do.after_next:
                    act_hidden(act, r + 2, 1)
                if do.main:
                    act_num(act, r, 0)

    def dve_small(dve, r, s, k):
        flat = scl[s][:].rearrange("p k b -> p (k b)")
        if k == 0:
            dve.wait_ge(ks_mm, r + 1)
            if not is0(r):
                dve.wait_ge(ks_turned, r)
            dve.tensor_scalar(relu[:], ps[:, MLP_BANK, 0:P], vec[:, VEC[tag + "_b2"]:VEC[tag + "_b2"] + 1],
                              0.0, ALU.add, ALU.max).then_inc(small, 1)
            return
        dve.wait_ge(small, 4 * r + k)
        if k == 1:
            dve.wait_ge(ks_turned, r + 1)
            ks = ps[:, MLP_BANK, P:2 * P].rearrange("p (k m) -> p k m", k=4)[:, :, 0:B]
            dve.tensor_scalar(sm[0][:].rearrange("p (k b) -> p k b", k=4), ks, 20.0, 1.0, ALU.mult, ALU.add).then_inc(small, 1)
        if k == 2:
            dve.tensor_tensor(sm[1][:], sm[0][:], sm[0][:], ALU.mult).then_inc(small, 1)
        if k == 3:
            dve.reciprocal(flat, sm[1][:]).then_inc(small, 1)

    def dve_logit(dve, r, s, u):
        dve.wait_ge(scl_spread, 8 * r + u + 1)
        if not (isinstance(r, int) and r < 2):
            dve.wait_ge(blurred, 2 * r + u // 4 - 3)
        shape = [P, 2, CB, BLK * BLK]
        s_in = ps[:, u % 4, :].rearrange("p (k m) -> p k m", k=CB).unsqueeze(1)
        dve.tensor_tensor(wgt[s][u][:], spread(gband[:].unsqueeze(2), shape), spread(s_in, shape),
                          ALU.mult).then_inc(logit, 1)

    def dve_mix(dve, r, i):
        nt = ps[:, NT_BANK, :].rearrange("p (k b m) -> p k b m", k=4, b=HALF)
        dve.wait_ge(num_turned, 2 * r + i + 1)
        dve.reciprocal(rz[:], nt[:, :, :, C]).then_inc(rz_ready, 1)
        dve.wait_ge(rz_ready, 2 * r + i + 1)
        if i == 0 and not is0(r):
            dve.wait_ge(low_mm, r)
        for cp in range(CP):
            ins = dve.tensor_tensor(mix[:, :, cp, HALF * i:HALF * i + HALF, :],
                                    nt[:, :, :, HEADS * cp:HEADS * cp + HEADS],
                                    spread(rz[:].unsqueeze(3), [P, 4, HALF, HEADS]), ALU.mult)
        ins.then_inc(mixed, 1)

    def dve_enhance(dve, r):
        dve.wait_ge(low_mm, r + 1)
        rows = pad[:, bass.ds(BLK * r + R, BLK), R:R + W].rearrange("p r (k c) -> p r k c", c=BLK)
        low = ps[:, NT_BANK, :].rearrange("p (k r c) -> p r k c", k=CB, r=BLK)
        dve.tensor_tensor(rows, rows, low, ALU.add).then_inc(enhanced, 1)

    def dve_stats(dve, r):
        dve.wait_ge(enhanced, r + 1)
        dve.bn_stats(stats[:, bass.ds(r, 1), :].rearrange("p o s -> p (o s)"),
                     pad[:, bass.ds(BLK * r + R, BLK), R:R + W]).then_inc(stat, 1)

    def dve_row(dve, r, s, do):
        for u in range(B):
            if do.main:
                dve_logit(dve, r, s, u)
            if u == 0 and do.lag2:
                dve_enhance(dve, r - 2)
            if u == 1 and do.lag2:
                dve_stats(dve, r - 2)
            if 1 < u < 5 and do.next:
                dve_small(dve, r + 1, 1 - s, u - 2)
                if u == 4:
                    dve_small(dve, r + 1, 1 - s, 3)
            if u == 2 and do.lag:
                dve_mix(dve, r - 1, 0)
            if u == 6 and do.lag:
                dve_mix(dve, r - 1, 1)

    class Row:

        def __init__(self, r):
            self.first, self.main, self.lag, self.lag2 = r == 0, r < RB, 0 < r <= RB, r > 1
            self.next, self.after_next = r + 1 < RB, r + 2 < RB

    def rows_of(eng, row):
        for r in range(2):
            row(eng, r, r, Row(r))
        with eng.Fori(0, 2) as i:
            for p in range(2):
                row(eng, 2 * i + 2 + p, p, Row(2))
        for r in range(RB - 2, RB + 2):
            row(eng, r, r % 2, Row(r))

    def quarter(j):
        return (pad[:, R + 16 * j:R + 16 * j + 16, R:R + W],
                result[:, j * PIX // 4:(j + 1) * PIX // 4].rearrange("p (h w) -> p h w", w=W))

    with nc.Block() as block:
        @block.sync
        def _(sp):
            if out is not None:
                for j in range(4):
                    sp.wait_ge(finished[j % 2], j // 2 + 1)
                    cols = slice(j * PIX // 4, (j + 1) * PIX // 4)
                    for cp in range(CP):
                        sp.dma_start(out[cp][:, cols], result[64 * cp:64 * cp + 64, cols]).then_inc(stored, 16)
                sp.wait_ge(stored, 16 * 4 * CP)

        @block.gpsimd
        def _(pool):
            def stage(g, s):
                if not (isinstance(g, int) and g < 2):
                    pool.wait_ge(xt_mm, 2 * (g - 1))
                for odd in range(2):
                    cols = pad[:, bass.ds(BLK * g, BLK), BLK * odd:BLK * odd + W]
                    ins = pool.tensor_copy(tile[s][:].rearrange("p (k o) r c -> p o k r c", o=2)[:, odd],
                                           cols.rearrange("p r (k c) -> p k r c", c=QC))
                ins.then_inc(staged, 1)
            stage(0, 0)
            for s in range(2):
                pool.memset(xt[s][:, :, :, C:2 * C], 0.0).then_inc(const_ready, 1)
            pool.wait_ge(const_ready, 2)
            for s in range(2):
                pool.memset(xt[s][:, :, :, C:C + 1], 1.0).then_inc(const_ready, 1)
            stage(1, 1)
            with pool.Fori(0, 3) as i:
                for p in range(2):
                    stage(2 * i + 2 + p, p)
            stage(RB, 0)
            if to_clear is not None:
                pool.memset(to_clear[:], 0.0).then_inc(sem("cleared"), 1)

        @block.tensor
        def _(pe):
            for a in arrived:
                pe.wait_ge(a, 16)
            pe_hidden(pe, 0, 0)
            pe_hidden(pe, 0, 1)
            pe_ks(pe, 0)
            pe_xt(pe, 0, 0, 0)
            pe_ks_turn(pe, 0)
            pe_spread(pe, 0, 0, 0)
            pe_spread(pe, 0, 0, 1)
            pe_xt(pe, 0, 0, 1)
            pe.wait_ge(const_ready, 4)
            rows_of(pe, pe_row)

        @block.scalar
        def _(act):
            act_hidden(act, 0, 0)
            act_hidden(act, 0, 1)
            act_xt(act, 0, 0, 0)
            act_xt(act, 0, 0, 1)
            rows_of(act, act_row)
            act.wait_ge(tail, 2)
            act.activation(std[:, 1:2], std[:, 0:1], ACT.Sqrt).then_inc(rooted, 1)
            if out is not None:
                act.wait_ge(tail, 5)
                for j in range(1, 4, 2):
                    rows, dst = quarter(j)
                    act.activation(dst, rows, ACT.Identity, bias=shift[:, 0:1], scale=norm[:, 1:2])\
                        .then_inc(finished[1], 1)

        @block.vector
        def _(dve):
            for a in arrived:
                dve.wait_ge(a, 16)
            dve.scalar_tensor_tensor(out=gband[:].rearrange("p t m -> p (t m)"),
                                     in0=gband_in[:].rearrange("p t m -> p (t m)"), scalar=-4.5,
                                     in1=gmask[:].rearrange("p t m -> p (t m)"),
                                     op0=ALU.mult, op1=ALU.add).then_inc(band_ready, 1)
            if beside is not None:
                beside(dve)
            for k in range(4):
                dve_small(dve, 0, 0, k)
            dve.wait_ge(band_ready, 1)
            rows_of(dve, dve_row)
            dve.wait_ge(stat, RB)
            dve.bn_aggr(mv[:], stats[:].rearrange("p r s -> p (r s)")).then_inc(tail, 1)
            dve.wait_ge(tail, 1)
            dve.tensor_scalar(std[:, 0:1], mv[:, 1:2], NORM_EPS, None, ALU.add).then_inc(tail, 1)
            dve.wait_ge(rooted, 1)
            dve.reciprocal(norm[:, 1:2], std[:, 1:2]).then_inc(tail, 1)
            dve.tensor_copy(norm[:, 0:1], mv[:, 0:1]).then_inc(tail, 1)
            if out is not None:
                dve.wait_ge(tail, 4)
                dve.scalar_tensor_tensor(out=shift[:], in0=norm[:, 0:1], scalar=-1.0, in1=norm[:, 1:2],
                                         op0=ALU.mult, op1=ALU.mult).then_inc(tail, 1)
                for j in range(0, 4, 2):
                    rows, dst = quarter(j)
                    dve.tensor_scalar(dst, rows, norm[:, 0:1], norm[:, 1:2], ALU.subtract, ALU.mult)\
                        .then_inc(finished[0], 1)


def binary_weights(dve, raw, negative, wb, loaded, ready):
    dve.wait_ge(loaded, 16)
    dve.tensor_scalar(negative[:], raw[:], 0.0, None, ALU.is_lt).then_inc(ready, 1)
    dve.wait_ge(ready, 1)
    dve.scalar_tensor_tensor(out=wb[:].rearrange("p t m -> p (t m)"), in0=raw[:], scalar=0.0,
                             in1=negative[:], op0=ALU.is_gt, op1=ALU.subtract).then_inc(ready, 1)


def binconv(nc, sem_, sb, sbr, vec, ps, wb, norm, pad, pad_to):
    def sem(name):
        return sem_("c_" + name)

    HALO = H + 2
    high = sbr("high", [P, HALO, HALO])
    rest = sbr("rest", [P, HALO, HALO])
    tap1 = sb("tap1", [P, TAPS])
    tapk = sb("tapk", [P, 3, 3])
    colk = sb("colk", [P, 3, 3])
    edge = sb("edge", [P, 3, 3])
    shift_map = sb("shift_map", [P, ROWS + 2, W])
    bn = sb("bn", [P, 4])
    resid = [sb(f"resid{s}", [P, ROWS, W]) for s in range(2)]
    lin = [sb(f"lin{s}", [P, ROWS, W]) for s in range(2)]

    bn_step = sem("bn_step")
    rooted = sem("rooted")
    normed = sem("normed")
    rounded = sem("rounded")
    split = sem("split")
    tap_mm = sem("tap_mm")
    map_step = sem("map_step")
    conv_mm = sem("conv_mm")
    resid_ready = sem("resid_ready")
    lin_ready = sem("lin_ready")
    clipped = sem("clipped")
    col = lambda name: vec[:, VEC[name]:VEC[name] + 1]
    TAP_BANK = 7

    def piece_rows(g):
        return (0 if g == 0 else ROWS * g + 2), ROWS * g + ROWS + 2

    def piece(t, g, off=0):
        first, last = piece_rows(g)
        return t[:, off + first:off + last, off:off + HALO]

    def fresh(g):
        first, last = max(0, piece_rows(g)[0] - 1), min(H, piece_rows(g)[1] - 1)
        return pad[:, R + first:R + last, R:R + W]

    def chunk(t, g):
        return t[:, R + ROWS * g:R + ROWS * g + ROWS, R:R + W]

    with nc.Block() as block:
        @block.tensor
        def _(pe):
            for g in range(CHUNKS):
                pe.wait_ge(split, g + 1)
                if g >= 4:
                    pe.wait_ge(lin_ready, g - 3)
                k = 0
                for t in range(TAPS):
                    dh, dw = t // 3, t % 3
                    for part in (high, rest):
                        mm = pe.matmul(ps[:, g % 4, :], wb[:, t, :],
                                       part[:, ROWS * g + dh:ROWS * g + dh + ROWS, dw:dw + W],
                                       start=(k == 0), stop=(k == 2 * TAPS - 1))
                        k += 1
                mm.then_inc(conv_mm, 1)
                if g == 0:
                    for t in range(TAPS):
                        mm = pe.matmul(ps[:, TAP_BANK, 2 * t:2 * t + 2], wb[:, t, :].bitcast(F32),
                                       vec[:, VEC["shift1"]:VEC["shift1"] + 2], start=True, stop=True)
                    mm.then_inc(tap_mm, 1)

        @block.scalar
        def _(act):
            for g in range(CHUNKS):
                act.wait_ge(normed, g + 1)
                act.copy(piece(high, g), piece(pad, g, R - 1)).then_inc(rounded, 1)
                if g == 1:
                    act.wait_ge(bn_step, 1)
                    act.activation(bn[:, 3:4], bn[:, 2:3], ACT.Sqrt).then_inc(rooted, 1)

        @block.vector
        def _(dve):
            def normalise(g):
                dve.tensor_scalar(fresh(g), fresh(g), norm[:, 0:1], norm[:, 1:2], ALU.subtract, ALU.mult)\
                    .then_inc(normed, 1)

            def rest_of(g):
                dve.wait_ge(rounded, g + 1)
                dve.tensor_tensor(piece(rest, g), piece(pad, g, R - 1), piece(high, g).bitcast(F32),
                                  ALU.subtract).then_inc(split, 1)

            dve.tensor_scalar(bn[:, 2:3], col("var"), NORM_EPS, None, ALU.add).then_inc(bn_step, 1)
            normalise(0)
            normalise(1)
            rest_of(0)
            normalise(2)
            rest_of(1)
            dve.wait_ge(rooted, 1)
            dve.reciprocal(bn[:, 1:2], bn[:, 3:4]).then_inc(bn_step, 1)
            dve.wait_ge(bn_step, 2)
            dve.tensor_tensor(bn[:, 0:1], bn[:, 1:2], col("gamma"), ALU.mult).then_inc(bn_step, 1)
            dve.wait_ge(bn_step, 3)
            dve.tensor_tensor(bn[:, 2:3], bn[:, 0:1], col("mean"), ALU.mult).then_inc(bn_step, 1)
            dve.scalar_tensor_tensor(out=bn[:, 1:2], in0=col("w1"), scalar=1.0, in1=bn[:, 0:1],
                                     op0=ALU.add, op1=ALU.mult).then_inc(bn_step, 1)
            dve.wait_ge(bn_step, 5)
            dve.tensor_tensor(bn[:, 2:3], col("beta"), bn[:, 2:3], ALU.subtract).then_inc(bn_step, 1)
            dve.wait_ge(tap_mm, 1)
            taps = ps[:, TAP_BANK, 0:2 * TAPS].rearrange("p (t i) -> p i t", i=2)
            dve.tensor_copy(tap1[:], taps[:, 0]).then_inc(map_step, 1)
            dve.wait_ge(map_step, 1)
            dve.scalar_tensor_tensor(out=tapk[:].rearrange("p r c -> p (r c)"), in0=taps[:, 1],
                                     scalar=col("w1"), in1=tap1[:], op0=ALU.mult, op1=ALU.add)\
                .then_inc(map_step, 1)
            step = 2
            for src, dst in ((lambda i: tapk[:, :, i], lambda i: colk[:, :, i]),
                             (lambda i: colk[:, i, :], lambda i: edge[:, i, :])):
                dve.wait_ge(map_step, step)
                dve.tensor_tensor(dst(0), src(1), src(2), ALU.add).then_inc(map_step, 1)
                dve.tensor_tensor(dst(2), src(0), src(1), ALU.add).then_inc(map_step, 1)
                dve.wait_ge(map_step, step + 2)
                dve.tensor_tensor(dst(1), dst(2), src(2), ALU.add).then_inc(map_step, 1)
                step += 3
            dve.wait_ge(map_step, step)
            dve.wait_ge(bn_step, 6)
            ef = edge[:].rearrange("p r c -> p (r c)")
            dve.tensor_scalar(ef, ef, bn[:, 0:1], bn[:, 2:3], ALU.mult, ALU.add).then_inc(map_step, 1)
            dve.wait_ge(map_step, step + 1)
            first = step + 1
            for rows, cls in ((slice(0, 1), 0), (slice(1, ROWS + 1), 1), (slice(ROWS + 1, ROWS + 2), 2)):
                n = rows.stop - rows.start
                for cols, ccls in ((slice(0, 1), 0), (slice(1, W - 1), 1), (slice(W - 1, W), 2)):
                    dve.tensor_copy(shift_map[:, rows, cols],
                                    spread(edge[:, cls:cls + 1, ccls:ccls + 1], [P, n, cols.stop - cols.start]))\
                        .then_inc(map_step, 1)
            for g in range(CHUNKS):
                if g + 3 < CHUNKS:
                    normalise(g + 3)
                if g + 2 < CHUNKS:
                    rest_of(g + 2)
                if g == 0:
                    dve.wait_ge(map_step, first + 9)
                if g >= 2:
                    dve.wait_ge(lin_ready, g - 1)
                at = 0 if g == 0 else 2 if g == CHUNKS - 1 else 1
                dve.tensor_tensor(resid[g % 2][:], chunk(pad, g), shift_map[:, at:at + ROWS], ALU.add)\
                    .then_inc(resid_ready, 1)
                dve.wait_ge(resid_ready, g + 1)
                dve.wait_ge(conv_mm, g + 1)
                if g >= 2:
                    dve.wait_ge(clipped, g - 1)
                dve.scalar_tensor_tensor(out=lin[g % 2][:].rearrange("p r w -> p (r w)"), in0=ps[:, g % 4, :],
                                         scalar=bn[:, 1:2], in1=resid[g % 2][:].rearrange("p r w -> p (r w)"),
                                         op0=ALU.mult, op1=ALU.add).then_inc(lin_ready, 1)
                dve.wait_ge(lin_ready, g + 1)
                dve.tensor_scalar(chunk(pad_to, g), lin[g % 2][:], 1.0, -1.0, ALU.min, ALU.max)\
                    .then_inc(clipped, 1)



def shape_constants():
    ident = np.eye(P, dtype=np.float32)
    plane_b = (np.arange(P) // HEADS) % B
    same = plane_b[:, None] == plane_b[None, :]
    centre = (ident - same / C).astype(np.float32)
    meansel = ((plane_b[:, None] == np.arange(32)) / C).astype(np.float32)
    qi, qj = np.divmod(np.arange(P), QC)
    pr, pc = np.divmod(np.arange(BLK * BLK), BLK)
    u = qi[:, None, None] + BLK * np.arange(2)[None, :, None] - pr[None, None, :]
    v = (qj[:, None, None] - pc[None, None, :]) + 0 * u
    inside = (u >= 0) & (u < KG) & (v >= 0) & (v < KG)
    gmask = np.where(inside, 0.0, OFF_BAND).astype(np.float32)
    perm = np.eye(P, dtype=np.float32).reshape(P, CP, B, HEADS).transpose(0, 2, 1, 3).reshape(P, P)
    bits = np.stack([np.arange(P) // 64, np.arange(P) % 2], 1)
    mask = (bits[:, :, None] == np.arange(2)).astype(np.float32)
    pair = np.tile(np.eye(64, dtype=np.float32), (CP, CP))
    return {"ident": ident, "centre": centre, "meansel": meansel,
            "perm": perm, "pair": pair, "mask": mask, "gmask": gmask}, (u, v, inside)


def lay_out(i):
    a, (u, v, inside) = shape_constants()
    part = np.arange(P)
    plane_cp, plane_b, plane_n = part // 64, (part // HEADS) % B, part % HEADS
    chan = CP * plane_n + plane_cp
    f = {k: np.asarray(x) for k, x in i.items()}
    a["x"] = f["x"]

    vec = np.zeros((P, len(VECS)), np.float32)
    for name, src in (("ln_w", "L0_conv_ln_w"), ("ln_b", "L0_conv_ln_b"), ("proj_b", "L0_conv_proj_b"),
                      ("shift1", "L2_conv_shift1"), ("shift2", "L2_conv_shift2"),
                      ("gamma", "L2_conv_gamma"), ("beta", "L2_conv_beta"),
                      ("mean", "L2_conv_running_mean"), ("var", "L2_conv_running_var"),
                      ("w1", "L2_conv_w1")):
        vec[:, VEC[name]] = f[src].reshape(C)[chan]
    for tag, lay in (("g1", "L1_conv_"), ("g3", "L3_conv_")):
        vec[:, VEC[tag + "_b1"]] = f[lay + "b1"][part % HIDDEN]
        vec[:, VEC[tag + "_b2"]] = f[lay + "b2"][0]
        w1 = np.zeros((P, 2, HALF, HIDDEN), np.float32)
        w1[part, plane_b // HALF, plane_b % HALF] = f[lay + "w1"][chan]
        a[tag + "_w1"] = w1.reshape(P, 2, P)
        w2 = np.zeros((P, 2, 32), np.float32)
        for i in range(2):
            w2[part, i, HALF * i + part // HIDDEN] = f[lay + "w2"][part % HIDDEN, 0]
        a[tag + "_w2"] = w2
        g = np.zeros((P, 2, BLK * BLK), np.float32)
        g[inside] = f[lay + "gauss_kernel"][u[inside], v[inside]]
        a[tag + "_gband"] = g
    a["vec"] = vec

    taps = np.zeros((2, len(KW), C, BAND), np.float32)
    for t in range(2):
        for k, width in enumerate(KW):
            first = W - 1 - width // 2
            taps[t, k, :, first:first + width] = f[f"L0_conv_w{2 - k}{t + 1}"].reshape(C, width)
    a["taps"] = taps.transpose(0, 2, 1, 3).reshape(2 * C, len(KW), BAND)
    one = np.ones(1, np.float32)
    a["bias_lhs"] = np.stack([np.concatenate([f["L0_conv_b" + k + str(t)] for k in "210"] + [one])
                              for t in (1, 2)], 1)
    pw = f["L0_conv_proj_w"]
    a["bias_rhs"] = np.concatenate([pw.T] * 3 + [f["L0_conv_proj_b"][None]])
    same = plane_b[:, None] == plane_b[None, :]
    ii, oo = np.nonzero(same)
    blk = np.zeros((P, P), np.float32)
    blk[ii, oo] = pw[chan[oo], chan[ii]]
    a["projblk"] = blk
    wt = f["L2_conv_weight"].reshape(C, C, 9)
    cw = np.zeros((P, 9, P), np.float32)
    cw[ii, :, oo] = wt[chan[oo], chan[ii]]
    a["c_weight"] = cw.reshape(P, 9 * P)
    return {k: np.ascontiguousarray(x) for k, x in a.items()}


def kernel(**inputs):
    import concourse.bacc as bacc
    from concourse.bass_utils import run_bass_kernel_spmd

    arrays = lay_out(inputs)
    nc = bacc.Bacc("TRN2", target_bir_lowering=False, num_devices=1)
    d = {k: nc.dram_tensor(f"in_{k}", x.shape, F32, kind="ExternalInput").ap() for k, x in arrays.items()}
    out = nc.dram_tensor("out", (B, C, H, W), F32, kind="ExternalOutput").ap()
    planes = out.rearrange("b (n cp) h w -> cp b n (h w)", cp=CP)
    band = nc.dram_tensor("band", (2 * C, BAND), F32, kind="Internal").ap()
    build(nc, d, band, [planes[cp].rearrange("b n f -> (b n) f") for cp in range(CP)])
    r = run_bass_kernel_spmd(nc, [{f"in_{k}": x for k, x in arrays.items()}], core_ids=[0])
    return r.results[0]["out"]
```
